# Optimizing a Trainium2 kernel written in Bass

```python
import numpy as np
import jax
import jax.numpy as jnp

def _softmax(x, axis=-1):
    return jax.nn.softmax(x, axis=axis)

def _gelu(x):
    return jax.nn.gelu(x, approximate=True)

def _silu(x):
    return jax.nn.silu(x)

def _sigmoid(x):
    return jax.nn.sigmoid(x)

def _layernorm(x, axis=-1, eps=1e-05):
    m = jnp.mean(x, axis=axis, keepdims=True)
    v = jnp.var(x, axis=axis, keepdims=True)
    return (x - m) / jnp.sqrt(v + eps)

def _scatter_add(tgt, idx, src, axis=0):
    return tgt.at[idx].add(src)

def _segment_sum(src, seg, n):
    return jax.ops.segment_sum(src, seg, n)
kernel_name = 'mk_seq_preln_d1_jaxref_r4_23bb2a'

def setup_inputs(seed: int=0):
    np.random.seed(seed)
    _w = jnp.asarray

    def _L0_attn_setup():
        import jax, jax.numpy as jnp
        import numpy as np
        B, T, D_MODEL, H = (4, 512, 256, 16)
        D_HEAD = D_MODEL // H
        THETA = 10000.0

        def _rope_tables(t_len, d_head, theta):
            inv_freq = 1.0 / theta ** (jnp.arange(0, d_head, 2, dtype=jnp.float32) / d_head)
            t = jnp.arange(t_len, dtype=jnp.float32)
            freqs = jnp.einsum('i,k->ik', t, inv_freq)
            return (jnp.cos(freqs), jnp.sin(freqs))

        def _apply_rope(x, cos, sin):
            c = cos[None, None, :, :]
            s = sin[None, None, :, :]
            x0, x1 = (x[..., ::2], x[..., 1::2])
            x_rot = jnp.stack((x0 * c - x1 * s, x0 * s + x1 * c), axis=-1)
            return x_rot.reshape(x.shape)
        key = jax.random.key(seed)
        ks = jax.random.split(key, 5)
        s = 0.02
        return {'x': jax.random.normal(ks[0], (B, T, D_MODEL), dtype=jnp.float32), 'Wq': jax.random.normal(ks[1], (D_MODEL, D_MODEL), dtype=jnp.float32) * s, 'bq': jnp.zeros((D_MODEL,), dtype=jnp.float32), 'Wk': jax.random.normal(ks[2], (D_MODEL, D_MODEL), dtype=jnp.float32) * s, 'bk': jnp.zeros((D_MODEL,), dtype=jnp.float32), 'Wv': jax.random.normal(ks[3], (D_MODEL, D_MODEL), dtype=jnp.float32) * s, 'bv': jnp.zeros((D_MODEL,), dtype=jnp.float32), 'Wo': jax.random.normal(ks[4], (D_MODEL, D_MODEL), dtype=jnp.float32) * s, 'bo': jnp.zeros((D_MODEL,), dtype=jnp.float32)}
    _L0_attn_in = _L0_attn_setup()

    def _L0_ffn_setup():
        import jax, jax.numpy as jnp
        import numpy as np
        B, T, C = (8, 512, 256)
        H = 1024
        E = 8
        K = 2
        LOAD_FACTOR = 1.2
        N_LAYER = 12

        def _get_expert_inputs(x, logits, expert_capacity):
            Tt = logits.shape[0]
            Cc = x.shape[1]
            top_k_logits, expert_indices = jax.lax.top_k(logits, K)
            expert_probs = jax.nn.softmax(top_k_logits, axis=-1)
            ei = jnp.swapaxes(expert_indices, 0, 1).ravel()
            one_hot = jax.nn.one_hot(ei, E, dtype=jnp.int32)
            pos = jnp.cumsum(one_hot, axis=0) * one_hot - 1
            pos = pos.reshape(-1, Tt, E)
            pos = jnp.swapaxes(pos, 0, 1)
            pos = jnp.max(pos, axis=2)
            ei = jnp.swapaxes(ei.reshape(-1, Tt), 0, 1)
            buf = jnp.zeros((E, expert_capacity, Cc), x.dtype)
            xr = jnp.repeat(x, K, axis=0)
            expert_inputs = buf.at[ei.ravel(), pos.ravel()].add(xr)
            return (expert_probs, pos, ei, expert_inputs)
        key = jax.random.key(seed)
        ks = jax.random.split(key, 9)
        std = 0.02
        proj_std = 0.02 * (2 * N_LAYER) ** (-0.5)
        return {'x': jax.random.normal(ks[0], (B, T, C), jnp.float32), 'router_w': jax.random.normal(ks[1], (C, E), jnp.float32) * std, 'router_b': jnp.zeros((E,), jnp.float32), 'w_c_fc': jax.random.normal(ks[2], (E, C, H), jnp.float32) * std, 'b_c_fc': jnp.zeros((E, 1, H), jnp.float32), 'w_gate': jax.random.normal(ks[3], (E, C, H), jnp.float32) * std, 'b_gate': jnp.zeros((E, 1, H), jnp.float32), 'w_c_proj': jax.random.normal(ks[4], (E, H, C), jnp.float32) * proj_std, 'b_c_proj': jnp.zeros((E, 1, C), jnp.float32)}
    _L0_ffn_in = _L0_ffn_setup()
    _d = {'L0_attn_x': _L0_attn_in['x'], 'L0_attn_Wq': _L0_attn_in['Wq'], 'L0_attn_bq': _L0_attn_in['bq'], 'L0_attn_Wk': _L0_attn_in['Wk'], 'L0_attn_bk': _L0_attn_in['bk'], 'L0_attn_Wv': _L0_attn_in['Wv'], 'L0_attn_bv': _L0_attn_in['bv'], 'L0_attn_Wo': _L0_attn_in['Wo'], 'L0_attn_bo': _L0_attn_in['bo'], 'L0_ffn_router_w': _L0_ffn_in['router_w'], 'L0_ffn_router_b': _L0_ffn_in['router_b'], 'L0_ffn_w_c_fc': _L0_ffn_in['w_c_fc'], 'L0_ffn_b_c_fc': _L0_ffn_in['b_c_fc'], 'L0_ffn_w_gate': _L0_ffn_in['w_gate'], 'L0_ffn_b_gate': _L0_ffn_in['b_gate'], 'L0_ffn_w_c_proj': _L0_ffn_in['w_c_proj'], 'L0_ffn_b_c_proj': _L0_ffn_in['b_c_proj']}
    _x0 = _d['L0_attn_x']
    _d['L0_attn_x'] = jax.random.normal(jax.random.fold_in(jax.random.key(seed), 1), (8, 512, 256), dtype=_x0.dtype)
    del _x0
    return _d

def reference(L0_attn_x, L0_attn_Wq, L0_attn_bq, L0_attn_Wk, L0_attn_bk, L0_attn_Wv, L0_attn_bv, L0_attn_Wo, L0_attn_bo, L0_ffn_router_w, L0_ffn_router_b, L0_ffn_w_c_fc, L0_ffn_b_c_fc, L0_ffn_w_gate, L0_ffn_b_gate, L0_ffn_w_c_proj, L0_ffn_b_c_proj):

    def _L0_attn_ref(x, Wq, bq, Wk, bk, Wv, bv, Wo, bo):
        import jax, jax.numpy as jnp
        import numpy as np
        B, T, D_MODEL, H = (4, 512, 256, 16)
        D_HEAD = D_MODEL // H
        THETA = 10000.0

        def _rope_tables(t_len, d_head, theta):
            inv_freq = 1.0 / theta ** (jnp.arange(0, d_head, 2, dtype=jnp.float32) / d_head)
            t = jnp.arange(t_len, dtype=jnp.float32)
            freqs = jnp.einsum('i,k->ik', t, inv_freq)
            return (jnp.cos(freqs), jnp.sin(freqs))

        def _apply_rope(x, cos, sin):
            c = cos[None, None, :, :]
            s = sin[None, None, :, :]
            x0, x1 = (x[..., ::2], x[..., 1::2])
            x_rot = jnp.stack((x0 * c - x1 * s, x0 * s + x1 * c), axis=-1)
            return x_rot.reshape(x.shape)
        b, t, c = x.shape
        h, dh = (H, D_HEAD)
        q = (x @ Wq.T + bq).reshape(b, t, h, dh).transpose(0, 2, 1, 3)
        k = (x @ Wk.T + bk).reshape(b, t, h, dh).transpose(0, 2, 1, 3)
        v = (x @ Wv.T + bv).reshape(b, t, h, dh).transpose(0, 2, 1, 3)
        cos, sin = _rope_tables(t, dh, THETA)
        q = _apply_rope(q, cos, sin)
        k = _apply_rope(k, cos, sin)
        scores = jnp.einsum('bhqd,bhkd->bhqk', q, k) / jnp.sqrt(jnp.float32(dh))
        causal = jnp.tril(jnp.ones((t, t), dtype=bool))
        scores = jnp.where(causal[None, None, :, :], scores, -jnp.inf)
        attn = jax.nn.softmax(scores, axis=-1)
        out = jnp.einsum('bhqk,bhkd->bhqd', attn, v)
        out = out.transpose(0, 2, 1, 3).reshape(b, t, c)
        return out @ Wo.T + bo

    def _L0_ffn_ref(x, router_w, router_b, w_c_fc, b_c_fc, w_gate, b_gate, w_c_proj, b_c_proj):
        import jax, jax.numpy as jnp
        import numpy as np
        B, T, C = (8, 512, 256)
        H = 1024
        E = 8
        K = 2
        LOAD_FACTOR = 1.2
        N_LAYER = 12

        def _get_expert_inputs(x, logits, expert_capacity):
            Tt = logits.shape[0]
            Cc = x.shape[1]
            top_k_logits, expert_indices = jax.lax.top_k(logits, K)
            expert_probs = jax.nn.softmax(top_k_logits, axis=-1)
            ei = jnp.swapaxes(expert_indices, 0, 1).ravel()
            one_hot = jax.nn.one_hot(ei, E, dtype=jnp.int32)
            pos = jnp.cumsum(one_hot, axis=0) * one_hot - 1
            pos = pos.reshape(-1, Tt, E)
            pos = jnp.swapaxes(pos, 0, 1)
            pos = jnp.max(pos, axis=2)
            ei = jnp.swapaxes(ei.reshape(-1, Tt), 0, 1)
            buf = jnp.zeros((E, expert_capacity, Cc), x.dtype)
            xr = jnp.repeat(x, K, axis=0)
            expert_inputs = buf.at[ei.ravel(), pos.ravel()].add(xr)
            return (expert_probs, pos, ei, expert_inputs)
        Bb, Tt, Cc = x.shape
        logits = jnp.einsum('btc,ce->bte', x, router_w) + router_b
        cap = int(LOAD_FACTOR * K * Tt // E)
        probs, pos, idx, einp = jax.vmap(lambda xb, lb: _get_expert_inputs(xb, lb, cap))(x, logits)
        if Bb % E == 0:
            t = einp.reshape(E, Bb // E, E, cap, Cc)
            t = jnp.swapaxes(t, 0, 2)
        else:
            t = jnp.swapaxes(einp, 0, 1)
        einp2 = t.reshape(E, Bb * cap, Cc)
        h = jnp.einsum('eti,eih->eth', einp2, w_c_fc) + b_c_fc
        g = jnp.einsum('eti,eih->eth', einp2, w_gate) + b_gate
        o = jnp.einsum('eth,eho->eto', jax.nn.silu(h * g), w_c_proj) + b_c_proj
        if Bb % E == 0:
            o = o.reshape(E, Bb // E, E, cap, Cc)
            o = jnp.swapaxes(o, 0, 2)
            o = o.reshape(Bb, E, cap, Cc)
        else:
            o = o.reshape(E, Bb, cap, Cc)
            o = jnp.swapaxes(o, 0, 1)

        def collect(eo, i, p, pr):
            sel = eo[i, p]
            return jnp.sum(pr[..., None] * sel, axis=1)
        return jax.vmap(collect)(o, idx, pos, probs)
    x = L0_attn_x
    x = x + _L0_attn_ref(_layernorm(x, axis=-1), L0_attn_Wq, L0_attn_bq, L0_attn_Wk, L0_attn_bk, L0_attn_Wv, L0_attn_bv, L0_attn_Wo, L0_attn_bo)
    x = x + _L0_ffn_ref(_layernorm(x, axis=-1), L0_ffn_router_w, L0_ffn_router_b, L0_ffn_w_c_fc, L0_ffn_b_c_fc, L0_ffn_w_gate, L0_ffn_b_gate, L0_ffn_w_c_proj, L0_ffn_b_c_proj)
    return x

_drawn_inputs = setup_inputs


def setup_inputs(seed=0):
    import zlib

    import numpy as np

    out = dict(_drawn_inputs(seed))
    spreads = {'L0_attn_bq': (0.0, 0.8),
     'L0_attn_bk': (0.0, 0.8),
     'L0_attn_bv': (0.0, 0.1),
     'L0_attn_bo': (0.0, 0.1),
     'L0_ffn_router_b': (0.0, 0.1),
     'L0_ffn_b_c_fc': (0.0, 0.8),
     'L0_ffn_b_gate': (0.0, 0.8),
     'L0_ffn_b_c_proj': (0.0, 0.443)}
    factors = {'L0_attn_Wq': 8.0,
     'L0_attn_Wk': 8.0,
     'L0_attn_Wv': 4.295,
     'L0_ffn_w_c_fc': 8.0,
     'L0_ffn_w_gate': 8.0,
     'L0_ffn_w_c_proj': 8.0}
    for name, (base, spread) in spreads.items():
        noise = np.random.default_rng([zlib.crc32(name.encode()), seed]).standard_normal(out[name].shape)
        drawn = base * np.exp(spread * noise) if base else spread * noise
        out[name] = jnp.asarray(drawn.astype(out[name].dtype))
    for name, factor in factors.items():
        out[name] = (out[name] * factor).astype(out[name].dtype)
    return out
```

```python
import concourse.bass as bass
from concourse import mybir
from contextlib import ExitStack

import numpy as np

F32 = mybir.dt.float32
F32R = mybir.dt.float32r
BF16 = mybir.dt.bfloat16
I32 = mybir.dt.int32
ALU = mybir.AluOpType
ACT = mybir.ActivationFunctionType
AXX = mybir.AxisListType.X

P = 128
BATCH, T, C = 8, 512, 256
TT = T // P
CK = C // P
HEADS, DH = 16, 16
GH = 4
NG = HEADS // GH
NP = 4
ZROW = NP * DH
MROW = ZROW + 1
ROWS = MROW + 1
SLOTS = 8
E, K, HID = 8, 2, 1024
CAP = int(1.2 * K * T // E)
EROWS = BATCH * CAP
NSLOT = E * EROWS
HK = HID // P
EPS = 1e-5
MASKED = -1e30
RSQRT_MAGIC = float(0x5F3759DF)
THETA = 10000.0

COS, SIN = 0, T
IDENT = 2 * T
CAUSAL = IDENT + P
LATER = CAUSAL + P
TRI = LATER + P
RANK = TRI + P
NCONST = RANK + E


def wait(eng, sem, n):
    if isinstance(n, int) and n <= 0:
        return
    eng.wait_ge(sem, n)


def wait_apart(eng, sem, n, passed):
    wait(eng, sem, n)
    if not isinstance(n, int):
        eng.sem_inc(passed, 1)


def there(b, first, last):
    return not isinstance(b, int) or first <= b <= last


def attention_phase(nc, d, rt):
    ctx = ExitStack()
    with ctx:
        def sb(name, shape, dt=F32):
            return ctx.enter_context(nc.sbuf_tensor(name, shape, dt))

        def sem(name):
            return ctx.enter_context(nc.semaphore(name))

        consts = sb("consts_sb", [P, NCONST])
        ident = consts[:, IDENT:IDENT + P]
        cos, sin = consts[:, COS:COS + T], consts[:, SIN:SIN + T]
        rank = consts[:, RANK:RANK + E]
        ident_bf = sb("ident_bf", [P, P], BF16)
        causal_bf = sb("causal_bf", [P, P], BF16)
        later_bf = sb("later_bf", [P, P], BF16)
        tri_bf = sb("tri_bf", [P, P], BF16)
        ones_bf = sb("ones_bf", [P, P], BF16)
        zeros = sb("zeros", [P, NSLOT * C // P // 18])
        wq = sb("wq_sb", [P, CK, C])
        wk = sb("wk_sb", [P, CK, C])
        wv = sb("wv_sb", [P, CK, C])
        wo = sb("wo_sb", [P, CK, C])
        wr = sb("wr_sb", [P, CK, E])
        bqk = sb("bqk", [P, 4])
        bv_all = sb("bv_all", [P, C])
        bo_all = sb("bo_all", [P, C])
        rb_all = sb("rb_all", [P, E])

        x_in = sb("x_in", [P, TT, C])
        stats1 = sb("stats1", [P, TT, 6])
        mv1 = sb("mv1", [P, TT, 2])
        rs1 = sb("rs1", [P, 3, TT])
        xn = sb("xn", [P, TT, C])
        xnT = sb("xnT", [P, CK, T])
        qk_b = sb("qk_b", [P, 2, T])
        rope_c = sb("rope_c", [P, 2, T])
        rope_s = sb("rope_s", [P, 2, T])
        hilo = sb("hilo", [P, 4, 2, T], F32R)
        v_next = sb("v_next", [P, TT, C])
        v_sb = sb("v_sb", [P, TT, HEADS, 2 * DH])
        qst = sb("qst", [ROWS, NG, GH, T], F32R)
        kst = sb("kst", [ROWS, NG, GH, T], F32R)
        mx = sb("mx", [P, 2, TT, GH])
        negmax = sb("negmax", [GH, 2, T], F32R)
        probs = sb("probs", [P, 2, GH, T])
        pv_sb = sb("pv_sb", [P, T])
        rden = sb("rden", [P, TT, GH])
        attn = sb("attn", [P, TT, C])
        attnT = sb("attnT", [P, CK, T])
        xr = sb("xr", [P, TT, C])
        x1 = sb("x1", [P, TT, C])
        stats2 = sb("stats2", [P, TT, 6])
        mv2 = sb("mv2", [P, TT, 2])
        rs2 = sb("rs2", [P, 3, TT])
        hn = sb("hn", [P, TT, C])
        hT = sb("hT", [P, CK, T])
        logits = sb("logits", [P, TT, E])
        top = sb("top", [P, 2, TT])
        picked = sb("picked", [P, 2, TT])
        eq = sb("eq", [P, TT, E])
        onehot = sb("onehot", [P, TT, K, E])
        onehot_bf = sb("onehot_bf", [P, TT, K, E], BF16)
        posm = sb("posm", [P, TT, K, E])
        pos = sb("pos", [P, TT, K])
        over = sb("over", [P, TT, K])
        slot_f = sb("slot_f", [P, TT, K])
        base = sb("base", [P, 1])
        put_at = sb("put_at", [P, TT * K], I32)
        dlt = sb("dlt", [P, TT])
        ex = sb("ex", [P, TT])

        ps = ctx.enter_context(nc.psum_tensor("ps", [P, 8, T], F32))
        S1 = 0
        S2 = 4
        pvb = ps[:, 6, :]
        misc = ps[:, 7, :]

        ld_const, ld_w = sem("ld_const"), sem("ld_w")
        ld_x, ld_xr, st_x1 = sem("ld_x"), sem("ld_xr"), sem("st_x1")
        st_hilo = sem("st_hilo")
        ld_stack = [sem(f"ld_stack{g}") for g in range(NG)]
        ld_max = sem("ld_max")
        st_zero, st_tok = sem("st_zero"), sem("st_tok")
        made, z_ready = sem("made"), sem("z_ready")
        stack_set = sem("stack_set")
        p1_done, p2_done, pv_done = sem("p1_done"), sem("p2_done"), sem("pv_done")
        maxT_done, atT_done = sem("maxT_done"), sem("atT_done")
        xT_done, qk_done, v_done = sem("xT_done"), sem("qk_done"), sem("v_done")
        oT_done, o_done, hT_done = sem("oT_done"), sem("o_done"), sem("hT_done")
        lg_done, pf_done = sem("lg_done"), sem("pf_done")
        exp_done, negmax_out, pv_out = sem("exp_done"), sem("negmax_out"), sem("pv_out")
        xT_out, qk_out, oT_out, hT_out = sem("xT_out"), sem("qk_out"), sem("oT_out"), sem("hT_out")
        ex_done = sem("ex_done")
        red_done, at_out, v_out, v_moved = sem("red_done"), sem("at_out"), sem("v_out"), sem("v_moved")
        o_out, lg_out, pf_out = sem("o_out"), sem("lg_out"), sem("pf_out")
        mv1_done, mv2_done, xn_done, h_done = sem("mv1_done"), sem("mv2_done"), sem("xn_done"), sem("h_done")
        sin_done, rope_done, oh_done, dlt_done, put_done = (sem("sin_done"), sem("rope_done"), sem("oh_done"),
                                                            sem("dlt_done"), sem("put_done"))
        rs1_done, rs2_done = sem("rs1_done"), sem("rs2_done")
        cos_done, hilo_done, xr_done = sem("cos_done"), sem("hilo_done"), sem("xr_done")
        dve_step, newton1, newton2 = sem("dve_step"), sem("newton1"), sem("newton2")
        hilo_half = sem("hilo_half")
        sp_passed, dve_passed, pool_passed = sem("sp_passed"), sem("dve_passed"), sem("pool_passed")

        PIECES = {
            (0, 0): ("M", 0), (0, 1): ("L", 0), (0, 3): ("A", 0), (0, 5): ("X", 0), (0, 6): ("X", 1), (0, 7): ("F", 0),
            (1, 0): ("M", 0), (1, 1): ("Q", 0), (1, 2): ("Q", 1), (1, 3): ("A", 0), (1, 4): ("Q", 2), (1, 5): ("Q", 3),
            (2, 0): ("M", 0), (2, 3): ("A", 0), (2, 4): ("V", 0), (2, 5): ("T", 0), (2, 6): ("T", 1), (2, 7): ("V", 1),
            (3, 0): ("M", 0), (3, 1): ("O", 0), (3, 2): ("O", 1), (3, 3): ("A", 0), (3, 6): ("H", 0), (3, 7): ("H", 1),
        }

        def piece_there(b, g, kind):
            s = 4 * b + g
            return {
                "M": there(s, 1, 32) if isinstance(b, int) else True,
                "A": there(s, 3, 34) if isinstance(b, int) else True,
                "X": there(b, -1, 6), "Q": there(b, -1, 6), "V": there(b, -1, 6),
                "T": there(b, 1, 8), "O": there(b, 1, 8), "H": there(b, 1, 8),
                "L": there(b, 2, 9), "F": there(b, 2, 9),
            }[kind]

        def freed(b, g, kind, n):
            return {
                "M": (negmax_out, 4 * b + g),
                "A": (at_out, 4 * b + g - 2),
                "X": (xT_out, 2 * b + 2 + n + 1),
                "Q": (qk_out, 4 * b + 4 + n + 1),
                "V": (v_out, 2 * b + 2 + n + 1),
                "T": (oT_out, 2 * b - 2 + n + 1),
                "O": (o_out, 2 * b - 2 + n + 1),
                "H": (hT_out, 2 * b - 2 + n + 1),
                "L": (lg_out, b - 2 + 1),
                "F": (pf_out, b - 2 + 1),
            }[kind]

        def last_piece(b, g, u):
            keys = sorted(PIECES)
            at = keys.index((g, u))
            for back in range(1, 2 * len(keys)):
                k = at - back
                bb = b if k >= 0 else b - 1
                gg, uu = keys[k % len(keys)]
                kind, n = PIECES[gg, uu]
                if (not isinstance(bb, int) or bb >= -1) and piece_there(bb, gg, kind):
                    if isinstance(bb, int) and bb == -1 and kind not in "XQV":
                        continue
                    return freed(bb, gg, kind, n)
            return None

        block = ctx.enter_context(nc.Block())

        @block.sync
        def _(sp):
            def load_x(b):
                wait(sp, xn_done, b)
                sp.dma_start(x_in[:], d["x"][bass.ts(b, T), :].rearrange("(t p) c -> p t c", p=P)).then_inc(ld_x, 16)

            def store_hilo(b, n):
                wait(sp, hilo_done, 4 * b + n + 1)
                dst = rt["qk"][b, n // 2, :, bass.ts(n % 2, P), :]
                sp.dma_start(dst.rearrange("h p t -> p h t"), hilo[:, n].bitcast(F32)).then_inc(st_hilo, 16)

            def load_stack(b, g):
                wait_apart(sp, st_hilo, 64 * (b + 1), sp_passed)
                wait_apart(sp, p2_done, 16 * (4 * b + g - 3), sp_passed)
                for side, stack, parts in ((0, qst, (0, 1, 0, 1)), (1, kst, (0, 0, 1, 1))):
                    for c, part in enumerate(parts):
                        src = rt["qk"][b, side, part, bass.ts(g, GH * DH), :]
                        sp.dma_start(stack[c * DH:(c + 1) * DH, g].bitcast(F32), src.rearrange("(h d) t -> d h t", d=DH))\
                            .then_inc(ld_stack[g], 16)

            def body(b):
                for g in range(4):
                    for u in range(SLOTS):
                        if u == 0 and g == 0 and there(b, 0, 6):
                            load_x(b + 1)
                        if u == 0 and g < 3 and there(b, 1, 7):
                            load_stack(b, g + 1)
                        if u == 0 and g == 3 and there(b, 0, 6):
                            load_stack(b + 1, 0)
                        if (g, u) == (2, 0) and there(b, 1, 8):
                            wait(sp, o_out, 2 * (b - 1))
                            sp.dma_start(xr[:], d["x"][bass.ts(b - 1, T), :].rearrange("(t p) c -> p t c", p=P))\
                                .then_inc(ld_xr, 16)
                        if (g, u) in ((1, 6), (1, 7), (2, 1), (2, 2)) and there(b, 0, 6):
                            store_hilo(b + 1, ((1, 6), (1, 7), (2, 1), (2, 2)).index((g, u)))
                        if (g, u) == (3, 4) and there(b, 1, 8):
                            wait(sp, o_out, 2 * b)
                            sp.dma_start(rt["x1"][bass.ts(b - 1, T), :].rearrange("(t p) c -> p t c", p=P), x1[:])\
                                .then_inc(st_x1, 16)

            sp.dma_start(consts[:], d["consts"]).then_inc(ld_const, 16)
            load_x(0)
            for w_sb, name in ((wq, "wqT"), (wk, "wkT"), (wv, "wvT"), (wo, "woT"), (wr, "wr")):
                sp.dma_start(w_sb[:], d[name].rearrange("(k p) n -> p k n", p=P)).then_inc(ld_w, 16)
            for n in range(CK):
                sp.dma_start(bqk[:, n:n + 1], d["bq"][bass.ts(n, P)].rearrange("(p a) -> p a", a=1)).then_inc(ld_w, 16)
                sp.dma_start(bqk[:, 2 + n:3 + n], d["bk"][bass.ts(n, P)].rearrange("(p a) -> p a", a=1))\
                    .then_inc(ld_w, 16)
            for all_rows, name in ((bv_all, "bv"), (bo_all, "bo"), (rb_all, "rb")):
                sp.dma_start(all_rows[:], d[name].rearrange("(a n) -> a n", a=1).to_broadcast([P, all_rows.shape[1]]))\
                    .then_inc(ld_w, 16)
            for n in range(4):
                store_hilo(0, n)
            for g in range(NG):
                load_stack(0, g)
            body(0)
            body(1)
            with sp.Fori(2, 7) as b:
                body(b)
            body(7)
            body(8)
            sp.wait_ge(st_x1, 16 * BATCH)

        @block.tensor
        def _(pe):
            mm = nc.tensor.matmul

            def pass1(b, g, u):
                s = 4 * b + g
                i, pr = u // 2, u % 2
                if u == 0:
                    wait(pe, ld_stack[g], 128 * (b + 1))
                wait(pe, red_done, 8 * s + u - 1)
                width = max(2 * P, P * (i + 1))
                for hh in range(2):
                    h, bank = 2 * pr + hh, ps[:, S1 + 2 * (u % 2) + hh, :]
                    mm(bank[:, 0:width], qst[0:MROW, g, h, bass.ts(i, P)], kst[0:MROW, g, h, 0:width],
                       start=True, stop=False)
                    last = mm(bank[:, bass.ts(i, P)], ident_bf[:], causal_bf[:], start=False, stop=True)
                last.then_inc(p1_done, 1)

            def pass2(t, g, u):
                j, pr = u // 2, u % 2
                if u == 0:
                    wait(pe, ld_max, 16 * (t + 1))
                q0 = min(P * j, T - 2 * P)
                for hh in range(2):
                    h, n = 2 * pr + hh, 2 * u + hh
                    wait(pe, exp_done, 16 * t + n - 1)
                    mm(ps[:, S2 + hh, 0:T - q0], kst[0:ROWS, g, h, bass.ts(j, P)], qst[0:ROWS, g, h, q0:T],
                       start=True, stop=False)
                    mm(ps[:, S2 + hh, P * j - q0:P * (j + 1) - q0], ident_bf[:], later_bf[:], start=False, stop=True)\
                        .then_inc(p2_done, 1)

            def pv(t, bt, g, j):
                wait(pe, exp_done, 16 * t + 4 * j + 4)
                if j == 0:
                    wait(pe, pv_out, t)
                    if g == 0:
                        wait(pe, v_moved, bt + 1)
                for h in range(GH):
                    last = mm(pvb[32 * h:32 * h + 32, P * j:T], v_sb[:, j, GH * g + h, :], probs[:, j % 2, h, P * j:T],
                              start=(j == 0), stop=(j == TT - 1))
                last.then_inc(pv_done, 1)

            def turn(dst, src_of, n):
                for k in range(n):
                    last = nc.tensor.transpose(dst[:, bass.ts(k, P)], src_of(k), ident)
                return last

            def piece(b, g, u):
                kind, n = PIECES[g, u]
                if not piece_there(b, g, kind):
                    return
                s = 4 * b + g
                free = last_piece(b, g, u)
                if free:
                    wait(pe, *free)
                if kind == "M":
                    wait(pe, red_done, 8 * s)
                    for i in range(TT):
                        last = nc.tensor.transpose(misc[0:GH, bass.ts(i, P)], mx[:, (g - 1) % 2, i, :], ident)
                    last.then_inc(maxT_done, 1)
                elif kind == "A":
                    wait(pe, pv_out, s - 2)
                    turn(misc, lambda k: pv_sb[:, bass.ts(k, P)], TT).then_inc(atT_done, 1)
                elif kind == "X":
                    wait(pe, xn_done, b + 2)
                    turn(misc, lambda k: xn[:, k, bass.ts(n, P)], TT).then_inc(xT_done, 1)
                elif kind == "Q":
                    wait(pe, xT_out, 2 * (b + 2))
                    w_sb = (wq, wk)[n // 2]
                    for c in range(CK):
                        last = mm(misc, w_sb[:, c, bass.ts(n % 2, P)], xnT[:, c, :], start=(c == 0), stop=(c == CK - 1))
                    last.then_inc(qk_done, 1)
                elif kind == "V":
                    for k in range(2):
                        for c in range(CK):
                            last = mm(misc[:, bass.ts(k, C)], xnT[:, c, bass.ts(2 * n + k, P)], wv[:, c, :],
                                      start=(c == 0), stop=(c == CK - 1))
                    last.then_inc(v_done, 1)
                elif kind == "T":
                    wait(pe, at_out, 4 * b)
                    turn(misc, lambda k: attn[:, k, bass.ts(n, P)], TT).then_inc(oT_done, 1)
                elif kind == "O":
                    wait(pe, oT_out, 2 * b)
                    for k in range(2):
                        for c in range(CK):
                            last = mm(misc[:, bass.ts(k, C)], attnT[:, c, bass.ts(2 * n + k, P)], wo[:, c, :],
                                      start=(c == 0), stop=(c == CK - 1))
                    last.then_inc(o_done, 1)
                elif kind == "H":
                    wait(pe, h_done, b)
                    turn(misc, lambda k: hn[:, k, bass.ts(n, P)], TT).then_inc(hT_done, 1)
                elif kind == "L":
                    wait(pe, hT_out, 2 * (b - 1))
                    for k in range(TT):
                        for c in range(CK):
                            last = mm(misc[:, bass.ts(k, E)], hT[:, c, bass.ts(k, P)], wr[:, c, :],
                                      start=(c == 0), stop=(c == CK - 1))
                    last.then_inc(lg_done, 1)
                elif kind == "F":
                    wait(pe, oh_done, b - 1)
                    out = misc[:, 0:TT * K * E].rearrange("p (t k e) -> p t k e", t=TT, k=K)
                    flat = misc[:, 0:TT * K * E]
                    mm(flat, tri_bf[:], onehot_bf[:].rearrange("p t k e -> p (t k e)"), start=True, stop=False)
                    for j in range(TT - 1):
                        mm(out[:, j + 1:TT].rearrange("p t k e -> p t (k e)"), ones_bf[:],
                           onehot_bf[:, j].rearrange("p k e -> p (k e)")
                           .rearrange("p (a n) -> p a n", a=1).to_broadcast([P, TT - 1 - j, K * E]),
                           start=False, stop=False)
                    for j in range(TT):
                        last = mm(out[:, :, 1, :], ones_bf[:],
                                  onehot_bf[:, j, 0:1, :].to_broadcast([P, TT, E]), start=False, stop=(j == TT - 1))
                    last.then_inc(pf_done, 1)

            def body(b):
                for g in range(4):
                    s = 4 * b + g
                    for u in range(SLOTS):
                        if there(b, 0, 7):
                            pass1(b, g, u)
                        if not isinstance(b, int) or 0 <= s - 2 <= 31:
                            pass2(s - 2, (g - 2) % 4, u)
                        if u in (3, 5, 7) and (not isinstance(b, int) or 0 <= s - 2 <= 31):
                            pv(s - 2, b - (g < 2), (g - 2) % 4, (u - 3) // 2)
                        if u == 1 and (not isinstance(b, int) or 0 <= s - 3 <= 31):
                            pv(s - 3, b - (g < 3), (g - 3) % 4, 3)
                        if (g, u) in PIECES:
                            piece(b, g, u)

            pe.wait_ge(made, 5)
            pe.wait_ge(ld_const, 16)
            pe.wait_ge(stack_set, 2)
            pe.wait_ge(ld_w, 16 * 12)
            for g, u in sorted(PIECES):
                if PIECES[g, u][0] in "XQV":
                    piece(-1, g, u)
            body(0)
            body(1)
            with pe.Fori(2, 7) as b:
                body(b)
            body(7)
            body(8)
            for g, u in sorted(PIECES):
                if PIECES[g, u][0] in "LF":
                    piece(9, g, u)

        @block.scalar
        def _(act):
            A = nc.scalar.activation

            def exps(t, u):
                j, pr = u // 2, u % 2
                q0 = min(P * j, T - 2 * P)
                for hh in range(2):
                    wait(act, p2_done, 16 * t + 2 * u + hh + 1)
                    if pr == 0 and hh == 0:
                        wait(act, pv_done, 4 * t + j - 1)
                    A(probs[:, j % 2, 2 * pr + hh, P * j:T], ps[:, S2 + hh, P * j - q0:T - q0], ACT.Exp,
                      scale=float(DH) ** -0.5).then_inc(exp_done, 1)

            def max_out(b, g):
                s = 4 * b + g
                wait(act, maxT_done, s)
                wait(act, p2_done, 16 * (s - 3) + 1)
                A(negmax[:, (g - 1) % 2, :], misc[0:GH, :], ACT.Copy, scale=-1.0).then_inc(negmax_out, 1)
                wait(act, negmax_out, s)
                wait(act, p2_done, 16 * (s - 4))
                act.dma_start(qst[MROW:MROW + 1, (g - 1) % 4].bitcast(F32), negmax[:, (g - 1) % 2, :].bitcast(F32)).then_inc(ld_max, 16)

            def body_slot(b, g, u):
                s = 4 * b + g
                if u == 1 and piece_there(b, g, "M"):
                    max_out(b, g)
                if u == 2 and (not isinstance(b, int) or 0 <= s - 3 <= 31):
                    wait(act, pv_done, 4 * (s - 2))
                    wait(act, atT_done, s - 3)
                    A(pv_sb[:], pvb, ACT.Copy).then_inc(pv_out, 1)
                if (g, u) in ((0, 6), (0, 7)) and piece_there(b, g, "X"):
                    n = u - 6
                    wait(act, xT_done, 2 * b + 2 + n + 1)
                    wait(act, v_done, 2 * (b + 1))
                    A(xnT[:, n, :], misc, ACT.Copy).then_inc(xT_out, 1)
                if g == 1 and u in (2, 3, 5, 6) and piece_there(b, g, "Q"):
                    n = (2, 3, 5, 6).index(u)
                    wait(act, qk_done, 4 * b + 4 + n + 1)
                    wait(act, cos_done, 4 * b + 4 + n - 1)
                    wait(act, sin_done, 4 * b + 4 + n - 1)
                    A(qk_b[:, n % 2, :], misc, ACT.Identity, bias=bqk[:, n:n + 1]).then_inc(qk_out, 1)
                if (g, u) in ((2, 6), (2, 7)) and piece_there(b, g, "T"):
                    n = u - 6
                    wait(act, oT_done, 2 * b - 2 + n + 1)
                    wait(act, o_done, 2 * (b - 1))
                    A(attnT[:, n, :], misc, ACT.Copy).then_inc(oT_out, 1)
                if (g, u) == (3, 7) and piece_there(b, g, "H"):
                    wait(act, hT_done, 2 * b - 2 + 1)
                    wait(act, lg_done, b - 1)
                    A(hT[:, 0, :], misc, ACT.Copy).then_inc(hT_out, 1)
                if (g, u) == (0, 0) and there(b, 2, 9):
                    wait(act, hT_done, 2 * (b - 1))
                    A(hT[:, 1, :], misc, ACT.Copy).then_inc(hT_out, 1)
                if (g, u) == (0, 4) and there(b, 2, 9):
                    wait(act, dlt_done, b - 1)
                    A(ex[:], dlt[:], ACT.Exp).then_inc(ex_done, 1)
                if not isinstance(b, int) or 0 <= s - 2 <= 31:
                    exps(s - 2, u)

            def body(b):
                for g in range(4):
                    for u in range(SLOTS):
                        body_slot(b, g, u)

            act.wait_ge(ld_w, 16 * 12)
            for g, u in ((0, 6), (0, 7), (1, 2), (1, 3), (1, 5), (1, 6)):
                body_slot(-1, g, u)
            body(0)
            body(1)
            with act.Fori(2, 7) as b:
                body(b)
            body(7)
            body(8)
            body_slot(9, 0, 0)
            body_slot(9, 0, 4)
            act.wait_ge(ld_max, 16 * 32)

        @block.vector
        def _(dve):
            V = nc.vector
            count = [0]

            def settle(steps_per_body, b, k, ins):
                ins.then_inc(dve_step, 1)
                dve.wait_ge(dve_step, (count[0] + k) if isinstance(b, int) else (count[0] + (b - 2) * steps_per_body + k))

            class Chain:
                def __init__(self, b):
                    self.b, self.k = b, 0

                def __call__(self, ins):
                    self.k += 1
                    settle(DVE_STEPS, self.b, self.k, ins)

            def layer_stats(chain, src, stats, mv, done):
                for k in range(TT):
                    ins = V.bn_stats(stats[:, k, :], src[:, k, :])
                chain(ins)
                if not isinstance(chain.b, int):
                    dve.sem_inc(dve_passed, 1)
                for k in range(TT):
                    ins = V.bn_aggr(mv[:, k, :], stats[:, k, :])
                ins.then_inc(done, 1)

            def normalise(dst, src, mv, rs, done):
                for k in range(TT):
                    ins = V.tensor_scalar(dst[:, k, :], src[:, k, :], mv[:, k, 0:1], rs[:, 1, k:k + 1],
                                          ALU.subtract, ALU.mult)
                ins.then_inc(done, 1)

            def choose(chain, b, k, src):
                chain(V.reduce_max(top[:, k, :], src, AXX))
                chain(V.tensor_tensor(eq[:], src, top[:, k, :].unsqueeze(2).to_broadcast([P, TT, E]), ALU.is_equal))
                chain(V.tensor_tensor(eq[:], eq[:], rank.unsqueeze(1).to_broadcast([P, TT, E]), ALU.mult))
                chain(V.reduce_max(picked[:, k, :], eq[:], AXX))
                chain(V.tensor_tensor(onehot[:, :, k, :], rank.unsqueeze(1).to_broadcast([P, TT, E]),
                                      picked[:, k, :].unsqueeze(2).to_broadcast([P, TT, E]), ALU.is_equal))

            def route(chain, b):
                wait(dve, lg_done, b - 1)
                V.tensor_tensor(logits[:], misc[:, 0:TT * E].rearrange("p (t e) -> p t e", t=TT),
                                rb_all[:].unsqueeze(1).to_broadcast([P, TT, E]), ALU.add).then_inc(lg_out, 1)
                dve.wait_ge(lg_out, b - 1)
                choose(chain, b, 0, logits[:])
                chain(V.scalar_tensor_tensor(logits[:], onehot[:, :, 0, :], -3e38, logits[:], ALU.mult, ALU.add))
                choose(chain, b, 1, logits[:])
                V.tensor_copy(onehot_bf[:], onehot[:]).then_inc(oh_done, 1)
                V.tensor_tensor(dlt[:], top[:, 1, :], top[:, 0, :], ALU.subtract).then_inc(dlt_done, 1)

            def probabilities(chain, b):
                wait(dve, ex_done, b - 1)
                pr = rt["prob"][:, bass.ts(b - 2, TT * K)].rearrange("p (t k) -> p t k", k=K)
                chain(V.tensor_scalar(dlt[:], ex[:], 1.0, None, ALU.add))
                chain(V.reciprocal(dlt[:], dlt[:]))
                chain(V.tensor_copy(pr[:, :, 0], dlt[:]))
                chain(V.tensor_tensor(pr[:, :, 1], ex[:], dlt[:], ALU.mult))

            def slots(chain, b):
                wait(dve, pf_done, b - 1)
                V.tensor_tensor(posm[:], misc[:, 0:TT * K * E].rearrange("p (t k e) -> p t k e", t=TT, k=K),
                                onehot[:], ALU.mult).then_inc(pf_out, 1)
                dve.wait_ge(pf_out, b - 1)
                chain(V.reduce_sum(pos[:], posm[:], AXX))
                chain(V.tensor_scalar(over[:], pos[:], float(CAP - 1), float(NSLOT), ALU.is_gt, ALU.mult))
                chain(V.tensor_scalar(pos[:], pos[:], float(CAP - 1), base[:, 0:1], ALU.min, ALU.add))
                chain(V.scalar_tensor_tensor(slot_f[:], picked[:].rearrange("p k t -> p t k"), -float(EROWS),
                                             pos[:], ALU.mult, ALU.add))
                chain(V.tensor_copy(rt["slot"][:, bass.ts(b - 2, TT * K)], slot_f[:].rearrange("p t k -> p (t k)")))
                V.tensor_tensor(put_at[:].rearrange("p (t k) -> p t k", k=K), slot_f[:], over[:], ALU.add)\
                    .then_inc(put_done, 1)
                chain(V.tensor_scalar(base[:], base[:], float(CAP), None, ALU.add))

            def body_slot(chain, b, g, u):
                s = 4 * b + g
                if u == 4 and piece_there(b, g, "A"):
                    at = misc.rearrange("p (t h r) -> p t h r", t=TT, h=GH)
                    wait(dve, atT_done, s - 2)
                    chain(V.reciprocal(rden[:], at[:, :, :, DH]))
                    g3 = (g - 3) % 4
                    if g == 3:
                        wait(dve, oT_done, 2 * b)
                    V.tensor_tensor(attn[:, :, g3 * GH * DH:(g3 + 1) * GH * DH].rearrange("p t (h r) -> p t h r", h=GH),
                                    at[:, :, :, 0:DH], rden[:].unsqueeze(3).to_broadcast([P, TT, GH, DH]),
                                    ALU.mult).then_inc(at_out, 1)
                if (g, u) in ((2, 5), (3, 0)) and there(b, -1, 6):
                    n = g - 2
                    wait(dve, v_done, 2 * b + 2 + n + 1)
                    wait(dve, v_moved, b + 1)
                    V.tensor_tensor(v_next[:, 2 * n:2 * n + 2, :], misc.rearrange("p (k c) -> p k c", k=2),
                                    bv_all[:].unsqueeze(1).to_broadcast([P, 2, C]), ALU.add).then_inc(v_out, 1)
                if (g, u) in ((3, 2), (3, 3)) and piece_there(b, g, "O"):
                    n = u - 2
                    wait(dve, o_done, 2 * b - 2 + n + 1)
                    wait(dve, xr_done, b)
                    wait(dve, st_x1, 16 * (b - 1))
                    V.tensor_tensor(x1[:, 2 * n:2 * n + 2, :], misc.rearrange("p (k c) -> p k c", k=2),
                                    xr[:, 2 * n:2 * n + 2, :], ALU.add).then_inc(o_out, 1)
                if (g, u) == (0, 2) and there(b, 2, 9):
                    route(chain, b)
                if (g, u) == (1, 0) and there(b, 2, 9):
                    slots(chain, b)
                if there(b, 0, 7):
                    wait(dve, p1_done, 8 * s + u + 1)
                    if u == 0:
                        wait(dve, maxT_done, s - 1)
                    i, pr = u // 2, u % 2
                    V.reduce_max(mx[:, g % 2, i, 2 * pr:2 * pr + 2],
                                 ps[:, S1 + 2 * (u % 2):S1 + 2 * (u % 2) + 2, 0:P * (i + 1)], AXX)\
                        .then_inc(red_done, 1)
                if (g, u) == (0, 0) and there(b, -1, 6):
                    wait(dve, ld_x, 16 * (b + 2))
                    layer_stats(chain, x_in, stats1, mv1, mv1_done)
                if (g, u) == (0, 3) and there(b, -1, 6):
                    wait(dve, rs1_done, b + 2)
                    wait(dve, xT_done, 2 * (b + 1))
                    normalise(xn, x_in, mv1, rs1, xn_done)
                if (g, u) == (0, 6) and there(b, 2, 9):
                    probabilities(chain, b)
                if g == 1 and u in (3, 4, 6, 7) and there(b, -1, 6):
                    n = (3, 4, 6, 7).index(u)
                    wait_apart(dve, qk_out, 4 * b + 4 + n + 1, dve_passed)
                    wait_apart(dve, hilo_done, 4 * b + 4 + n - 1, dve_passed)
                    chain(V.stream_shuffle(rope_s[:, n % 2, :], qk_b[:, n % 2, :], [i ^ 1 for i in range(32)]))
                    V.tensor_tensor(rope_s[:, n % 2, :], rope_s[:, n % 2, :], sin, ALU.mult).then_inc(sin_done, 1)
                if (g, u) in ((1, 4), (1, 5), (1, 7), (2, 0)) and there(b, -1, 6):
                    n = ((1, 4), (1, 5), (1, 7), (2, 0)).index((g, u))
                    wait(dve, sin_done, 4 * b + 4 + n + 1)
                    wait(dve, cos_done, 4 * b + 4 + n + 1)
                    V.tensor_tensor(rope_s[:, n % 2, :], rope_c[:, n % 2, :], rope_s[:, n % 2, :], ALU.add)\
                        .then_inc(rope_done, 1)
                if (g, u) == (2, 2) and there(b, 0, 7):
                    wait(dve, v_out, 2 * (b + 1))
                    wait(dve, pv_done, 16 * b)
                    V.tensor_copy(v_sb[:, :, :, 0:DH],
                                  v_next[:].rearrange("p t (h r) -> p t h r", h=HEADS)).then_inc(v_moved, 1)
                if (g, u) == (3, 3) and piece_there(b, g, "O"):
                    wait(dve, o_out, 2 * b)
                    layer_stats(chain, x1, stats2, mv2, mv2_done)
                if (g, u) == (3, 5) and piece_there(b, g, "O"):
                    wait(dve, rs2_done, b)
                    wait(dve, st_tok, 16 * 8 * (b - 1))
                    wait(dve, hT_done, 2 * (b - 1))
                    normalise(hn, x1, mv2, rs2, h_done)

            def body(b):
                chain = Chain(b)
                for g in range(4):
                    for u in range(SLOTS):
                        body_slot(chain, b, g, u)
                return chain.k

            DVE_STEPS = 4 + 1 + 1 + 11 + 4 + 6 + 4

            chain = Chain(0)
            chain(V.memset(v_sb[:], 1.0))
            V.memset(ones_bf[:], 1.0).then_inc(made, 1)
            chain(V.memset(base[:], float(E * EROWS)))
            dve.wait_ge(ld_const, 16)
            V.tensor_copy(ident_bf[:], ident).then_inc(made, 1)
            V.tensor_copy(causal_bf[:], consts[:, CAUSAL:CAUSAL + P]).then_inc(made, 1)
            V.tensor_copy(later_bf[:], consts[:, LATER:LATER + P]).then_inc(made, 1)
            V.tensor_copy(tri_bf[:], consts[:, TRI:TRI + P]).then_inc(made, 1)
            dve.wait_ge(ld_w, 16 * 12)
            for g, u in ((0, 0), (0, 3), (1, 3), (1, 4), (1, 5), (1, 6), (1, 7), (2, 0), (2, 5), (3, 0)):
                body_slot(chain, -1, g, u)
            count[0] += chain.k
            count[0] += body(0)
            count[0] += body(1)
            with dve.Fori(2, 7) as b:
                n = body(b)
                assert n == DVE_STEPS, n
            count[0] += 5 * DVE_STEPS
            count[0] += body(7)
            count[0] += body(8)
            chain = Chain(9)
            for g, u in ((0, 2), (0, 6), (1, 0)):
                body_slot(chain, 9, g, u)

        @block.gpsimd
        def _(pool):
            G = nc.gpsimd

            def rsqrt(before, mv, rs, done, newton_step):
                k = [0]

                def step(ins):
                    k[0] += 1
                    ins.then_inc(newton_step, 1)
                    wait_apart(pool, newton_step, NEWTON * before + k[0], pool_passed)

                v, y, a = rs[:, 0, :], rs[:, 1, :], rs[:, 2, :]
                step(G.tensor_scalar(v, mv[:, :, 1], EPS, None, ALU.add))
                step(G.tensor_scalar(y.bitcast(I32), v.bitcast(I32), -0.5, RSQRT_MAGIC, ALU.mult, ALU.add))
                for it in range(3):
                    step(G.tensor_tensor(a, y, y, ALU.mult))
                    step(G.tensor_tensor(a, a, v, ALU.mult))
                    step(G.tensor_scalar(a, a, -0.5, 1.5, ALU.mult, ALU.add))
                    if it < 2:
                        step(G.tensor_tensor(y, y, a, ALU.mult))
                G.tensor_tensor(y, y, a, ALU.mult).then_inc(done, 1)

            NEWTON = 13

            def body_slot(b, g, u):
                s = 4 * b + g
                if (g, u) == (0, 1) and there(b, -1, 6):
                    wait(pool, mv1_done, b + 2)
                    wait_apart(pool, xn_done, b + 1, pool_passed)
                    rsqrt(b + 1, mv1, rs1, rs1_done, newton1)
                if (g, u) == (3, 4) and there(b, 1, 8):
                    wait(pool, mv2_done, b)
                    wait_apart(pool, h_done, b - 1, pool_passed)
                    rsqrt(b - 1, mv2, rs2, rs2_done, newton2)
                if g == 1 and u in (2, 3, 5, 6) and there(b, -1, 6):
                    n = (2, 3, 5, 6).index(u)
                    wait(pool, qk_out, 4 * b + 4 + n + 1)
                    wait(pool, rope_done, 4 * b + 4 + n - 1)
                    G.tensor_tensor(rope_c[:, n % 2, :], qk_b[:, n % 2, :], cos, ALU.mult).then_inc(cos_done, 1)
                if (g, u) in ((1, 5), (1, 6), (2, 0), (2, 1)) and there(b, -1, 6):
                    n = ((1, 5), (1, 6), (2, 0), (2, 1)).index((g, u))
                    wait(pool, rope_done, 4 * b + 4 + n + 1)
                    wait_apart(pool, st_hilo, 64 * (b + 1), pool_passed)
                    G.tensor_scalar(hilo[:, n, 0, :], rope_s[:, n % 2, :], 1.0, 0.0, ALU.mult, ALU.add)\
                        .then_inc(hilo_half, 1)
                    pool.wait_ge(hilo_half, 4 * b + 4 + n + 1)
                    G.tensor_tensor(hilo[:, n, 1, :], rope_s[:, n % 2, :], hilo[:, n, 0, :].bitcast(F32),
                                    ALU.subtract).then_inc(hilo_done, 1)
                if (g, u) == (2, 5) and there(b, 1, 8):
                    wait(pool, ld_xr, 16 * b)
                    G.tensor_tensor(xr[:], xr[:], bo_all[:].unsqueeze(1).to_broadcast([P, TT, C]), ALU.add)\
                        .then_inc(xr_done, 1)
                if g == 2 and there(b, 2, 9):
                    scatter(b, u)

            def scatter(b, n):
                if n == 0:
                    wait_apart(pool, put_done, b - 1, pool_passed)
                G.indirect_dma_start(out=rt["tok"], out_offset=bass.IndirectOffsetOnAxis(ap=put_at[:, n:n + 1], axis=0),
                                     in_=hn[:, n // K, :], in_offset=None, bounds_check=NSLOT - 1, oob_is_err=False)\
                    .then_inc(st_tok, 16)

            def body(b):
                for g in range(4):
                    for u in range(SLOTS):
                        body_slot(b, g, u)

            G.memset(kst[ZROW:ROWS].bitcast(F32), 1.0).then_inc(stack_set, 1)
            pool.wait_ge(stack_set, 1)
            G.memset(qst[ZROW:ROWS].bitcast(F32), 0.0).then_inc(stack_set, 1)
            pool.wait_ge(stack_set, 2)
            G.memset(zeros[:], 0.0).then_inc(z_ready, 1)
            pool.wait_ge(z_ready, 1)
            flat = rt["tok"].rearrange("n c -> (n c)").rearrange("(p x) -> p x", p=P)
            width = zeros.shape[1]
            for n in range(flat.shape[1] // width):
                pool.dma_start(flat[:, bass.ts(n, width)], zeros[:]).then_inc(st_zero, 16)
            for g, u in ((0, 1), (1, 2), (1, 3), (1, 5), (1, 6), (2, 0), (2, 1)):
                body_slot(-1, g, u)
            body(0)
            body(1)
            pool.wait_ge(st_zero, 16 * (flat.shape[1] // width))
            with pool.Fori(2, 7) as b:
                body(b)
            body(7)
            body(8)
            for n in range(TT * K):
                scatter(9, n)
            pool.wait_ge(st_tok, 16 * 8 * BATCH)


def constants():
    r = np.arange(P)
    inv = (np.float32(1.0) / np.float32(THETA) ** (np.arange(0, DH, 2, dtype=np.float32) / np.float32(DH)))
    freq = inv[(r % DH) // 2].astype(np.float32)
    ang = np.arange(T, dtype=np.float32)[None, :] * freq[:, None]
    table = np.zeros((P, NCONST), np.float32)
    table[:, COS:COS + T] = np.cos(ang)
    table[:, SIN:SIN + T] = np.sin(ang) * np.where(r % 2 == 0, -1.0, 1.0)[:, None]
    table[:, IDENT:IDENT + P] = np.eye(P)
    table[:, CAUSAL:CAUSAL + P] = np.where(r[None, :] > r[:, None], MASKED, 0.0)
    table[:, LATER:LATER + P] = np.where(r[:, None] > r[None, :], MASKED, 0.0)
    table[:, TRI:TRI + P] = r[:, None] < r[None, :]
    table[:, RANK:RANK + E] = E - np.arange(E)
    return table


def expert_phase(nc, d, rt):
    FULL = 3 * P
    BLK = ((0, FULL), (FULL, FULL), (2 * FULL, EROWS - 2 * FULL))
    WMAX = BLK[2][1]
    RING = 12
    NT = tuple(-(-w // P) for _, w in BLK)
    TB = (0, NT[0], NT[0] + NT[1])
    NTE = sum(NT)
    OB = 5
    WP = 2 * HID // 8
    ctx = ExitStack()
    with ctx:
        def sb(name, shape, dt=F32):
            return ctx.enter_context(nc.sbuf_tensor(name, shape, dt))

        def sem(name):
            return ctx.enter_context(nc.semaphore(name))

        ident = sb("ident_e", [P, P])
        raw = sb("raw", [P, 2, 2 * HID])
        w_hi = [[sb(f"w{kind}_hi{par}", [P, 2 * HID], F32R) for kind in "fgp"] for par in range(2)]
        w_lo = [[sb(f"w{kind}_lo{par}", [P, 2 * HID], F32R) for kind in "fgp"] for par in range(2)]
        b_fc = sb("b_fc", [P, E, HK])
        b_gate = sb("b_gate", [P, E, HK])
        b_proj = sb("b_proj", [P, 2, C])
        rows = sb("rows", [P, 2, 4, C])
        xh = sb("xh", [P, 2, CK, WMAX], F32R)
        xl = sb("xl", [P, 2, CK, WMAX], F32R)
        ah = sb("ah", [P, RING, WMAX], F32R)
        al = sb("al", [P, RING, WMAX], F32R)
        fc = sb("fc", [P, 2, WMAX])
        gated = sb("gated", [P, 2, WMAX])
        hid = sb("hid", [P, 2, WMAX])
        o_sb = sb("o_sb", [P, OB, C])
        ps = ctx.enter_context(nc.psum_tensor("ps_e", [P, 8, T], F32))
        FC, GATE, TURN, PROJ = 0, 2, 4, 6

        ld_once, ld_tail = sem("ld_once"), sem("ld_tail")
        ld_rows = [sem(f"ld_rows{i}") for i in range(2)]
        ld_raw = [sem(f"ld_raw{i}") for i in range(2)]
        ld_bp = [sem(f"ld_bp{i}") for i in range(2)]
        st_o = [sem(f"st_o{i}") for i in range(OB)]
        w_half, w_split, w_ready = sem("w_half"), sem("w_split"), sem("w_ready")
        turned, xh_done, xl_done = sem("turned"), sem("xh_done"), sem("xl_done")
        fc_done, gate_done, fc_out, gated_done = sem("fc_done"), sem("gate_done"), sem("fc_out"), sem("gated_done")
        hid_done, ah_done, al_done = sem("hid_done"), sem("ah_done"), sem("al_done")
        proj_done, tile_out = sem("proj_done"), sem("tile_out")
        act_passed, pool_passed = sem("act_passed"), sem("pool_passed_e")

        def step_of(e, n):
            return (e - 1, 2) if n < 0 else (e + 1, 0) if n > 2 else (e, n)

        def nth_weights(half, par, j):
            return 3 * half + (3 * par + j) // 2

        def nth_rows(half, par, n):
            return 3 * half + (3 * par + n) // 2

        def real(e):
            return not isinstance(e, int) or 0 <= e < E

        def experts(eng, body):
            body(0, 0)
            with eng.Fori(0, E // 2 - 1) as i:
                body(i, 1)
                body(i + 1, 0)
            body(E // 2 - 1, 1)

        def tiles(n):
            return [(k, min(P, BLK[n][1] - P * k)) for k in range(NT[n])]

        def side(par, n):
            return (3 * par + n) % 2

        def slots_at(name, e, off, size):
            return rt[name][bass.ds(e * EROWS + off, size), :]

        block = ctx.enter_context(nc.Block())

        @block.sync
        def _(sp):
            def load_rows(e, n, par):
                off, width = BLK[n]
                full = width // P
                sp.dma_start(rows[:, par, 0:full], slots_at("tok", e, off, full * P).rearrange("(k p) c -> p k c", p=P))\
                    .then_inc(ld_rows[par], 16)
                if width % P:
                    sp.dma_start(rows[0:width % P, par, full], slots_at("tok", e, off + full * P, width % P))\
                        .then_inc(ld_tail, 16)

            def load_weights(e, j, epar):
                src = d[("wf", "wg", "wp")[j]][e].rearrange("(k p) n -> p k n", p=P)
                dst = raw[:, (3 * epar + j) % 2, :].rearrange("p (k n) -> p k n", k=src.shape[1])
                sp.dma_start(dst, src).then_inc(ld_raw[(3 * epar + j) % 2], 16)

            def load_bias(e, epar):
                sp.dma_start(b_proj[:, epar, :], d["bp"][e].to_broadcast([P, C])).then_inc(ld_bp[epar], 16)

            def store(e, n):
                for k, size in tiles(n):
                    q = TB[n] + k
                    wait(sp, tile_out, NTE * e + q + 1)
                    sp.dma_start(slots_at("o", e, BLK[n][0] + P * k, size), o_sb[0:size, q % OB, :]).then_inc(st_o[q % OB], 16)

            def body(half, par):
                e = 2 * half + par
                for n in range(3):
                    e2, n2 = step_of(e, n + 1)
                    if real(e2):
                        if not (isinstance(e, int) and 3 * e + n < 1):
                            sp.wait_ge(turned, 2 * (3 * e + n))
                        load_rows(e2, n2, side(par, n + 1))
                    if real(e + 1):
                        sp.wait_ge(w_ready, 3 * e + n + 2)
                        load_weights(e + 1, n, 1 - par)
                    e0, n0 = step_of(e, n - 1)
                    if real(e0):
                        store(e0, n0)
                    if n == 0 and real(e + 1):
                        load_bias(e + 1, 1 - par)

            sp.dma_start(ident[:], d["consts"][:, IDENT:IDENT + P]).then_inc(ld_once, 16)
            load_rows(0, 0, 0)
            load_weights(0, 0, 0)
            load_weights(0, 1, 0)
            sp.dma_start(b_fc[:], d["bf"]).then_inc(ld_once, 16)
            sp.dma_start(b_gate[:], d["bg"]).then_inc(ld_once, 16)
            load_bias(0, 0)
            sp.wait_ge(w_ready, 1)
            load_weights(0, 2, 0)
            experts(sp, body)
            store(E - 1, 2)
            for stored in st_o:
                sp.wait_ge(stored, 16 * NTE // OB * E)

        @block.tensor
        def _(pe):
            mm = nc.tensor.matmul

            def product(out, pairs):
                terms = [(w[0], x[0]) for w, x in pairs] + [(w[1], x[0]) for w, x in pairs] + [(w[0], x[1]) for w, x in pairs]
                for i, (w, x) in enumerate(terms):
                    last = mm(out, w, x, start=(i == 0), stop=(i == len(terms) - 1))
                return last

            def turn(e, half, epar, n, c):
                par = side(epar, n)
                if c == 0:
                    pe.wait_ge(ld_rows[par], 16 * nth_rows(half, epar, n) + 16)
                    if n == 2:
                        pe.wait_ge(ld_tail, 16 * e + 16)
                if not (isinstance(e, int) and 3 * e + n < 1):
                    pe.wait_ge(xl_done, 2 * (3 * e + n - 1) + c + 1)
                for k, size in tiles(n):
                    last = nc.tensor.transpose(ps[:, TURN + c, P * k:P * k + size], rows[0:size, par, k, bass.ts(c, P)],
                                               ident[0:size, 0:size])
                last.then_inc(turned, 1)

            def up(e, n, par, hc):
                width, sd = BLK[n][1], side(par, n)
                u = 8 * (3 * e + n) + hc
                if hc == 0:
                    pe.wait_ge(xl_done, 2 * (3 * e + n) + 2)
                if n == 0 and hc == 0:
                    pe.wait_ge(w_ready, 3 * e + 2)
                for kind, bank, free, done in ((0, FC, fc_out, fc_done), (1, GATE, gated_done, gate_done)):
                    if not (isinstance(e, int) and u < 2):
                        pe.wait_ge(free, u - 1)
                    w = [w_[par][kind][:].rearrange("p (c n) -> p c n", c=CK) for w_ in (w_hi, w_lo)]
                    product(ps[:, bank + hc % 2, 0:width],
                            [([w_[:, c, bass.ts(hc, P)] for w_ in w], [x[:, sd, c, 0:width] for x in (xh, xl)])
                             for c in range(CK)]).then_inc(done, 1)

            def project(e, n, par):
                if n == 0:
                    pe.wait_ge(w_ready, 3 * e + 3)
                for k, size in tiles(n):
                    q = TB[n] + k
                    if not (isinstance(e, int) and NTE * e + q < 2):
                        pe.wait_ge(tile_out, NTE * e + q - 1)
                    if k == 0:
                        pe.wait_ge(al_done, 8 * (3 * e + n) + 8)
                    wh, wl = (w_[par][2][:].rearrange("p (h n) -> p h n", h=HK) for w_ in (w_hi, w_lo))
                    a = [[x[:, (8 * n + hc) % RING, P * k:P * k + size] for x in (ah, al)] for hc in range(HK)]
                    product(ps[0:size, PROJ + q % 2, 0:C],
                            [(a[hc], (wh[:, hc, :], wl[:, hc, :])) for hc in range(HK)]).then_inc(proj_done, 1)

            def body(half, par):
                e = 2 * half + par
                for n in range(3):
                    for hc in range(HK):
                        up(e, n, par, hc)
                        e0, n0 = step_of(e, n - 1)
                        if hc == 1 and real(e0):
                            project(e0, n0, par if n else 1 - par)
                        e2, n2 = step_of(e, n + 1)
                        if hc in (3, 5) and real(e2):
                            half2, par2 = (half, par) if n < 2 else (half + par, 1 - par)
                            turn(e2, half2, par2, n2, (hc - 3) // 2)

            pe.wait_ge(ld_once, 16 * 3)
            turn(0, 0, 0, 0, 0)
            turn(0, 0, 0, 0, 1)
            experts(pe, body)
            project(E - 1, 2, 1)

        def split_in(eng, e, n, par, c, high):
            k = 2 * (3 * e + n) + c
            width = BLK[n][1]
            src = ps[:, TURN + c, 0:width]
            if high:
                eng.wait_ge(turned, k + 1)
                nc.scalar.activation(xh[:, par, c, 0:width], src, ACT.Copy).then_inc(xh_done, 1)
            else:
                eng.wait_ge(xh_done, k + 1)
                nc.vector.tensor_tensor(xl[:, par, c, 0:width], src, xh[:, par, c, 0:width].bitcast(F32), ALU.subtract)\
                    .then_inc(xl_done, 1)

        @block.scalar
        def _(act):
            A = nc.scalar.activation

            def silu(e, n, hc):
                u = 8 * (3 * e + n) + hc
                n, hc = (n, hc) if hc >= 0 else ((n - 1) % 3, HK - 1)
                if isinstance(e, int) and u < 0:
                    return
                width = BLK[n][1]
                act.wait_ge(gated_done, u + 1)
                if not (isinstance(e, int) and u < 2):
                    act.wait_ge(al_done, u - 1)
                A(hid[:, hc % 2, 0:width], gated[:, hc % 2, 0:width], ACT.Silu).then_inc(hid_done, 1)

            def body(half, par):
                e = 2 * half + par
                for n in range(3):
                    width = BLK[n][1]
                    for hc in range(HK):
                        u = 8 * (3 * e + n) + hc
                        wait_apart(act, fc_done, u + 1, act_passed)
                        if not (isinstance(e, int) and u < 2):
                            wait_apart(act, gated_done, u - 1, act_passed)
                        A(fc[:, hc % 2, 0:width], ps[:, FC + hc % 2, 0:width], ACT.Identity,
                          bias=b_fc[:, e, hc:hc + 1]).then_inc(fc_out, 1)
                        silu(e, n, hc - 1)
                        e2, n2 = step_of(e, n + 1)
                        if hc in (4, 6) and real(e2):
                            split_in(act, e2, n2, side(par, n + 1), (hc - 4) // 2, True)

            act.wait_ge(ld_once, 16 * 3)
            for j in range(3):
                act.wait_ge(ld_raw[j % 2], 16 * (j // 2 + 1))
                A(w_hi[0][j][:], raw[:, j % 2, :], ACT.Copy).then_inc(w_half, 1)
                if j < 2:
                    split_in(act, 0, 0, 0, j, True)
            experts(act, body)
            silu(E, 0, -1)

        @block.vector
        def _(dve):
            V = nc.vector

            def hid_hi(e, n, hc):
                u = 8 * (3 * e + n) + hc
                if isinstance(e, int) and u < 0:
                    return
                e, n, hc = (e, n, hc) if hc >= 0 else (*step_of(e, n - 1), HK - 1)
                gone = NTE * e + (TB[n] if hc >= RING - HK else (-NT[2], 0, TB[1])[n])
                if not (isinstance(gone, int) and gone <= 0):
                    dve.wait_ge(proj_done, gone)
                width = BLK[n][1]
                dve.wait_ge(hid_done, u + 1)
                V.tensor_copy(ah[:, (8 * n + hc) % RING, 0:width], hid[:, hc % 2, 0:width]).then_inc(ah_done, 1)

            def tiles_out(e, half, n, par):
                if n == 0:
                    dve.wait_ge(ld_bp[par], 16 * half + 16)
                for k, size in tiles(n):
                    q = TB[n] + k
                    dve.wait_ge(proj_done, NTE * e + q + 1)
                    if not (isinstance(e, int) and NTE * e + q < OB):
                        dve.wait_ge(st_o[q % OB], 16 * (NTE // OB * e + q // OB))
                    V.tensor_tensor(o_sb[0:size, q % OB, :], ps[0:size, PROJ + q % 2, 0:C], b_proj[0:size, par, :],
                                    ALU.add).then_inc(tile_out, 1)

            def body(half, par):
                e = 2 * half + par
                for n in range(3):
                    width = BLK[n][1]
                    for hc in range(HK):
                        u = 8 * (3 * e + n) + hc
                        dve.wait_ge(gate_done, u + 1)
                        dve.wait_ge(fc_out, u + 1)
                        if not (isinstance(e, int) and u < 2):
                            dve.wait_ge(hid_done, u - 1)
                        V.scalar_tensor_tensor(gated[:, hc % 2, 0:width], ps[:, GATE + hc % 2, 0:width],
                                               b_gate[:, e, hc:hc + 1], fc[:, hc % 2, 0:width],
                                               ALU.add, ALU.mult).then_inc(gated_done, 1)
                        hid_hi(e, n, hc - 1)
                        e0, n0 = step_of(e, n - 1)
                        if hc == 1 and real(e0):
                            tiles_out(e0, half if n else half - (1 - par), n0, par if n else 1 - par)
                        e2, n2 = step_of(e, n + 1)
                        if hc in (5, 7) and real(e2):
                            split_in(dve, e2, n2, side(par, n + 1), (hc - 5) // 2, False)

            for j in range(3):
                dve.wait_ge(w_half, j + 1)
                V.tensor_tensor(w_lo[0][j][:], raw[:, j % 2, :], w_hi[0][j][:].bitcast(F32), ALU.subtract)\
                    .then_inc(w_ready, 1)
                if j < 2:
                    split_in(dve, 0, 0, 0, j, False)
            experts(dve, body)
            hid_hi(E, 0, -1)
            tiles_out(E - 1, E // 2 - 1, 2, 1)

        @block.gpsimd
        def _(pool):
            G = nc.gpsimd

            def hid_lo(e, n, hc):
                u = 8 * (3 * e + n) + hc
                if isinstance(e, int) and u < 0:
                    return
                n, hc = (n, hc) if hc >= 0 else ((n - 1) % 3, HK - 1)
                width, at = BLK[n][1], (8 * n + hc) % RING
                pool.wait_ge(ah_done, u + 1)
                G.tensor_tensor(al[:, at, 0:width], hid[:, hc % 2, 0:width], ah[:, at, 0:width].bitcast(F32),
                                ALU.subtract).then_inc(al_done, 1)

            def body(half, par):
                e = 2 * half + par
                """Beside the hidden chunks' low parts, a 24th of the next expert's weights is split a chunk."""
                for n in range(3):
                    for hc in range(HK):
                        ahead = real(e + 1)
                        cols = slice(WP * hc, WP * (hc + 1))
                        src = raw[:, (3 * (1 - par) + n) % 2, cols]
                        if ahead:
                            if hc == 0:
                                pool.wait_ge(ld_raw[(3 * (1 - par) + n) % 2], 16 * nth_weights(half + par, 1 - par, n) + 16)
                                if n < 2 and not (isinstance(e, int) and e < 1):
                                    pool.wait_ge(gate_done, 24 * e)
                                if n == 2 and not (isinstance(e, int) and e < 1):
                                    pool.wait_ge(proj_done, NTE * e)
                                if not isinstance(e, int):
                                    pool.sem_inc(pool_passed, 1)
                            G.tensor_scalar(w_hi[1 - par][n][:, cols], src, 1.0, 0.0, ALU.mult, ALU.add)\
                                .then_inc(w_split, 1)
                        hid_lo(e, n, hc - 1)
                        if ahead:
                            pool.wait_ge(w_split, 8 * (3 * e + n) + hc + 1)
                            ins = G.tensor_tensor(w_lo[1 - par][n][:, cols], src,
                                                  w_hi[1 - par][n][:, cols].bitcast(F32), ALU.subtract)
                            if hc == HK - 1:
                                ins.then_inc(w_ready, 1)

            experts(pool, body)
            hid_lo(E, 0, -1)


def combine_phase(nc, d, rt):
    ctx = ExitStack()
    with ctx:
        def sb(name, shape, dt=F32):
            return ctx.enter_context(nc.sbuf_tensor(name, shape, dt))

        def sem(name):
            return ctx.enter_context(nc.semaphore(name))

        NB = TT * K
        at = sb("at", [P, 2, NB], I32)
        got = sb("got", [P, 2, NB, C])
        x1 = sb("x1_c", [P, 2, TT, C])
        y = sb("y", [P, 2, TT, C])
        at_ready, summed, half = sem("at_ready"), sem("summed"), sem("half")
        pool_passed = sem("pool_passed_c")
        gathered = [sem(f"gathered{p}") for p in range(2)]
        ld_x1 = [sem(f"ld_x1_{p}") for p in range(2)]
        st_y = [sem(f"st_y{p}") for p in range(2)]
        block = ctx.enter_context(nc.Block())

        def batches(eng, body):
            for par in range(2):
                body(0, par)
            with eng.Fori(1, BATCH // 2 - 1) as i:
                for par in range(2):
                    body(i, par)
            for par in range(2):
                body(BATCH // 2 - 1, par)

        def first(i):
            return isinstance(i, int) and i == 0

        def final(i):
            return isinstance(i, int) and i == BATCH // 2 - 1

        @block.sync
        def _(sp):
            def store(b, par):
                sp.wait_ge(summed, b + 1)
                sp.dma_start(d["out"][bass.ts(b, T), :].rearrange("(t p) c -> p t c", p=P), y[:, par])\
                    .then_inc(st_y[par], 16)

            def body(i, par):
                b = 2 * i + par
                if not first(i):
                    sp.wait_ge(summed, b - 1)
                sp.dma_start(x1[:, par], rt["x1"][bass.ts(b, T), :].rearrange("(t p) c -> p t c", p=P))\
                    .then_inc(ld_x1[par], 16)
                if not first(i) or par:
                    store(b - 1, 1 - par)

            batches(sp, body)
            store(BATCH - 1, 1)
            for stored in st_y:
                sp.wait_ge(stored, 16 * BATCH // 2)

        @block.gpsimd
        def _(pool):
            def body(i, par):
                b = 2 * i + par
                wait_apart(pool, at_ready, b + 1, pool_passed)
                if not first(i):
                    wait_apart(pool, summed, b - 1, pool_passed)
                for n in range(NB):
                    nc.gpsimd.indirect_dma_start(
                        out=got[:, par, n, :], out_offset=None, in_=rt["o"],
                        in_offset=bass.IndirectOffsetOnAxis(ap=at[:, par, n:n + 1], axis=0),
                        bounds_check=NSLOT - 1, oob_is_err=False).then_inc(gathered[par], 16)

            batches(pool, body)

        @block.vector
        def _(dve):
            V = nc.vector

            def fetch(b, par):
                V.tensor_copy(at[:, par, :], rt["slot"][:, bass.ts(b, NB)]).then_inc(at_ready, 1)

            def body(i, par):
                b = 2 * i + par
                dve.wait_ge(gathered[par], 16 * NB * i + 16 * NB)
                dve.wait_ge(ld_x1[par], 16 * i + 16)
                if not final(i):
                    fetch(b + 2, par)
                if not first(i):
                    dve.wait_ge(st_y[par], 16 * i)
                for k, dst in ((0, half), (1, summed)):
                    for t in range(TT):
                        ins = V.scalar_tensor_tensor(y[:, par, t, :], got[:, par, K * t + k, :],
                                                     rt["prob"][:, bass.ds(b * NB + K * t + k, 1)],
                                                     (y if k else x1)[:, par, t, :], ALU.mult, ALU.add)
                    ins.then_inc(dst, 1)
                    if k == 0:
                        dve.wait_ge(half, b + 1)

            fetch(0, 0)
            fetch(1, 1)
            batches(dve, body)


def build(nc, d):
    ctx = ExitStack()
    with ctx:
        def dram(name, shape):
            return nc.dram_tensor(name, shape, F32, kind="Internal").ap()

        rt = {
            "qk": dram("qk_parts", [BATCH, 2, 2, C, T]),
            "x1": dram("x1_rows", [BATCH * T, C]),
            "tok": dram("slot_tokens", [NSLOT, C]),
            "o": dram("slot_outputs", [NSLOT, C]),
            "slot": ctx.enter_context(nc.sbuf_tensor("slot_all", [P, BATCH * TT * K], I32)),
            "prob": ctx.enter_context(nc.sbuf_tensor("prob_all", [P, BATCH * TT * K], F32)),
        }
        attention_phase(nc, d, rt)
        expert_phase(nc, d, rt)
        combine_phase(nc, d, rt)


def kernel(**inputs):
    import numpy as _np
    import concourse.bacc as _bacc
    from concourse import mybir as _mybir
    from concourse.bass_utils import run_bass_kernel_spmd as _run

    def attn(name):
        return _np.asarray(inputs["L0_attn_" + name])

    def ffn(name):
        return _np.asarray(inputs["L0_ffn_" + name])

    arrays = {
        "x": attn("x").reshape(BATCH * T, C),
        "wqT": attn("Wq").T, "wkT": attn("Wk").T, "wvT": attn("Wv").T, "woT": attn("Wo").T,
        "bq": attn("bq"), "bk": attn("bk"), "bv": attn("bv"), "bo": attn("bo"),
        "wr": ffn("router_w"), "rb": ffn("router_b"),
        "wf": ffn("w_c_fc"), "wg": ffn("w_gate"), "wp": ffn("w_c_proj"),
        "bf": ffn("b_c_fc").reshape(E, HK, P).transpose(2, 0, 1),
        "bg": ffn("b_gate").reshape(E, HK, P).transpose(2, 0, 1),
        "bp": ffn("b_c_proj"),
        "consts": constants(),
    }
    arrays = {"in_" + k: _np.ascontiguousarray(v) for k, v in arrays.items()}
    nc = _bacc.Bacc("TRN2", target_bir_lowering=False, num_devices=1)
    d = {k[3:]: nc.dram_tensor(k, v.shape, _mybir.dt.from_np(v.dtype), kind="ExternalInput").ap()
         for k, v in arrays.items()}
    d["out"] = nc.dram_tensor("out_rows", [BATCH * T, C], F32, kind="ExternalOutput").ap()
    build(nc, d)
    r = _run(nc, [arrays], core_ids=[0])
    return r.results[0]["out_rows"].reshape(BATCH, T, C)
```

```python
import concourse.bass as bass
from concourse import mybir
from contextlib import ExitStack

import numpy as np

F32 = mybir.dt.float32
F32R = mybir.dt.float32r
BF16 = mybir.dt.bfloat16
I32 = mybir.dt.int32
ALU = mybir.AluOpType
ACT = mybir.ActivationFunctionType
AXX = mybir.AxisListType.X

P = 128
BATCH, T, C = 8, 512, 256
TT = T // P
CK = C // P
HEADS, DH = 16, 16
GH = 4
NG = HEADS // GH
NP = 4
ZROW = NP * DH
MROW = ZROW + 1
ROWS = MROW + 1
SLOTS = 8
FILLS = 16
E, K, HID = 8, 2, 1024
CAP = int(1.2 * K * T // E)
EROWS = BATCH * CAP
NSLOT = E * EROWS
HK = HID // P
EPS = 1e-5
MASKED = -1e30
RSQRT_MAGIC = float(0x5F3759DF)
THETA = 10000.0

COS, SIN = 0, T
IDENT = 2 * T
CAUSAL = IDENT + P
LATER = CAUSAL + P
TRI = LATER + P
RANK = TRI + P
NCONST = RANK + E


def wait(eng, sem, n):
    if isinstance(n, int) and n <= 0:
        return
    eng.wait_ge(sem, n)


def wait_apart(eng, sem, n, passed):
    wait(eng, sem, n)
    if not isinstance(n, int):
        eng.sem_inc(passed, 1)


def there(b, first, last):
    return not isinstance(b, int) or first <= b <= last


def attention_phase(nc, d, rt):
    ctx = ExitStack()
    with ctx:
        def sb(name, shape, dt=F32):
            return ctx.enter_context(nc.sbuf_tensor(name, shape, dt))

        def sem(name):
            return ctx.enter_context(nc.semaphore(name))

        consts = sb("consts_sb", [P, NCONST])
        ident = consts[:, IDENT:IDENT + P]
        cos, sin = consts[:, COS:COS + T], consts[:, SIN:SIN + T]
        rank = consts[:, RANK:RANK + E]
        ident_bf = sb("ident_bf", [P, P], BF16)
        causal_bf = sb("causal_bf", [P, P], BF16)
        later_bf = sb("later_bf", [P, P], BF16)
        tri_bf = sb("tri_bf", [P, P], BF16)
        ones_bf = sb("ones_bf", [P, P], BF16)
        zeros = sb("zeros", [P, NSLOT * C // P // FILLS])
        wq = sb("wq_sb", [P, CK, C])
        wk = sb("wk_sb", [P, CK, C])
        wv = sb("wv_sb", [P, CK, C])
        wo = sb("wo_sb", [P, CK, C])
        wr = sb("wr_sb", [P, CK, 32])
        bqk = sb("bqk", [P, 4])
        bv_all = sb("bv_all", [P, C])
        bo_all = sb("bo_all", [P, C])
        rb_all = sb("rb_all", [P, E])

        x_in = sb("x_in", [P, TT, C])
        stats1 = sb("stats1", [P, TT, 6])
        mv1 = sb("mv1", [P, TT, 2])
        rs1 = sb("rs1", [P, 3, TT])
        xn = sb("xn", [P, TT, C])
        xnT = sb("xnT", [P, CK, T])
        qk_b = sb("qk_b", [P, 2, T])
        rope_c = sb("rope_c", [P, 2, T])
        rope_s = sb("rope_s", [P, 2, T])
        hilo = sb("hilo", [P, 4, 2, T], F32R)
        v_next = sb("v_next", [P, TT, C])
        v_sb = sb("v_sb", [P, TT, HEADS, 2 * DH])
        qst = sb("qst", [ROWS, NG, GH, T], F32R)
        kst = sb("kst", [ROWS, NG, GH, T], F32R)
        mx = sb("mx", [P, 2, TT, GH])
        negmax = sb("negmax", [GH, 2, T], F32R)
        probs = sb("probs", [P, 2, GH, T])
        pv_sb = sb("pv_sb", [P, T])
        rden = sb("rden", [P, TT, GH])
        attn = sb("attn", [P, TT, C])
        attnT = sb("attnT", [P, CK, T])
        xr = sb("xr", [P, TT, C])
        x1 = sb("x1", [P, TT, C])
        stats2 = sb("stats2", [P, TT, 6])
        mv2 = sb("mv2", [P, TT, 2])
        rs2 = sb("rs2", [P, 3, TT])
        hn = sb("hn", [P, TT, C])
        hT = sb("hT", [P, CK, T])
        lgT = sb("lgT", [P, P])
        logits = sb("logits", [P, TT, E])
        top = sb("top", [P, 2, TT])
        picked = sb("picked", [P, 2, TT])
        eq = sb("eq", [P, TT, E])
        onehot = sb("onehot", [P, TT, K, E])
        onehot_bf = sb("onehot_bf", [P, TT, K, E], BF16)
        posm = sb("posm", [P, TT, K, E])
        pos = sb("pos", [P, TT, K])
        over = sb("over", [P, TT, K])
        slot_f = sb("slot_f", [P, TT, K])
        base = sb("base", [P, 1])
        put_at = sb("put_at", [P, TT * K], I32)
        dlt = sb("dlt", [P, TT])
        ex = sb("ex", [P, TT])

        ps = ctx.enter_context(nc.psum_tensor("ps", [P, 8, T], F32))
        S1 = 0
        S2 = 4
        pvb = ps[:, 6, :]
        misc = ps[:, 7, :]

        ld_const, ld_w = sem("ld_const"), sem("ld_w")
        ld_x, ld_xr, st_x1 = sem("ld_x"), sem("ld_xr"), sem("st_x1")
        st_hilo = [sem(f"st_hilo{c}") for c in range(CK)]
        ld_stack = [sem(f"ld_stack{g}") for g in range(NG)]
        ld_max = sem("ld_max")
        st_zero, st_tok = sem("st_zero"), sem("st_tok")
        made, z_ready = sem("made"), sem("z_ready")
        ld_rows1, wr_set = sem("ld_rows1"), sem("wr_set")
        p1_done, p2_done, pv_done = sem("p1_done"), sem("p2_done"), sem("pv_done")
        maxT_done, atT_done = sem("maxT_done"), sem("atT_done")
        xT_done, qk_done, v_done = sem("xT_done"), sem("qk_done"), sem("v_done")
        oT_done, o_done, hT_done = sem("oT_done"), sem("o_done"), sem("hT_done")
        lt_done, lg_done, pf_done = sem("lt_done"), sem("lg_done"), sem("pf_done")
        exp_done, negmax_out, pv_out = sem("exp_done"), sem("negmax_out"), sem("pv_out")
        xT_out, qk_out, oT_out, hT_out = sem("xT_out"), sem("qk_out"), sem("oT_out"), sem("hT_out")
        lt_out, ex_done = sem("lt_out"), sem("ex_done")
        red_done, at_out, v_out, v_moved = sem("red_done"), sem("at_out"), sem("v_out"), sem("v_moved")
        o_out, lg_out, pf_out = sem("o_out"), sem("lg_out"), sem("pf_out")
        mv1_done, mv2_done, xn_done, h_done = sem("mv1_done"), sem("mv2_done"), sem("xn_done"), sem("h_done")
        sin_done, rope_done, oh_done, dlt_done, put_done = (sem("sin_done"), sem("rope_done"), sem("oh_done"),
                                                            sem("dlt_done"), sem("put_done"))
        rs1_done, rs2_done = sem("rs1_done"), sem("rs2_done")
        cos_done, hilo_done, xr_done = sem("cos_done"), sem("hilo_done"), sem("xr_done")
        dve_step, newton1, newton2 = sem("dve_step"), sem("newton1"), sem("newton2")
        hilo_half = sem("hilo_half")
        sp_passed, dve_passed, pool_passed = sem("sp_passed"), sem("dve_passed"), sem("pool_passed")

        PIECES = {
            (0, 0): ("M", 0), (0, 1): ("H", 0), (0, 2): ("H", 1), (0, 3): ("A", 0), (0, 4): ("L", 0), (0, 5): ("R", 0),
            (0, 6): ("X", 0), (0, 7): ("X", 1),
            (1, 0): ("M", 0), (1, 1): ("Q", 0), (1, 3): ("A", 0), (1, 4): ("Q", 1), (1, 6): ("Q", 2),
            (2, 0): ("M", 0), (2, 1): ("Q", 3), (2, 2): ("F", 0), (2, 3): ("A", 0), (2, 4): ("V", 0), (2, 5): ("T", 0),
            (2, 6): ("T", 1), (2, 7): ("V", 1),
            (3, 0): ("M", 0), (3, 1): ("O", 0), (3, 2): ("O", 1), (3, 3): ("A", 0),
        }
        Q_AT = ((1, 1), (1, 4), (1, 6), (2, 1))
        FIRST = [at for at in sorted(PIECES) if PIECES[at][0] in "XQV"]

        def bank_of(b, g, u):
            return ps[:, FIRST.index((g, u)), :] if isinstance(b, int) and b == -1 else misc

        def piece_there(b, g, kind):
            s = 4 * b + g
            return {
                "M": there(s, 1, 32) if isinstance(b, int) else True,
                "A": there(s, 3, 34) if isinstance(b, int) else True,
                "X": there(b, -1, 6), "Q": there(b, -1, 6), "V": there(b, -1, 6),
                "T": there(b, 1, 8), "O": there(b, 1, 8),
                "H": there(b, 2, 9), "L": there(b, 2, 9), "R": there(b, 2, 9), "F": there(b, 2, 9),
            }[kind]

        def freed(b, g, kind, n):
            return {
                "M": (negmax_out, 4 * b + g),
                "A": (at_out, 4 * b + g - 2),
                "X": (xT_out, 2 * b + 2 + n + 1),
                "Q": (qk_out, 4 * b + 4 + n + 1),
                "V": (v_out, 2 * b + 2 + n + 1),
                "T": (oT_out, 2 * b - 2 + n + 1),
                "O": (o_out, 2 * b - 2 + n + 1),
                "H": (hT_out, 2 * (b - 2) + n + 1),
                "L": (lt_out, b - 2 + 1),
                "R": (lg_out, b - 2 + 1),
                "F": (pf_out, b - 2 + 1),
            }[kind]

        def last_piece(b, g, u):
            if isinstance(b, int) and b == -1:
                return None
            keys = sorted(PIECES)
            at = keys.index((g, u))
            for back in range(1, 2 * len(keys)):
                k = at - back
                bb = b if k >= 0 else b - 1
                gg, uu = keys[k % len(keys)]
                kind, n = PIECES[gg, uu]
                if (not isinstance(bb, int) or bb >= -1) and piece_there(bb, gg, kind):
                    if isinstance(bb, int) and bb == -1 and kind not in "XQV":
                        continue
                    return freed(bb, gg, kind, n)
            return None

        block = ctx.enter_context(nc.Block())

        @block.sync
        def _(sp):
            def load_x(b):
                wait(sp, xn_done, b)
                sp.dma_start(x_in[:], d["x"][bass.ts(b, T), :].rearrange("(t p) c -> p t c", p=P)).then_inc(ld_x, 16)

            def store_hilo(b, n):
                wait(sp, hilo_done, 4 * b + n + 1)
                dst = rt["qk"][b, n % 2, :, bass.ts(n // 2, P), :]
                sp.dma_start(dst.rearrange("h p t -> p h t"), hilo[:, n].bitcast(F32)).then_inc(st_hilo[n // 2], 16)

            def load_stack(b, g):
                wait_apart(sp, st_hilo[g // 2], 32 * (b + 1), sp_passed)
                wait_apart(sp, p2_done, 16 * (4 * b + g - 3), sp_passed)
                for side, stack, parts in ((0, qst, (0, 1, 0, 1)), (1, kst, (0, 0, 1, 1))):
                    for c, part in enumerate(parts):
                        src = rt["qk"][b, side, part, bass.ts(g, GH * DH), :]
                        sp.dma_start(stack[c * DH:(c + 1) * DH, g].bitcast(F32), src.rearrange("(h d) t -> d h t", d=DH))\
                            .then_inc(ld_stack[g], 16)

            def send_max(b, g):
                s = 4 * b + g
                wait(sp, negmax_out, s)
                wait(sp, p2_done, 16 * (s - 4))
                sp.dma_start(qst[MROW:MROW + 1, (g - 1) % 4].bitcast(F32), negmax[:, (g - 1) % 2, :].bitcast(F32))\
                    .then_inc(ld_max, 16)

            def body(b):
                for g in range(4):
                    for u in range(SLOTS):
                        if u == 0 and g == 0 and there(b, 1, 6):
                            load_x(b + 1)
                        if u == 0 and g < 3 and there(b, 1, 7):
                            load_stack(b, g + 1)
                        if u == 0 and g == 3 and there(b, 0, 6):
                            load_stack(b + 1, 0)
                        if u == 1 and piece_there(b, g, "M"):
                            send_max(b, g)
                        if (g, u) == (2, 0) and there(b, 1, 8):
                            wait(sp, o_out, 2 * (b - 1))
                            sp.dma_start(xr[:], d["x"][bass.ts(b - 1, T), :].rearrange("(t p) c -> p t c", p=P))\
                                .then_inc(ld_xr, 16)
                        if (g, u) in ((1, 7), (2, 2), (2, 4), (3, 1)) and there(b, 0, 6):
                            store_hilo(b + 1, ((1, 7), (2, 2), (2, 4), (3, 1)).index((g, u)))
                        if (g, u) == (3, 4) and there(b, 1, 8):
                            wait(sp, o_out, 2 * b)
                            sp.dma_start(rt["x1"][bass.ts(b - 1, T), :].rearrange("(t p) c -> p t c", p=P), x1[:])\
                                .then_inc(st_x1, 16)

            load_x(0)
            sp.dma_start(consts[:], d["consts"]).then_inc(ld_const, 16)
            for w_sb, name in ((wq, "wqT"), (wk, "wkT"), (wv, "wvT"), (wo, "woT")):
                sp.dma_start(w_sb[:], d[name].rearrange("(k p) n -> p k n", p=P)).then_inc(ld_w, 16)
            load_x(1)
            for n in range(4):
                store_hilo(0, n)
                if n % 2:
                    load_stack(0, n - 1)
                    load_stack(0, n)
            body(0)
            body(1)
            with sp.Fori(2, 7) as b:
                body(b)
            body(7)
            body(8)
            sp.wait_ge(st_x1, 16 * BATCH)

        @block.tensor
        def _(pe):
            mm = nc.tensor.matmul

            def pass1(b, g, u):
                s = 4 * b + g
                i, pr = u // 2, u % 2
                if u == 0:
                    wait(pe, ld_stack[g], 128 * (b + 1))
                wait(pe, red_done, 8 * s + u - 1)
                width = max(2 * P, P * (i + 1))
                for hh in range(2):
                    h, bank = 2 * pr + hh, ps[:, S1 + 2 * (u % 2) + hh, :]
                    mm(bank[:, 0:width], qst[0:MROW, g, h, bass.ts(i, P)], kst[0:MROW, g, h, 0:width],
                       start=True, stop=False)
                    last = mm(bank[:, bass.ts(i, P)], ident_bf[:], causal_bf[:], start=False, stop=True)
                last.then_inc(p1_done, 1)

            def pass2(t, g, u):
                j, pr = u // 2, u % 2
                if u == 0:
                    wait(pe, ld_max, 16 * (t + 1))
                q0 = min(P * j, T - 2 * P)
                for hh in range(2):
                    h, n = 2 * pr + hh, 2 * u + hh
                    wait(pe, exp_done, 16 * t + n - 1)
                    mm(ps[:, S2 + hh, 0:T - q0], kst[0:ROWS, g, h, bass.ts(j, P)], qst[0:ROWS, g, h, q0:T],
                       start=True, stop=False)
                    mm(ps[:, S2 + hh, P * j - q0:P * (j + 1) - q0], ident_bf[:], later_bf[:], start=False, stop=True)\
                        .then_inc(p2_done, 1)

            def pv(t, bt, g, j):
                wait(pe, exp_done, 16 * t + 4 * j + 4)
                if j == 0:
                    wait(pe, pv_out, t)
                    if g == 0:
                        wait(pe, v_moved, bt + 1)
                for h in range(GH):
                    last = mm(pvb[32 * h:32 * h + 32, P * j:T], v_sb[:, j, GH * g + h, :], probs[:, j % 2, h, P * j:T],
                              start=(j == 0), stop=(j == TT - 1))
                last.then_inc(pv_done, 1)

            def turn(dst, src_of, n):
                for k in range(n):
                    last = nc.tensor.transpose(dst[:, bass.ts(k, P)], src_of(k), ident)
                return last

            def piece(b, g, u):
                kind, n = PIECES[g, u]
                if not piece_there(b, g, kind):
                    return
                s, misc = 4 * b + g, bank_of(b, g, u)
                free = last_piece(b, g, u)
                if free:
                    wait(pe, *free)
                if kind == "M":
                    wait(pe, red_done, 8 * s)
                    for i in range(TT):
                        last = nc.tensor.transpose(misc[0:GH, bass.ts(i, P)], mx[:, (g - 1) % 2, i, :], ident)
                    last.then_inc(maxT_done, 1)
                elif kind == "A":
                    wait(pe, pv_out, s - 2)
                    turn(misc, lambda k: pv_sb[:, bass.ts(k, P)], TT).then_inc(atT_done, 1)
                elif kind == "X":
                    wait(pe, xn_done, b + 2)
                    turn(misc, lambda k: xn[:, k, bass.ts(n, P)], TT).then_inc(xT_done, 1)
                elif kind == "Q":
                    wait(pe, xT_out, 2 * (b + 2))
                    w_sb = (wq, wk)[n % 2]
                    for c in range(CK):
                        last = mm(misc, w_sb[:, c, bass.ts(n // 2, P)], xnT[:, c, :], start=(c == 0), stop=(c == CK - 1))
                    last.then_inc(qk_done, 1)
                elif kind == "V":
                    for k in range(2):
                        for c in range(CK):
                            last = mm(misc[:, bass.ts(k, C)], xnT[:, c, bass.ts(2 * n + k, P)], wv[:, c, :],
                                      start=(c == 0), stop=(c == CK - 1))
                    last.then_inc(v_done, 1)
                elif kind == "T":
                    wait(pe, at_out, 4 * b)
                    turn(misc, lambda k: attn[:, k, bass.ts(n, P)], TT).then_inc(oT_done, 1)
                elif kind == "O":
                    wait(pe, oT_out, 2 * b)
                    for k in range(2):
                        for c in range(CK):
                            last = mm(misc[:, bass.ts(k, C)], attnT[:, c, bass.ts(2 * n + k, P)], wo[:, c, :],
                                      start=(c == 0), stop=(c == CK - 1))
                    last.then_inc(o_done, 1)
                elif kind == "H":
                    wait(pe, h_done, b - 1)
                    turn(misc, lambda k: hn[:, k, bass.ts(n, P)], TT).then_inc(hT_done, 1)
                elif kind == "L":
                    wait(pe, hT_out, 2 * (b - 1))
                    for c in range(CK):
                        for k in range(TT):
                            last = mm(misc[32 * k:32 * k + 32, 0:P], wr[:, c, :], hT[:, c, bass.ts(k, P)],
                                      start=(c == 0), stop=(c == CK - 1))
                    last.then_inc(lt_done, 1)
                elif kind == "R":
                    wait(pe, lt_out, b - 1)
                    turn(misc, lambda k: lgT[:], 1).then_inc(lg_done, 1)
                elif kind == "F":
                    wait(pe, oh_done, b - 1)
                    out = misc[:, 0:TT * K * E].rearrange("p (t k e) -> p t k e", t=TT, k=K)
                    flat = misc[:, 0:TT * K * E]
                    mm(flat, tri_bf[:], onehot_bf[:].rearrange("p t k e -> p (t k e)"), start=True, stop=False)
                    for j in range(TT - 1):
                        mm(out[:, j + 1:TT].rearrange("p t k e -> p t (k e)"), ones_bf[:],
                           onehot_bf[:, j].rearrange("p k e -> p (k e)")
                           .rearrange("p (a n) -> p a n", a=1).to_broadcast([P, TT - 1 - j, K * E]),
                           start=False, stop=False)
                    for j in range(TT):
                        last = mm(out[:, :, 1, :], ones_bf[:],
                                  onehot_bf[:, j, 0:1, :].to_broadcast([P, TT, E]), start=False, stop=(j == TT - 1))
                    last.then_inc(pf_done, 1)

            def body(b):
                for g in range(4):
                    s = 4 * b + g
                    for u in range(SLOTS):
                        if there(b, 0, 7):
                            pass1(b, g, u)
                        if not isinstance(b, int) or 0 <= s - 2 <= 31:
                            pass2(s - 2, (g - 2) % 4, u)
                        if u in (3, 5, 7) and (not isinstance(b, int) or 0 <= s - 2 <= 31):
                            pv(s - 2, b - (g < 2), (g - 2) % 4, (u - 3) // 2)
                        if u == 1 and (not isinstance(b, int) or 0 <= s - 3 <= 31):
                            pv(s - 3, b - (g < 3), (g - 3) % 4, 3)
                        if (g, u) in PIECES:
                            piece(b, g, u)

            pe.wait_ge(ld_const, 16)
            pe.wait_ge(ld_w, 16 * 12)
            for g, u in FIRST:
                piece(-1, g, u)
            pe.wait_ge(made, 5)
            pe.wait_ge(ld_rows1, 32)
            body(0)
            body(1)
            with pe.Fori(2, 7) as b:
                body(b)
            body(7)
            body(8)
            for g, u in sorted(PIECES):
                if PIECES[g, u][0] in "HLRF":
                    piece(9, g, u)

        @block.scalar
        def _(act):
            A = nc.scalar.activation

            def exps(t, u):
                j, pr = u // 2, u % 2
                q0 = min(P * j, T - 2 * P)
                for hh in range(2):
                    wait(act, p2_done, 16 * t + 2 * u + hh + 1)
                    if pr == 0 and hh == 0:
                        wait(act, pv_done, 4 * t + j - 1)
                    A(probs[:, j % 2, 2 * pr + hh, P * j:T], ps[:, S2 + hh, P * j - q0:T - q0], ACT.Exp,
                      scale=float(DH) ** -0.5).then_inc(exp_done, 1)

            def max_out(b, g):
                s = 4 * b + g
                wait(act, maxT_done, s)
                wait(act, p2_done, 16 * (s - 3) + 1)
                A(negmax[:, (g - 1) % 2, :], misc[0:GH, :], ACT.Copy, scale=-1.0).then_inc(negmax_out, 1)

            def body_slot(b, g, u):
                s = 4 * b + g
                if u == 1 and piece_there(b, g, "M"):
                    max_out(b, g)
                if u == 2 and (not isinstance(b, int) or 0 <= s - 3 <= 31):
                    wait(act, pv_done, 4 * (s - 2))
                    wait(act, atT_done, s - 3)
                    A(pv_sb[:], pvb, ACT.Copy).then_inc(pv_out, 1)
                if (g, u) in ((0, 7), (1, 0)) and piece_there(b, g, "X"):
                    n = g
                    wait(act, xT_done, 2 * b + 2 + n + 1)
                    wait(act, v_done, 2 * (b + 1))
                    A(xnT[:, n, :], bank_of(b, 0, 6 + n), ACT.Copy).then_inc(xT_out, 1)
                if (g, u - 1) in Q_AT and piece_there(b, g, "Q"):
                    n = Q_AT.index((g, u - 1))
                    wait(act, qk_done, 4 * b + 4 + n + 1)
                    wait(act, cos_done, 4 * b + 4 + n - 1)
                    wait(act, sin_done, 4 * b + 4 + n - 1)
                    part = 2 * (n % 2) + n // 2
                    A(qk_b[:, n % 2, :], bank_of(b, g, u - 1), ACT.Identity, bias=bqk[:, part:part + 1])\
                        .then_inc(qk_out, 1)
                if (g, u) in ((2, 6), (2, 7)) and piece_there(b, g, "T"):
                    n = u - 6
                    wait(act, oT_done, 2 * b - 2 + n + 1)
                    wait(act, o_done, 2 * (b - 1))
                    A(attnT[:, n, :], misc, ACT.Copy).then_inc(oT_out, 1)
                if (g, u) in ((0, 2), (0, 3)) and there(b, 2, 9):
                    n = u - 2
                    wait(act, hT_done, 2 * (b - 2) + n + 1)
                    A(hT[:, n, :], misc, ACT.Copy).then_inc(hT_out, 1)
                if (g, u) == (0, 5) and there(b, 2, 9):
                    wait(act, lt_done, b - 1)
                    A(lgT[:], misc[:, 0:P], ACT.Copy).then_inc(lt_out, 1)
                if (g, u) == (1, 4) and there(b, 2, 9):
                    wait(act, dlt_done, b - 1)
                    A(ex[:], dlt[:], ACT.Exp).then_inc(ex_done, 1)
                if not isinstance(b, int) or 0 <= s - 2 <= 31:
                    exps(s - 2, u)

            def body(b):
                for g in range(4):
                    for u in range(SLOTS):
                        body_slot(b, g, u)

            for n in range(CK):
                act.dma_start(bqk[:, n:n + 1], d["bq"][bass.ts(n, P)].rearrange("(p a) -> p a", a=1)).then_inc(ld_w, 16)
                act.dma_start(bqk[:, 2 + n:3 + n], d["bk"][bass.ts(n, P)].rearrange("(p a) -> p a", a=1))\
                    .then_inc(ld_w, 16)
            for all_rows, name in ((bv_all, "bv"), (bo_all, "bo"), (rb_all, "rb")):
                act.dma_start(all_rows[:], d[name].rearrange("(a n) -> a n", a=1).to_broadcast([P, all_rows.shape[1]]))\
                    .then_inc(ld_w, 16)
            act.wait_ge(wr_set, 1)
            act.dma_start(wr[:, :, 0:E], d["wr"].rearrange("(k p) n -> p k n", p=P)).then_inc(ld_w, 16)
            act.wait_ge(ld_w, 16 * 12)
            for g, u in ((0, 7), (1, 0), *((g, u + 1) for g, u in Q_AT)):
                body_slot(-1, g, u)
            body(0)
            body(1)
            with act.Fori(2, 7) as b:
                body(b)
            body(7)
            body(8)
            for g, u in ((0, 2), (0, 3), (0, 5), (1, 4)):
                body_slot(9, g, u)

        @block.vector
        def _(dve):
            V = nc.vector
            count = [0]

            def settle(steps_per_body, b, k, ins):
                ins.then_inc(dve_step, 1)
                dve.wait_ge(dve_step, (count[0] + k) if isinstance(b, int) else (count[0] + (b - 2) * steps_per_body + k))

            class Chain:
                def __init__(self, b):
                    self.b, self.k = b, 0

                def __call__(self, ins):
                    self.k += 1
                    settle(DVE_STEPS, self.b, self.k, ins)

            def layer_stats(chain, src, stats, mv, done):
                for k in range(TT):
                    ins = V.bn_stats(stats[:, k, :], src[:, k, :])
                chain(ins)
                if not isinstance(chain.b, int):
                    dve.sem_inc(dve_passed, 1)
                for k in range(TT):
                    ins = V.bn_aggr(mv[:, k, :], stats[:, k, :])
                ins.then_inc(done, 1)

            def normalise(dst, src, mv, rs, done):
                for k in range(TT):
                    ins = V.tensor_scalar(dst[:, k, :], src[:, k, :], mv[:, k, 0:1], rs[:, 1, k:k + 1],
                                          ALU.subtract, ALU.mult)
                ins.then_inc(done, 1)

            def choose(chain, b, k, src):
                chain(V.reduce_max(top[:, k, :], src, AXX))
                chain(V.tensor_tensor(eq[:], src, top[:, k, :].unsqueeze(2).to_broadcast([P, TT, E]), ALU.is_equal))
                chain(V.tensor_tensor(eq[:], eq[:], rank.unsqueeze(1).to_broadcast([P, TT, E]), ALU.mult))
                chain(V.reduce_max(picked[:, k, :], eq[:], AXX))
                chain(V.tensor_tensor(onehot[:, :, k, :], rank.unsqueeze(1).to_broadcast([P, TT, E]),
                                      picked[:, k, :].unsqueeze(2).to_broadcast([P, TT, E]), ALU.is_equal))

            def route(chain, b, part):
                if part == 0:
                    wait(dve, lg_done, b - 1)
                    V.tensor_tensor(logits[:], misc[:, 0:P].rearrange("p (t r) -> p t r", t=TT)[:, :, 0:E],
                                    rb_all[:].unsqueeze(1).to_broadcast([P, TT, E]), ALU.add).then_inc(lg_out, 1)
                    return
                if part == 1:
                    dve.wait_ge(lg_out, b - 1)
                    choose(chain, b, 0, logits[:])
                    return
                chain(V.scalar_tensor_tensor(logits[:], onehot[:, :, 0, :], -3e38, logits[:], ALU.mult, ALU.add))
                choose(chain, b, 1, logits[:])
                V.tensor_copy(onehot_bf[:], onehot[:]).then_inc(oh_done, 1)
                V.tensor_tensor(dlt[:], top[:, 1, :], top[:, 0, :], ALU.subtract).then_inc(dlt_done, 1)

            def probabilities(chain, b):
                wait(dve, ex_done, b - 1)
                pr = rt["prob"][:, bass.ts(b - 2, TT * K)].rearrange("p (t k) -> p t k", k=K)
                chain(V.tensor_scalar(dlt[:], ex[:], 1.0, None, ALU.add))
                chain(V.reciprocal(dlt[:], dlt[:]))
                chain(V.tensor_copy(pr[:, :, 0], dlt[:]))
                chain(V.tensor_tensor(pr[:, :, 1], ex[:], dlt[:], ALU.mult))

            def slots(chain, b, part):
                if part == 0:
                    wait(dve, pf_done, b - 1)
                    V.tensor_tensor(posm[:], misc[:, 0:TT * K * E].rearrange("p (t k e) -> p t k e", t=TT, k=K),
                                    onehot[:], ALU.mult).then_inc(pf_out, 1)
                    return
                dve.wait_ge(pf_out, b - 1)
                chain(V.reduce_sum(pos[:], posm[:], AXX))
                chain(V.tensor_scalar(over[:], pos[:], float(CAP - 1), float(NSLOT), ALU.is_gt, ALU.mult))
                chain(V.tensor_scalar(pos[:], pos[:], float(CAP - 1), base[:, 0:1], ALU.min, ALU.add))
                chain(V.scalar_tensor_tensor(slot_f[:], picked[:].rearrange("p k t -> p t k"), -float(EROWS),
                                             pos[:], ALU.mult, ALU.add))
                chain(V.tensor_copy(rt["slot"][:, bass.ts(b - 2, TT * K)], slot_f[:].rearrange("p t k -> p (t k)")))
                V.tensor_tensor(put_at[:].rearrange("p (t k) -> p t k", k=K), slot_f[:], over[:], ALU.add)\
                    .then_inc(put_done, 1)
                chain(V.tensor_scalar(base[:], base[:], float(CAP), None, ALU.add))

            def body_slot(chain, b, g, u):
                s = 4 * b + g
                if u == 4 and piece_there(b, g, "A"):
                    at = misc.rearrange("p (t h r) -> p t h r", t=TT, h=GH)
                    wait(dve, atT_done, s - 2)
                    chain(V.reciprocal(rden[:], at[:, :, :, DH]))
                    g3 = (g - 3) % 4
                    if g == 3:
                        wait(dve, oT_done, 2 * b)
                    V.tensor_tensor(attn[:, :, g3 * GH * DH:(g3 + 1) * GH * DH].rearrange("p t (h r) -> p t h r", h=GH),
                                    at[:, :, :, 0:DH], rden[:].unsqueeze(3).to_broadcast([P, TT, GH, DH]),
                                    ALU.mult).then_inc(at_out, 1)
                if (g, u) in ((2, 5), (3, 0)) and there(b, -1, 6):
                    n = g - 2
                    wait(dve, v_done, 2 * b + 2 + n + 1)
                    wait(dve, v_moved, b + 1)
                    V.tensor_tensor(v_next[:, 2 * n:2 * n + 2, :], bank_of(b, 2, 4 + 3 * n).rearrange("p (k c) -> p k c", k=2),
                                    bv_all[:].unsqueeze(1).to_broadcast([P, 2, C]), ALU.add).then_inc(v_out, 1)
                if (g, u) in ((3, 2), (3, 3)) and piece_there(b, g, "O"):
                    n = u - 2
                    wait(dve, o_done, 2 * b - 2 + n + 1)
                    wait(dve, xr_done, b)
                    wait(dve, st_x1, 16 * (b - 1))
                    V.tensor_tensor(x1[:, 2 * n:2 * n + 2, :], misc.rearrange("p (k c) -> p k c", k=2),
                                    xr[:, 2 * n:2 * n + 2, :], ALU.add).then_inc(o_out, 1)
                if (g, u) in ((0, 6), (0, 7), (1, 1)) and there(b, 2, 9):
                    route(chain, b, ((0, 6), (0, 7), (1, 1)).index((g, u)))
                if there(b, 0, 7):
                    wait(dve, p1_done, 8 * s + u + 1)
                    if u == 0:
                        wait(dve, maxT_done, s - 1)
                    i, pr = u // 2, u % 2
                    V.reduce_max(mx[:, g % 2, i, 2 * pr:2 * pr + 2],
                                 ps[:, S1 + 2 * (u % 2):S1 + 2 * (u % 2) + 2, 0:P * (i + 1)], AXX)\
                        .then_inc(red_done, 1)
                if (g, u) == (0, 0) and there(b, -1, 6):
                    wait(dve, ld_x, 16 * (b + 2))
                    layer_stats(chain, x_in, stats1, mv1, mv1_done)
                if (g, u) == (0, 5) and there(b, -1, 6):
                    wait(dve, rs1_done, b + 2)
                    wait(dve, xT_done, 2 * (b + 1))
                    normalise(xn, x_in, mv1, rs1, xn_done)
                if (g, u) == (1, 5) and there(b, 2, 9):
                    probabilities(chain, b)
                if g == 2 and u in (3, 6) and there(b, 2, 9):
                    slots(chain, b, u // 6)
                if (g, u) in ((1, 3), (1, 6), (2, 0), (2, 5)) and there(b, -1, 6):
                    n = ((1, 3), (1, 6), (2, 0), (2, 5)).index((g, u))
                    wait_apart(dve, qk_out, 4 * b + 4 + n + 1, dve_passed)
                    wait_apart(dve, hilo_done, 4 * b + 4 + n - 1, dve_passed)
                    chain(V.stream_shuffle(rope_s[:, n % 2, :], qk_b[:, n % 2, :], [i ^ 1 for i in range(32)]))
                    V.tensor_tensor(rope_s[:, n % 2, :], rope_s[:, n % 2, :], sin, ALU.mult).then_inc(sin_done, 1)
                if (g, u) in ((1, 4), (1, 7), (2, 1), (2, 7)) and there(b, -1, 6):
                    n = ((1, 4), (1, 7), (2, 1), (2, 7)).index((g, u))
                    wait(dve, sin_done, 4 * b + 4 + n + 1)
                    wait(dve, cos_done, 4 * b + 4 + n + 1)
                    V.tensor_tensor(rope_s[:, n % 2, :], rope_c[:, n % 2, :], rope_s[:, n % 2, :], ALU.add)\
                        .then_inc(rope_done, 1)
                if (g, u) == (2, 2) and there(b, 0, 7):
                    wait(dve, v_out, 2 * (b + 1))
                    wait(dve, pv_done, 16 * b)
                    V.tensor_copy(v_sb[:, :, :, 0:DH],
                                  v_next[:].rearrange("p t (h r) -> p t h r", h=HEADS)).then_inc(v_moved, 1)
                if (g, u) == (3, 3) and piece_there(b, g, "O"):
                    wait(dve, o_out, 2 * b)
                    layer_stats(chain, x1, stats2, mv2, mv2_done)
                if (g, u) == (3, 7) and piece_there(b, g, "O"):
                    wait(dve, rs2_done, b)
                    wait(dve, st_tok, 16 * 8 * (b - 1))
                    wait(dve, hT_done, 2 * (b - 1))
                    normalise(hn, x1, mv2, rs2, h_done)

            def body(b):
                chain = Chain(b)
                for g in range(4):
                    for u in range(SLOTS):
                        body_slot(chain, b, g, u)
                return chain.k

            DVE_STEPS = 4 + 1 + 1 + 11 + 4 + 6 + 4

            chain = Chain(0)
            V.memset(wr[:], 0.0).then_inc(wr_set, 1)
            body_slot(chain, -1, 0, 0)
            chain(V.memset(v_sb[:], 1.0))
            V.memset(ones_bf[:], 1.0).then_inc(made, 1)
            chain(V.memset(base[:], float(E * EROWS)))
            dve.wait_ge(ld_const, 16)
            body_slot(chain, -1, 0, 5)
            V.tensor_copy(ident_bf[:], ident).then_inc(made, 1)
            V.tensor_copy(causal_bf[:], consts[:, CAUSAL:CAUSAL + P]).then_inc(made, 1)
            V.tensor_copy(later_bf[:], consts[:, LATER:LATER + P]).then_inc(made, 1)
            V.tensor_copy(tri_bf[:], consts[:, TRI:TRI + P]).then_inc(made, 1)
            dve.wait_ge(ld_w, 16 * 12)
            for g, u in ((1, 3), (1, 4), (1, 6), (1, 7), (2, 0), (2, 1), (2, 5), (2, 7), (3, 0)):
                body_slot(chain, -1, g, u)
            count[0] += chain.k
            count[0] += body(0)
            count[0] += body(1)
            with dve.Fori(2, 7) as b:
                n = body(b)
                assert n == DVE_STEPS, n
            count[0] += 5 * DVE_STEPS
            count[0] += body(7)
            count[0] += body(8)
            chain = Chain(9)
            for g, u in ((0, 6), (0, 7), (1, 1), (2, 3), (2, 6), (1, 5)):
                body_slot(chain, 9, g, u)

        @block.gpsimd
        def _(pool):
            G = nc.gpsimd

            def rsqrt(before, mv, rs, done, newton_step):
                k = [0]

                def step(ins):
                    k[0] += 1
                    ins.then_inc(newton_step, 1)
                    wait_apart(pool, newton_step, NEWTON * before + k[0], pool_passed)

                v, y, a = rs[:, 0, :], rs[:, 1, :], rs[:, 2, :]
                step(G.tensor_scalar(v, mv[:, :, 1], EPS, None, ALU.add))
                step(G.tensor_scalar(y.bitcast(I32), v.bitcast(I32), -0.5, RSQRT_MAGIC, ALU.mult, ALU.add))
                for it in range(3):
                    step(G.tensor_tensor(a, y, y, ALU.mult))
                    step(G.tensor_tensor(a, a, v, ALU.mult))
                    step(G.tensor_scalar(a, a, -0.5, 1.5, ALU.mult, ALU.add))
                    if it < 2:
                        step(G.tensor_tensor(y, y, a, ALU.mult))
                G.tensor_tensor(y, y, a, ALU.mult).then_inc(done, 1)

            NEWTON = 13

            def body_slot(b, g, u):
                s = 4 * b + g
                if (g, u) == (0, 1) and there(b, -1, 6):
                    wait(pool, mv1_done, b + 2)
                    wait_apart(pool, xn_done, b + 1, pool_passed)
                    rsqrt(b + 1, mv1, rs1, rs1_done, newton1)
                if (g, u) == (3, 4) and there(b, 1, 8):
                    wait(pool, mv2_done, b)
                    wait_apart(pool, h_done, b - 1, pool_passed)
                    rsqrt(b - 1, mv2, rs2, rs2_done, newton2)
                if (g, u - 1) in Q_AT and there(b, -1, 6):
                    n = Q_AT.index((g, u - 1))
                    wait(pool, qk_out, 4 * b + 4 + n + 1)
                    wait(pool, rope_done, 4 * b + 4 + n - 1)
                    G.tensor_tensor(rope_c[:, n % 2, :], qk_b[:, n % 2, :], cos, ALU.mult).then_inc(cos_done, 1)
                if (g, u) in ((1, 5), (2, 0), (2, 2), (2, 7)) and there(b, -1, 6):
                    n = ((1, 5), (2, 0), (2, 2), (2, 7)).index((g, u))
                    wait(pool, rope_done, 4 * b + 4 + n + 1)
                    wait_apart(pool, st_hilo[n // 2], 32 * (b + 1), pool_passed)
                    G.tensor_scalar(hilo[:, n, 0, :], rope_s[:, n % 2, :], 1.0, 0.0, ALU.mult, ALU.add)\
                        .then_inc(hilo_half, 1)
                    pool.wait_ge(hilo_half, 4 * b + 4 + n + 1)
                    G.tensor_tensor(hilo[:, n, 1, :], rope_s[:, n % 2, :], hilo[:, n, 0, :].bitcast(F32),
                                    ALU.subtract).then_inc(hilo_done, 1)
                if (g, u) == (2, 5) and there(b, 1, 8):
                    wait(pool, ld_xr, 16 * b)
                    G.tensor_tensor(xr[:], xr[:], bo_all[:].unsqueeze(1).to_broadcast([P, TT, C]), ALU.add)\
                        .then_inc(xr_done, 1)
                if (2, 7) <= (g, u) < (3, 3) and there(b, 2, 9):
                    for n in range(2):
                        scatter(b, 2 * (8 * g + u - 23) + n)

            def scatter(b, n):
                if n == 0:
                    wait_apart(pool, put_done, b - 1, pool_passed)
                G.indirect_dma_start(out=rt["tok"], out_offset=bass.IndirectOffsetOnAxis(ap=put_at[:, n:n + 1], axis=0),
                                     in_=hn[:, n // K, :], in_offset=None, bounds_check=NSLOT - 1, oob_is_err=False)\
                    .then_inc(st_tok, 16)

            def fill(n):
                flat = rt["tok"].rearrange("n c -> (n c)").rearrange("(p x) -> p x", p=P)
                pool.wait_ge(z_ready, 1)
                pool.dma_start(flat[:, bass.ts(n, zeros.shape[1])], zeros[:]).then_inc(st_zero, 16)

            def body(b):
                for g in range(4):
                    for u in range(SLOTS):
                        body_slot(b, g, u)
                        if isinstance(b, int) and b < 2 and u in (0, 7):
                            fill(8 * b + 2 * g + u // 7)

            pool.dma_start(kst[ZROW:ROWS].rearrange("r g h t -> r (g h t)"),
                          d["rows"][1:2].bitcast(F32R).to_broadcast([2, NG * GH * T])).then_inc(ld_rows1, 16)
            pool.dma_start(qst[ZROW:MROW].rearrange("r g h t -> r (g h t)"), d["rows"][0:1].bitcast(F32R))\
                .then_inc(ld_rows1, 16)
            G.memset(zeros[:], 0.0).then_inc(z_ready, 1)
            for g, u in ((0, 1), (1, 2), (1, 5), (1, 7), (2, 0), (2, 2), (2, 7)):
                body_slot(-1, g, u)
            body(0)
            body(1)
            pool.wait_ge(st_zero, 16 * FILLS)
            with pool.Fori(2, 7) as b:
                body(b)
            body(7)
            body(8)
            for n in range(TT * K):
                scatter(9, n)
            pool.wait_ge(st_tok, 16 * 8 * BATCH)


def constants():
    r = np.arange(P)
    inv = (np.float32(1.0) / np.float32(THETA) ** (np.arange(0, DH, 2, dtype=np.float32) / np.float32(DH)))
    freq = inv[(r % DH) // 2].astype(np.float32)
    ang = np.arange(T, dtype=np.float32)[None, :] * freq[:, None]
    table = np.zeros((P, NCONST), np.float32)
    table[:, COS:COS + T] = np.cos(ang)
    table[:, SIN:SIN + T] = np.sin(ang) * np.where(r % 2 == 0, -1.0, 1.0)[:, None]
    table[:, IDENT:IDENT + P] = np.eye(P)
    table[:, CAUSAL:CAUSAL + P] = np.where(r[None, :] > r[:, None], MASKED, 0.0)
    table[:, LATER:LATER + P] = np.where(r[:, None] > r[None, :], MASKED, 0.0)
    table[:, TRI:TRI + P] = r[:, None] < r[None, :]
    table[:, RANK:RANK + E] = E - np.arange(E)
    return table


def expert_phase(nc, d, rt):
    FULL = 3 * P
    BLK = ((0, FULL), (FULL, FULL), (2 * FULL, EROWS - 2 * FULL))
    WMAX = BLK[2][1]
    RING = 12
    NT = tuple(-(-w // P) for _, w in BLK)
    TB = (0, NT[0], NT[0] + NT[1])
    NTE = sum(NT)
    OB = 5
    WP = 2 * HID // 8
    ctx = ExitStack()
    with ctx:
        def sb(name, shape, dt=F32):
            return ctx.enter_context(nc.sbuf_tensor(name, shape, dt))

        def sem(name):
            return ctx.enter_context(nc.semaphore(name))

        ident = sb("ident_e", [P, P])
        raw = sb("raw", [P, 2, 2 * HID])
        w_hi = [[sb(f"w{kind}_hi{par}", [P, 2 * HID], F32R) for kind in "fgp"] for par in range(2)]
        w_lo = [[sb(f"w{kind}_lo{par}", [P, 2 * HID], F32R) for kind in "fgp"] for par in range(2)]
        b_fc = sb("b_fc", [P, E, HK])
        b_gate = sb("b_gate", [P, E, HK])
        b_proj = sb("b_proj", [P, 2, C])
        rows = sb("rows", [P, 2, 4, C])
        xh = sb("xh", [P, 2, CK, WMAX], F32R)
        xl = sb("xl", [P, 2, CK, WMAX], F32R)
        ah = sb("ah", [P, RING, WMAX], F32R)
        al = sb("al", [P, RING, WMAX], F32R)
        fc = sb("fc", [P, 2, WMAX])
        gated = sb("gated", [P, 2, WMAX])
        hid = sb("hid", [P, 2, WMAX])
        o_sb = sb("o_sb", [P, OB, C])
        ps = ctx.enter_context(nc.psum_tensor("ps_e", [P, 8, T], F32))
        FC, GATE, TURN, PROJ = 0, 2, 4, 6

        ld_once, ld_tail = sem("ld_once"), sem("ld_tail")
        ld_rows = [sem(f"ld_rows{i}") for i in range(2)]
        ld_raw = [sem(f"ld_raw{i}") for i in range(2)]
        ld_bp = [sem(f"ld_bp{i}") for i in range(2)]
        st_o = [sem(f"st_o{i}") for i in range(OB)]
        w_half, w_split, w_ready = sem("w_half"), sem("w_split"), sem("w_ready")
        turned, xh_done, xl_done = sem("turned"), sem("xh_done"), sem("xl_done")
        fc_done, gate_done, fc_out, gated_done = sem("fc_done"), sem("gate_done"), sem("fc_out"), sem("gated_done")
        hid_done, ah_done, al_done = sem("hid_done"), sem("ah_done"), sem("al_done")
        LAST = E - 1
        NB = TT * K
        got = [w_[0][kind][:].bitcast(F32).rearrange("p (n c) -> p n c", n=NB) for w_ in (w_hi, w_lo) for kind in range(3)]
        y = [raw[:, i // 2, :].rearrange("p (i t c) -> p i t c", i=2, t=TT)[:, i % 2] for i in range(4)]
        gathered = [sem(f"gathered{i}") for i in range(len(got))]
        ld_y = [sem(f"ld_y{i}") for i in range(len(y))]
        st_y = [sem(f"st_y{i}") for i in range(len(y))]
        summed, first_sum = sem("summed"), sem("first_sum")
        proj_done, tile_out = sem("proj_done"), sem("tile_out")
        act_passed, pool_passed = sem("act_passed"), sem("pool_passed_e")

        def step_of(e, n):
            return (e - 1, 2) if n < 0 else (e + 1, 0) if n > 2 else (e, n)

        def nth_weights(half, par, j):
            return 3 * half + (3 * par + j) // 2

        def nth_rows(half, par, n):
            return 3 * half + (3 * par + n) // 2

        def real(e):
            return not isinstance(e, int) or 0 <= e < E

        def experts(eng, body):
            body(0, 0)
            with eng.Fori(0, E // 2 - 1) as i:
                body(i, 1)
                body(i + 1, 0)
            body(E // 2 - 1, 1)

        def tiles(n):
            return [(k, min(P, BLK[n][1] - P * k)) for k in range(NT[n])]

        def side(par, n):
            return (3 * par + n) % 2

        def slots_at(name, e, off, size):
            return rt[name][bass.ds(e * EROWS + off, size), :]

        block = ctx.enter_context(nc.Block())

        @block.sync
        def _(sp):
            def load_rows(e, n, par):
                off, width = BLK[n]
                full = width // P
                sp.dma_start(rows[:, par, 0:full], slots_at("tok", e, off, full * P).rearrange("(k p) c -> p k c", p=P))\
                    .then_inc(ld_rows[par], 16)
                if width % P:
                    sp.dma_start(rows[0:width % P, par, full], slots_at("tok", e, off + full * P, width % P))\
                        .then_inc(ld_tail, 16)

            def load_weights(e, j, epar):
                src = d[("wf", "wg", "wp")[j]][e].rearrange("(k p) n -> p k n", p=P)
                dst = raw[:, (3 * epar + j) % 2, :].rearrange("p (k n) -> p k n", k=src.shape[1])
                sp.dma_start(dst, src).then_inc(ld_raw[(3 * epar + j) % 2], 16)

            def load_bias(e, epar):
                sp.dma_start(b_proj[:, epar, :], d["bp"][e].to_broadcast([P, C])).then_inc(ld_bp[epar], 16)

            def store(e, n):
                for k, size in tiles(n):
                    q = TB[n] + k
                    wait(sp, tile_out, NTE * e + q + 1)
                    sp.dma_start(slots_at("o", e, BLK[n][0] + P * k, size), o_sb[0:size, q % OB, :]).then_inc(st_o[q % OB], 16)

            def body(half, par):
                e = 2 * half + par
                for n in range(3):
                    e2, n2 = step_of(e, n + 1)
                    if real(e2):
                        if not (isinstance(e, int) and 3 * e + n < 1):
                            sp.wait_ge(turned, 2 * (3 * e + n))
                        load_rows(e2, n2, side(par, n + 1))
                    if real(e + 1):
                        sp.wait_ge(w_ready, 3 * e + n + 2)
                        load_weights(e + 1, n, 1 - par)
                    e0, n0 = step_of(e, n - 1)
                    if real(e0):
                        store(e0, n0)
                    if n == 0 and real(e + 1):
                        load_bias(e + 1, 1 - par)

            sp.dma_start(ident[:], d["consts"][:, IDENT:IDENT + P]).then_inc(ld_once, 16)
            load_rows(0, 0, 0)
            load_weights(0, 0, 0)
            load_weights(0, 1, 0)
            sp.dma_start(b_fc[:], d["bf"]).then_inc(ld_once, 16)
            sp.dma_start(b_gate[:], d["bg"]).then_inc(ld_once, 16)
            load_bias(0, 0)
            sp.wait_ge(w_ready, 1)
            load_weights(0, 2, 0)
            experts(sp, body)
            store(LAST, 2)
            for stored in st_o:
                sp.wait_ge(stored, 16 * NTE // OB * E)
            for stored in st_y:
                sp.wait_ge(stored, 16 * BATCH // len(y))

        @block.tensor
        def _(pe):
            mm = nc.tensor.matmul

            def product(out, pairs):
                terms = [(w[0], x[0]) for w, x in pairs] + [(w[1], x[0]) for w, x in pairs] + [(w[0], x[1]) for w, x in pairs]
                for i, (w, x) in enumerate(terms):
                    last = mm(out, w, x, start=(i == 0), stop=(i == len(terms) - 1))
                return last

            def turn(e, half, epar, n, c):
                par = side(epar, n)
                if c == 0:
                    pe.wait_ge(ld_rows[par], 16 * nth_rows(half, epar, n) + 16)
                    if n == 2:
                        pe.wait_ge(ld_tail, 16 * e + 16)
                if not (isinstance(e, int) and 3 * e + n < 1):
                    pe.wait_ge(xl_done, 2 * (3 * e + n - 1) + c + 1)
                for k, size in tiles(n):
                    last = nc.tensor.transpose(ps[:, TURN + c, P * k:P * k + size], rows[0:size, par, k, bass.ts(c, P)],
                                               ident[0:size, 0:size])
                last.then_inc(turned, 1)

            def up(e, n, par, hc):
                width, sd = BLK[n][1], side(par, n)
                u = 8 * (3 * e + n) + hc
                if hc == 0:
                    pe.wait_ge(xl_done, 2 * (3 * e + n) + 2)
                if n == 0 and hc == 0:
                    pe.wait_ge(w_ready, 3 * e + 2)
                for kind, bank, free, done in ((0, FC, fc_out, fc_done), (1, GATE, gated_done, gate_done)):
                    if not (isinstance(e, int) and u < 2):
                        pe.wait_ge(free, u - 1)
                    w = [w_[par][kind][:].rearrange("p (c n) -> p c n", c=CK) for w_ in (w_hi, w_lo)]
                    product(ps[:, bank + hc % 2, 0:width],
                            [([w_[:, c, bass.ts(hc, P)] for w_ in w], [x[:, sd, c, 0:width] for x in (xh, xl)])
                             for c in range(CK)]).then_inc(done, 1)

            def project(e, n, par):
                if n == 0:
                    pe.wait_ge(w_ready, 3 * e + 3)
                for k, size in tiles(n):
                    q = TB[n] + k
                    if not (isinstance(e, int) and NTE * e + q < 2):
                        pe.wait_ge(tile_out, NTE * e + q - 1)
                    if k == 0:
                        pe.wait_ge(al_done, 8 * (3 * e + n) + 8)
                    wh, wl = (w_[par][2][:].rearrange("p (h n) -> p h n", h=HK) for w_ in (w_hi, w_lo))
                    a = [[x[:, (8 * n + hc) % RING, P * k:P * k + size] for x in (ah, al)] for hc in range(HK)]
                    product(ps[0:size, PROJ + q % 2, 0:C],
                            [(a[hc], (wh[:, hc, :], wl[:, hc, :])) for hc in range(HK)]).then_inc(proj_done, 1)

            def body(half, par):
                e = 2 * half + par
                for n in range(3):
                    for hc in range(HK):
                        up(e, n, par, hc)
                        e0, n0 = step_of(e, n - 1)
                        if hc == 2 and real(e0):
                            project(e0, n0, par if n else 1 - par)
                        e2, n2 = step_of(e, n + 1)
                        if hc in (2, 4) and real(e2):
                            half2, par2 = (half, par) if n < 2 else (half + par, 1 - par)
                            turn(e2, half2, par2, n2, (hc - 2) // 2)

            pe.wait_ge(ld_once, 16 * 3)
            turn(0, 0, 0, 0, 0)
            turn(0, 0, 0, 0, 1)
            experts(pe, body)
            project(E - 1, 2, 1)

        def split_in(eng, e, n, par, c, high):
            k = 2 * (3 * e + n) + c
            width = BLK[n][1]
            src = ps[:, TURN + c, 0:width]
            if high:
                eng.wait_ge(turned, k + 1)
                nc.scalar.activation(xh[:, par, c, 0:width], src, ACT.Copy).then_inc(xh_done, 1)
            else:
                eng.wait_ge(xh_done, k + 1)
                nc.vector.tensor_tensor(xl[:, par, c, 0:width], src, xh[:, par, c, 0:width].bitcast(F32), ALU.subtract)\
                    .then_inc(xl_done, 1)

        @block.scalar
        def _(act):
            A = nc.scalar.activation

            def silu(e, n, hc):
                u = 8 * (3 * e + n) + hc
                n, hc = (n, hc) if hc >= 0 else ((n - 1) % 3, HK - 1)
                if isinstance(e, int) and u < 0:
                    return
                width = BLK[n][1]
                act.wait_ge(gated_done, u + 1)
                if not (isinstance(e, int) and u < 2):
                    act.wait_ge(al_done, u - 1)
                A(hid[:, hc % 2, 0:width], gated[:, hc % 2, 0:width], ACT.Silu).then_inc(hid_done, 1)

            def body(half, par):
                e = 2 * half + par
                for n in range(3):
                    width = BLK[n][1]
                    for hc in range(HK):
                        u = 8 * (3 * e + n) + hc
                        wait_apart(act, fc_done, u + 1, act_passed)
                        if not (isinstance(e, int) and u < 2):
                            wait_apart(act, gated_done, u - 1, act_passed)
                        A(fc[:, hc % 2, 0:width], ps[:, FC + hc % 2, 0:width], ACT.Identity,
                          bias=b_fc[:, e, hc:hc + 1]).then_inc(fc_out, 1)
                        silu(e, n, hc - 1)
                        e2, n2 = step_of(e, n + 1)
                        if hc in (3, 5) and real(e2):
                            split_in(act, e2, n2, side(par, n + 1), (hc - 3) // 2, True)

            act.wait_ge(ld_once, 16 * 3)
            for j in range(3):
                act.wait_ge(ld_raw[j % 2], 16 * (j // 2 + 1))
                A(w_hi[0][j][:], raw[:, j % 2, :], ACT.Copy).then_inc(w_half, 1)
                if j < 2:
                    split_in(act, 0, 0, 0, j, True)
            experts(act, body)
            silu(E, 0, -1)

            def batch_rows(name, b):
                return name[bass.ts(b, T), :].rearrange("(t p) c -> p t c", p=P)

            def load_y(b):
                act.dma_start(y[b % 4], batch_rows(rt["x1"], b)).then_inc(ld_y[b % 4], 16)

            act.wait_ge(w_ready, 3 * E)
            for b in range(4):
                load_y(b)
            for b in range(BATCH):
                act.wait_ge(summed, b + 1)
                act.dma_start(batch_rows(d["out"], b), y[b % 4]).then_inc(st_y[b % 4], 16)
                if 0 < b < 5:
                    act.wait_ge(st_y[b - 1], 16)
                    load_y(b + 3)

        @block.vector
        def _(dve):
            V = nc.vector

            def hid_hi(e, n, hc):
                u = 8 * (3 * e + n) + hc
                if isinstance(e, int) and u < 0:
                    return
                e, n, hc = (e, n, hc) if hc >= 0 else (*step_of(e, n - 1), HK - 1)
                gone = NTE * e + (TB[n] if hc >= RING - HK else (-NT[2], 0, TB[1])[n])
                if not (isinstance(gone, int) and gone <= 0):
                    dve.wait_ge(proj_done, gone)
                width = BLK[n][1]
                dve.wait_ge(hid_done, u + 1)
                V.tensor_copy(ah[:, (8 * n + hc) % RING, 0:width], hid[:, hc % 2, 0:width]).then_inc(ah_done, 1)

            def hid_lo(n, hc):
                u = 8 * (3 * LAST + n) + hc
                n, hc = (n, hc) if hc >= 0 else (n - 1, HK - 1)
                width, at = BLK[n][1], (8 * n + hc) % RING
                dve.wait_ge(ah_done, u + 1)
                dve.wait_ge(al_done, u)
                V.tensor_tensor(al[:, at, 0:width], hid[:, hc % 2, 0:width], ah[:, at, 0:width].bitcast(F32),
                                ALU.subtract).then_inc(al_done, 1)

            def combine(b):
                dve.wait_ge(gathered[b % len(got)], 16 * NB * (b // len(got) + 1))
                dve.wait_ge(ld_y[b % 4], 16 * (b // 4 + 1))
                for k, done in ((0, first_sum), (1, summed)):
                    for t in range(TT):
                        col = b * NB + K * t + k
                        ins = V.scalar_tensor_tensor(y[b % 4][:, t, :], got[b % len(got)][:, K * t + k, :],
                                                     rt["prob"][:, col:col + 1], y[b % 4][:, t, :], ALU.mult, ALU.add)
                    ins.then_inc(done, 1)
                    if k == 0:
                        dve.wait_ge(first_sum, b + 1)

            def tiles_out(e, half, n, par):
                if n == 0:
                    dve.wait_ge(ld_bp[par], 16 * half + 16)
                for k, size in tiles(n):
                    q = TB[n] + k
                    dve.wait_ge(proj_done, NTE * e + q + 1)
                    if not (isinstance(e, int) and NTE * e + q < OB):
                        dve.wait_ge(st_o[q % OB], 16 * (NTE // OB * e + q // OB))
                    V.tensor_tensor(o_sb[0:size, q % OB, :], ps[0:size, PROJ + q % 2, 0:C], b_proj[0:size, par, :],
                                    ALU.add).then_inc(tile_out, 1)

            def body(half, par):
                e = 2 * half + par
                for n in range(3):
                    width = BLK[n][1]
                    for hc in range(HK):
                        u = 8 * (3 * e + n) + hc
                        dve.wait_ge(gate_done, u + 1)
                        dve.wait_ge(fc_out, u + 1)
                        if not (isinstance(e, int) and u < 2):
                            dve.wait_ge(hid_done, u - 1)
                        V.scalar_tensor_tensor(gated[:, hc % 2, 0:width], ps[:, GATE + hc % 2, 0:width],
                                               b_gate[:, e, hc:hc + 1], fc[:, hc % 2, 0:width],
                                               ALU.add, ALU.mult).then_inc(gated_done, 1)
                        hid_hi(e, n, hc - 1)
                        if isinstance(e, int) and e == LAST and 8 * n + hc > 8:
                            hid_lo(n, hc - 1)
                        e0, n0 = step_of(e, n - 1)
                        if hc == 2 and real(e0):
                            tiles_out(e0, half if n else half - (1 - par), n0, par if n else 1 - par)
                        e2, n2 = step_of(e, n + 1)
                        if hc in (4, 6) and real(e2):
                            split_in(dve, e2, n2, side(par, n + 1), (hc - 4) // 2, False)

            for j in range(3):
                dve.wait_ge(w_half, j + 1)
                V.tensor_tensor(w_lo[0][j][:], raw[:, j % 2, :], w_hi[0][j][:].bitcast(F32), ALU.subtract)\
                    .then_inc(w_ready, 1)
                if j < 2:
                    split_in(dve, 0, 0, 0, j, False)
            experts(dve, body)
            hid_hi(E, 0, -1)
            hid_lo(3, -1)
            tiles_out(LAST, LAST // 2, 2, 1)
            for b in range(BATCH):
                combine(b)

        @block.gpsimd
        def _(pool):
            G = nc.gpsimd

            def hid_lo(e, n, hc):
                u = 8 * (3 * e + n) + hc
                if isinstance(e, int) and u < 0:
                    return
                n, hc = (n, hc) if hc >= 0 else ((n - 1) % 3, HK - 1)
                width, at = BLK[n][1], (8 * n + hc) % RING
                pool.wait_ge(ah_done, u + 1)
                G.tensor_tensor(al[:, at, 0:width], hid[:, hc % 2, 0:width], ah[:, at, 0:width].bitcast(F32),
                                ALU.subtract).then_inc(al_done, 1)

            def body(half, par):
                e = 2 * half + par
                """Beside the hidden chunks' low parts, a 24th of the next expert's weights is split a chunk."""
                for n in range(3 if real(e + 1) else 1):
                    for hc in range(HK):
                        ahead = real(e + 1)
                        cols = slice(WP * hc, WP * (hc + 1))
                        src = raw[:, (3 * (1 - par) + n) % 2, cols]
                        if ahead:
                            if hc == 0:
                                pool.wait_ge(ld_raw[(3 * (1 - par) + n) % 2], 16 * nth_weights(half + par, 1 - par, n) + 16)
                                if n < 2 and not (isinstance(e, int) and e < 1):
                                    pool.wait_ge(gate_done, 24 * e)
                                if n == 2 and not (isinstance(e, int) and e < 1):
                                    pool.wait_ge(proj_done, NTE * e)
                                if not isinstance(e, int):
                                    pool.sem_inc(pool_passed, 1)
                            G.tensor_scalar(w_hi[1 - par][n][:, cols], src, 1.0, 0.0, ALU.mult, ALU.add)\
                                .then_inc(w_split, 1)
                        hid_lo(e, n, hc - 1)
                        if ahead:
                            pool.wait_ge(w_split, 8 * (3 * e + n) + hc + 1)
                            ins = G.tensor_tensor(w_lo[1 - par][n][:, cols], src,
                                                  w_hi[1 - par][n][:, cols].bitcast(F32), ALU.subtract)
                            if hc == HK - 1:
                                ins.then_inc(w_ready, 1)

            def stored(q):
                pool.wait_ge(st_o[q % OB], 16 * (NTE // OB * LAST + q // OB + 1))

            def gather(b):
                buf = b % len(got)
                if b >= len(got):
                    pool.wait_ge(summed, b - len(got) + 1)
                there_now = LAST * EROWS + (b + 1) * CAP
                for n in range(NB):
                    G.indirect_dma_start(
                        out=got[buf][:, n, :], out_offset=None, in_=rt["o"][0:there_now],
                        in_offset=bass.IndirectOffsetOnAxis(ap=rt["slot"][:, b * NB + n:b * NB + n + 1], axis=0),
                        bounds_check=there_now - 1, oob_is_err=False).then_inc(gathered[buf], 16)

            experts(pool, body)
            hid_lo(LAST, 1, -1)
            pool.wait_ge(gate_done, 24 * LAST)
            pool.wait_ge(proj_done, NTE * LAST)
            for i in range(OB):
                pool.wait_ge(st_o[i], 16 * NTE // OB * LAST)
            rows_out = 0
            for b in range(BATCH):
                for q in range(NTE):
                    n = max(n for n in range(3) if TB[n] <= q)
                    first_row = BLK[n][0] + P * (q - TB[n])
                    if rows_out <= first_row < (b + 1) * CAP:
                        stored(q)
                rows_out = (b + 1) * CAP
                gather(b)


def build(nc, d):
    ctx = ExitStack()
    with ctx:
        def dram(name, shape):
            return nc.dram_tensor(name, shape, F32, kind="Internal").ap()

        rt = {
            "qk": dram("qk_parts", [BATCH, 2, 2, C, T]),
            "x1": dram("x1_rows", [BATCH * T, C]),
            "tok": dram("slot_tokens", [NSLOT, C]),
            "o": dram("slot_outputs", [NSLOT, C]),
            "slot": ctx.enter_context(nc.sbuf_tensor("slot_all", [P, BATCH * TT * K], I32)),
            "prob": ctx.enter_context(nc.sbuf_tensor("prob_all", [P, BATCH * TT * K], F32)),
        }
        attention_phase(nc, d, rt)
        expert_phase(nc, d, rt)


def kernel(**inputs):
    import numpy as _np
    import concourse.bacc as _bacc
    from concourse import mybir as _mybir
    from concourse.bass_utils import run_bass_kernel_spmd as _run

    def attn(name):
        return _np.asarray(inputs["L0_attn_" + name])

    def ffn(name):
        return _np.asarray(inputs["L0_ffn_" + name])

    arrays = {
        "x": attn("x").reshape(BATCH * T, C),
        "wqT": attn("Wq").T, "wkT": attn("Wk").T, "wvT": attn("Wv").T, "woT": attn("Wo").T,
        "bq": attn("bq"), "bk": attn("bk"), "bv": attn("bv"), "bo": attn("bo"),
        "wr": ffn("router_w"), "rb": ffn("router_b"),
        "wf": ffn("w_c_fc"), "wg": ffn("w_gate"), "wp": ffn("w_c_proj"),
        "bf": ffn("b_c_fc").reshape(E, HK, P).transpose(2, 0, 1),
        "bg": ffn("b_gate").reshape(E, HK, P).transpose(2, 0, 1),
        "bp": ffn("b_c_proj"),
        "consts": constants(),
        "rows": np.stack([np.zeros(NG * GH * T, np.float32), np.ones(NG * GH * T, np.float32)]),
    }
    arrays = {"in_" + k: _np.ascontiguousarray(v) for k, v in arrays.items()}
    nc = _bacc.Bacc("TRN2", target_bir_lowering=False, num_devices=1)
    d = {k[3:]: nc.dram_tensor(k, v.shape, _mybir.dt.from_np(v.dtype), kind="ExternalInput").ap()
         for k, v in arrays.items()}
    d["out"] = nc.dram_tensor("out_rows", [BATCH * T, C], F32, kind="ExternalOutput").ap()
    build(nc, d)
    r = _run(nc, [arrays], core_ids=[0])
    return r.results[0]["out_rows"].reshape(BATCH, T, C)
```

```python
import concourse.bass as bass
from concourse import mybir
from contextlib import ExitStack

import numpy as np

F32 = mybir.dt.float32
F32R = mybir.dt.float32r
BF16 = mybir.dt.bfloat16
I32 = mybir.dt.int32
ALU = mybir.AluOpType
ACT = mybir.ActivationFunctionType
AXX = mybir.AxisListType.X

P = 128
BATCH, T, C = 8, 512, 256
TT = T // P
CK = C // P
HEADS, DH = 16, 16
GH = 4
NG = HEADS // GH
NP = 4
ZROW = NP * DH
MROW = ZROW + 1
ROWS = MROW + 1
SLOTS = 8
FILLS = 12
E, K, HID = 8, 2, 1024
CAP = int(1.2 * K * T // E)
EROWS = BATCH * CAP
NSLOT = E * EROWS
HK = HID // P
EPS = 1e-5
MASKED = -1e30
RSQRT_MAGIC = float(0x5F3759DF)
THETA = 10000.0

FIRST_LOAD_AT = ((7, 3, 2), (8, 0, 6))
FIRST_SPLIT_AT = ((8, 0, 1), (8, 0, 3), (8, 1, 3))
LATE_FROM = (2, 2)

COS, SIN = 0, T
IDENT = 2 * T
CAUSAL = IDENT + P
LATER = CAUSAL + P
TRI = LATER + P
RANK = TRI + P
NCONST = RANK + E


def wait(eng, sem, n):
    if isinstance(n, int) and n <= 0:
        return
    eng.wait_ge(sem, n)


def wait_apart(eng, sem, n, passed):
    wait(eng, sem, n)
    if not isinstance(n, int):
        eng.sem_inc(passed, 1)


def there(b, first, last):
    return not isinstance(b, int) or first <= b <= last


def product3(nc, out, pairs):
    terms = [(w[0], x[0]) for w, x in pairs] + [(w[1], x[0]) for w, x in pairs] + [(w[0], x[1]) for w, x in pairs]
    for i, (w, x) in enumerate(terms):
        last = nc.tensor.matmul(out, w, x, start=(i == 0), stop=(i == len(terms) - 1))
    return last


class Region:
    def __init__(self, nc, place):
        self.nc, (self.at, self.end) = nc, place

    def skip(self, size):
        self.at += size

    def take(self, name, shape, dt=F32):
        offset = self.at
        self.at += int(np.prod(shape[1:])) * (2 if dt == BF16 else 4)
        assert self.at <= self.end
        return self.nc.alloc_sbuf_tensor_at(name, shape, dt, offset=offset, align_bytes=4)[:]


def set_apart(nc, ctx, name, size):
    place = nc.sbuf_base, nc.sbuf_base + size
    ctx.enter_context(nc.sbuf_tensor(name, [P, size // 4], F32))
    assert nc.sbuf_base == place[1]
    return place


def attention_phase(nc, d, rt, block, outer):
    ctx = ExitStack()
    with ctx:
        def sb(name, shape, dt=F32):
            return ctx.enter_context(nc.sbuf_tensor(name, shape, dt))

        def sem(name):
            rt[name] = outer.enter_context(nc.semaphore(name))
            return rt[name]

        early, late, kept = (Region(nc, rt[name]) for name in ("early", "late", "kept"))

        rope_table = early.take("rope_table", [P, 2 * T])
        cos, sin = rope_table[:, COS:COS + T], rope_table[:, SIN:SIN + T]
        consts = kept.take("consts_sb", [P, NCONST - 2 * T])
        ident = consts[:, IDENT - 2 * T:IDENT - 2 * T + P]
        rank = consts[:, RANK - 2 * T:RANK - 2 * T + E]
        rt["ident"] = ident
        ident_bf = sb("ident_bf", [P, P], BF16)
        causal_bf = sb("causal_bf", [P, P], BF16)
        later_bf = sb("later_bf", [P, P], BF16)
        tri_bf = kept.take("tri_bf", [P, P], BF16)
        ones_bf = kept.take("ones_bf", [P, P], BF16)
        zeros = early.take("zeros", [P, NSLOT * C // P // FILLS])
        wq = [early.take(f"wq_{part}", [P, CK, C], F32R) for part in ("hi", "lo")]
        wk = [early.take(f"wk_{part}", [P, CK, C], F32R) for part in ("hi", "lo")]
        wv = [early.take(f"wv_{part}", [P, CK, C], F32R) for part in ("hi", "lo")]
        wr = kept.take("wr", [P, CK, 32])
        bqk = sb("bqk", [P, 4])
        bv_all = sb("bv_all", [P, C])
        bo_all = kept.take("bo_all", [P, C])
        rb_all = kept.take("rb_all", [P, E])

        attn = late.take("attn", [P, TT, C])
        attnT = late.take("attnT", [P, CK, T])
        xr = late.take("xr", [P, TT, C])
        pv_sb = late.take("pv_sb", [P, T])
        wo = late.take("wo", [P, CK, C])
        hT = late.take("hT", [P, CK, T])
        x1 = late.take("x1", [P, TT, C])
        raw_q, raw_k = (late.take(f"raw_{side}", [P, CK, C]) for side in "qk")
        raw_v = Region(nc, (late.at, late.end)).take("raw_v", [P, CK, C])
        hn = late.take("hn", [P, TT, C])
        x_in = early.take("x_in", [P, TT, C])
        stats1 = sb("stats1", [P, TT, 6])
        mv1 = sb("mv1", [P, TT, 2])
        rs1 = sb("rs1", [P, 3, TT])
        xn = early.take("xn", [P, TT, C])
        xnT = [early.take(f"xnT_{part}", [P, CK, T], F32R) for part in ("hi", "lo")]
        qk_b = early.take("qk_b", [P, 2, T])
        rope_c = early.take("rope_c", [P, 2, T])
        rope_s = early.take("rope_s", [P, 2, T])
        hilo = early.take("hilo", [P, 4, 2, T], F32R)
        v_next = sb("v_next", [P, TT, C])
        v_sb = sb("v_sb", [P, TT, HEADS, 2 * DH])
        qst = sb("qst", [ROWS, NG, GH, T], F32R)
        kst = sb("kst", [ROWS, NG, GH, T], F32R)
        mx = sb("mx", [P, 2, TT, GH])
        negmax = sb("negmax", [GH, 2, T], F32R)
        probs = sb("probs", [P, 2, GH, T])
        rden = kept.take("rden", [P, TT, GH])
        stats2 = kept.take("stats2", [P, TT, 6])
        mv2 = kept.take("mv2", [P, TT, 2])
        rs2 = kept.take("rs2", [P, 3, TT])
        lgT = kept.take("lgT", [P, P])
        logits = kept.take("logits", [P, TT, E])
        top = kept.take("top", [P, 2, TT])
        picked = kept.take("picked", [P, 2, TT])
        eq = kept.take("eq", [P, TT, E])
        onehot = kept.take("onehot", [P, TT, K, E])
        onehot_bf = kept.take("onehot_bf", [P, TT, K, E], BF16)
        posm = kept.take("posm", [P, TT, K, E])
        pos = kept.take("pos", [P, TT, K])
        over = kept.take("over", [P, TT, K])
        slot_f = kept.take("slot_f", [P, TT, K])
        base = kept.take("base", [P, 1])
        put_at = kept.take("put_at", [P, TT * K], I32)
        dlt = kept.take("dlt", [P, TT])
        ex = kept.take("ex", [P, TT])

        ps = rt["ps"]
        S1 = 0
        S2 = 4
        pvb = ps[:, 6, :]
        misc = ps[:, 7, :]

        ld_const, ld_w = sem("ld_const"), sem("ld_w")
        ld_x, ld_xr, st_x1 = sem("ld_x"), sem("ld_xr"), sem("st_x1")
        st_hilo = [sem(f"st_hilo{c}") for c in range(CK)]
        ld_stack = [sem(f"ld_stack{g}") for g in range(NG)]
        ld_max = sem("ld_max")
        st_zero, st_tok = sem("st_zero"), sem("st_tok")
        made, z_ready = sem("made"), sem("z_ready")
        ld_ones, wr_set = sem("ld_ones"), sem("wr_set")
        p1_done, p2_done, pv_done = sem("p1_done"), sem("p2_done"), sem("pv_done")
        maxT_done, atT_done = sem("maxT_done"), sem("atT_done")
        xT_done, qk_done, v_done = sem("xT_done"), sem("qk_done"), sem("v_done")
        oT_done, o_done, hT_done = sem("oT_done"), sem("o_done"), sem("hT_done")
        lt_done, lg_done, pf_done = sem("lt_done"), sem("lg_done"), sem("pf_done")
        exp_done, negmax_out, pv_out = sem("exp_done"), sem("negmax_out"), sem("pv_out")
        xl_out, w_split = sem("xl_out"), sem("w_split")
        xT_out, qk_out, oT_out, hT_out = sem("xT_out"), sem("qk_out"), sem("oT_out"), sem("hT_out")
        lt_out, ex_done = sem("lt_out"), sem("ex_done")
        red_done, at_out, v_out, v_moved = sem("red_done"), sem("at_out"), sem("v_out"), sem("v_moved")
        o_out, lg_out, pf_out = sem("o_out"), sem("lg_out"), sem("pf_out")
        mv1_done, mv2_done, xn_done, h_done = sem("mv1_done"), sem("mv2_done"), sem("xn_done"), sem("h_done")
        sin_done, rope_done, oh_done, dlt_done, put_done = (sem("sin_done"), sem("rope_done"), sem("oh_done"),
                                                            sem("dlt_done"), sem("put_done"))
        rs1_done, rs2_done = sem("rs1_done"), sem("rs2_done")
        cos_done, hilo_done, xr_done = sem("cos_done"), sem("hilo_done"), sem("xr_done")
        dve_step, newton1, newton2 = sem("dve_step"), sem("newton1"), sem("newton2")
        hilo_half = sem("hilo_half")
        sp_passed, dve_passed, pool_passed = sem("sp_passed"), sem("dve_passed"), sem("pool_passed")

        PIECES = {
            (0, 0): ("M", 0), (0, 1): ("H", 0), (0, 2): ("H", 1), (0, 3): ("A", 0), (0, 4): ("L", 0), (0, 5): ("R", 0),
            (0, 6): ("X", 0), (0, 7): ("X", 1),
            (1, 0): ("M", 0), (1, 1): ("Q", 0), (1, 3): ("A", 0), (1, 4): ("Q", 1), (1, 5): ("F", 0),
            (1, 6): ("Q", 2),
            (2, 0): ("M", 0), (2, 1): ("Q", 3), (2, 3): ("A", 0), (2, 4): ("V", 0), (2, 5): ("T", 0),
            (2, 6): ("T", 1), (2, 7): ("V", 1),
            (3, 0): ("M", 0), (3, 1): ("O", 0), (3, 2): ("O", 1), (3, 3): ("A", 0),
        }
        Q_AT = ((1, 1), (1, 4), (1, 6), (2, 1))
        FIRST = [at for at in sorted(PIECES) if PIECES[at][0] in "XQV"]

        def bank_of(b, g, u):
            return ps[:, FIRST.index((g, u)), :] if isinstance(b, int) and b == -1 else misc

        def piece_there(b, g, kind):
            s = 4 * b + g
            return {
                "M": there(s, 1, 32) if isinstance(b, int) else True,
                "A": there(s, 3, 34) if isinstance(b, int) else True,
                "X": there(b, -1, 6), "Q": there(b, -1, 6), "V": there(b, -1, 6),
                "T": there(b, 1, 8), "O": there(b, 1, 8),
                "H": there(b, 2, 9), "L": there(b, 2, 9), "R": there(b, 2, 9), "F": there(b, 2, 9),
            }[kind]

        def freed(b, g, kind, n):
            return {
                "M": (negmax_out, 4 * b + g),
                "A": (at_out, 4 * b + g - 2),
                "X": (xl_out, 2 * b + 2 + n + 1),
                "Q": (qk_out, 4 * b + 4 + n + 1),
                "V": (v_out, 2 * b + 2 + n + 1),
                "T": (oT_out, 2 * b - 2 + n + 1),
                "O": (o_out, 2 * b - 2 + n + 1),
                "H": (hT_out, 2 * (b - 2) + n + 1),
                "L": (lt_out, b - 2 + 1),
                "R": (lg_out, b - 2 + 1),
                "F": (pf_out, b - 2 + 1),
            }[kind]

        def last_piece(b, g, u):
            if isinstance(b, int) and b == -1:
                return None
            keys = sorted(PIECES)
            at = keys.index((g, u))
            for back in range(1, 2 * len(keys)):
                k = at - back
                bb = b if k >= 0 else b - 1
                gg, uu = keys[k % len(keys)]
                kind, n = PIECES[gg, uu]
                if (not isinstance(bb, int) or bb >= -1) and piece_there(bb, gg, kind):
                    if isinstance(bb, int) and bb == -1 and kind not in "XQV":
                        continue
                    return freed(bb, gg, kind, n)
            return None

        def before_late(b):
            return [(g, u) for g in range(NG) for u in range(SLOTS)
                    if not (isinstance(b, int) and b == BATCH) or (g, u) < LATE_FROM]

        @block.sync
        def _(sp):
            def load_x(b):
                wait(sp, xn_done, b)
                sp.dma_start(x_in[:], d["x"][bass.ts(b, T), :].rearrange("(t p) c -> p t c", p=P)).then_inc(ld_x, 16)

            def store_hilo(b, n):
                wait(sp, hilo_done, 4 * b + n + 1)
                dst = rt["qk"][b, n % 2, :, bass.ts(n // 2, P), :]
                sp.dma_start(dst.rearrange("h p t -> p h t"), hilo[:, n].bitcast(F32)).then_inc(st_hilo[n // 2], 16)

            def load_stack(b, g):
                wait_apart(sp, st_hilo[g // 2], 32 * (b + 1), sp_passed)
                wait_apart(sp, p2_done, 16 * (4 * b + g - 3), sp_passed)
                group = bass.ts(g, GH * DH)
                for i in range(2):
                    q = rt["qk"][b, 0, :, group, :].rearrange("c (d h) t -> d c (h t)", h=GH)
                    k = rt["qk"][b, 1, i, group, :].rearrange("(d c h) t -> d c (h t)", h=GH, c=1)\
                        .to_broadcast([DH, 2, GH * T])
                    for stack, src in ((qst, q), (kst, k)):
                        rows = stack[2 * DH * i:2 * DH * (i + 1), g].rearrange("r h t -> r (h t)").bitcast(F32)
                        sp.dma_start(rows, src).then_inc(ld_stack[g], 16)

            def send_max(b, g):
                s = 4 * b + g
                wait(sp, negmax_out, s)
                wait(sp, p2_done, 16 * (s - 4))
                sp.dma_start(qst[MROW:MROW + 1, (g - 1) % 4].bitcast(F32), negmax[:, (g - 1) % 2, :].bitcast(F32))\
                    .then_inc(ld_max, 16)

            def body_slot(b, g, u):
                if isinstance(b, int) and (b, g, u) in FIRST_LOAD_AT:
                    rt["load_first_weights"](sp, FIRST_LOAD_AT.index((b, g, u)))
                if u == 0 and g == 0 and there(b, 1, 6):
                    load_x(b + 1)
                if u == 0 and g < 3 and there(b, 1, 7):
                    load_stack(b, g + 1)
                if u == 0 and g == 3 and there(b, 0, 6):
                    load_stack(b + 1, 0)
                if u == 1 and piece_there(b, g, "M"):
                    send_max(b, g)
                if (g, u) == (1, 4) and there(b, 1, 8):
                    wait(sp, o_out, 2 * (b - 1))
                    sp.dma_start(xr[:], d["x"][bass.ts(b - 1, T), :].rearrange("(t p) c -> p t c", p=P))\
                        .then_inc(ld_xr, 16)
                if (g, u) in ((1, 7), (2, 2), (2, 4), (3, 1)) and there(b, 0, 6):
                    store_hilo(b + 1, ((1, 7), (2, 2), (2, 4), (3, 1)).index((g, u)))
                if (g, u) == (3, 4) and there(b, 1, 8):
                    wait(sp, o_out, 2 * b)
                    sp.dma_start(rt["x1"][bass.ts(b - 1, T), :].rearrange("(t p) c -> p t c", p=P), x1[:])\
                        .then_inc(st_x1, 16)

            def body(b):
                for g, u in before_late(b):
                    body_slot(b, g, u)

            load_x(0)
            sp.dma_start(consts[:], d["consts"][:, 2 * T:]).then_inc(ld_const, 16)
            sp.dma_start(rope_table, d["consts"][:, 0:2 * T]).then_inc(ld_w, 16)
            for w_sb, name in ((raw_q, "wqT"), (raw_k, "wkT"), (raw_v, "wvT"), (wo, "woT")):
                sp.dma_start(w_sb[:], d[name].rearrange("(k p) n -> p k n", p=P)).then_inc(ld_w, 16)
            load_x(1)
            for n in range(4):
                store_hilo(0, n)
                if n == 1:
                    load_stack(0, 0)
            for g in range(1, NG):
                load_stack(0, g)
            body(0)
            body(1)
            with sp.Fori(2, 7) as b:
                body(b)
            body(7)
            body(8)
            rt["late_slot"]["sp"] = body_slot

        @block.tensor
        def _(pe):
            mm = nc.tensor.matmul

            def pass1(b, g, u):
                s = 4 * b + g
                i, pr = u // 2, u % 2
                if u == 0:
                    wait(pe, ld_stack[g], 64 * (b + 1))
                wait(pe, red_done, 8 * s + u - 1)
                width = max(2 * P, P * (i + 1))
                for hh in range(2):
                    h, bank = 2 * pr + hh, ps[:, S1 + 2 * (u % 2) + hh, :]
                    mm(bank[:, 0:width], qst[0:MROW, g, h, bass.ts(i, P)], kst[0:MROW, g, h, 0:width],
                       start=True, stop=False)
                    last = mm(bank[:, bass.ts(i, P)], ident_bf[:], causal_bf[:], start=False, stop=True)
                last.then_inc(p1_done, 1)

            def pass2(t, g, u):
                j, pr = u // 2, u % 2
                if u == 0:
                    wait(pe, ld_max, 16 * (t + 1))
                q0 = min(P * j, T - 2 * P)
                for hh in range(2):
                    h, n = 2 * pr + hh, 2 * u + hh
                    wait(pe, exp_done, 16 * t + n - 1)
                    mm(ps[:, S2 + hh, 0:T - q0], kst[0:ROWS, g, h, bass.ts(j, P)], qst[0:ROWS, g, h, q0:T],
                       start=True, stop=False)
                    mm(ps[:, S2 + hh, P * j - q0:P * (j + 1) - q0], ident_bf[:], later_bf[:], start=False, stop=True)\
                        .then_inc(p2_done, 1)

            def pv(t, bt, g, j):
                wait(pe, exp_done, 16 * t + 4 * j + 4)
                if j == 0:
                    wait(pe, pv_out, t)
                    if g == 0:
                        wait(pe, v_moved, bt + 1)
                for h in range(GH):
                    last = mm(pvb[32 * h:32 * h + 32, P * j:T], v_sb[:, j, GH * g + h, :], probs[:, j % 2, h, P * j:T],
                              start=(j == 0), stop=(j == TT - 1))
                last.then_inc(pv_done, 1)

            def turn(dst, src_of, n):
                for k in range(n):
                    last = nc.tensor.transpose(dst[:, bass.ts(k, P)], src_of(k), ident)
                return last

            def piece(b, g, u):
                kind, n = PIECES[g, u]
                if not piece_there(b, g, kind):
                    return
                s, misc = 4 * b + g, bank_of(b, g, u)
                free = last_piece(b, g, u)
                if free:
                    wait(pe, *free)
                if kind == "M":
                    wait(pe, red_done, 8 * s)
                    for i in range(TT):
                        last = nc.tensor.transpose(misc[0:GH, bass.ts(i, P)], mx[:, (g - 1) % 2, i, :], ident)
                    last.then_inc(maxT_done, 1)
                elif kind == "A":
                    wait(pe, pv_out, s - 2)
                    turn(misc, lambda k: pv_sb[:, bass.ts(k, P)], TT).then_inc(atT_done, 1)
                elif kind == "X":
                    wait(pe, xn_done, b + 2)
                    turn(misc, lambda k: xn[:, k, bass.ts(n, P)], TT).then_inc(xT_done, 1)
                elif kind == "Q":
                    wait(pe, xl_out, 2 * (b + 2))
                    product3(nc, misc, [([w[:, c, bass.ts(n // 2, P)] for w in (wq, wk)[n % 2]], [x[:, c, :] for x in xnT])
                                   for c in range(CK)]).then_inc(qk_done, 1)
                elif kind == "V":
                    for k in range(2):
                        last = product3(nc, misc[:, bass.ts(k, C)],
                                       [([x[:, c, bass.ts(2 * n + k, P)] for x in xnT], [w[:, c, :] for w in wv])
                                        for c in range(CK)])
                    last.then_inc(v_done, 1)
                elif kind == "T":
                    wait(pe, at_out, 4 * b)
                    turn(misc, lambda k: attn[:, k, bass.ts(n, P)], TT).then_inc(oT_done, 1)
                elif kind == "O":
                    wait(pe, oT_out, 2 * b)
                    for k in range(2):
                        for c in range(CK):
                            last = mm(misc[:, bass.ts(k, C)], attnT[:, c, bass.ts(2 * n + k, P)], wo[:, c, :],
                                      start=(c == 0), stop=(c == CK - 1))
                    last.then_inc(o_done, 1)
                elif kind == "H":
                    wait(pe, h_done, b - 1)
                    turn(misc, lambda k: hn[:, k, bass.ts(n, P)], TT).then_inc(hT_done, 1)
                elif kind == "L":
                    wait(pe, hT_out, 2 * (b - 1))
                    for c in range(CK):
                        for k in range(TT):
                            last = mm(misc[32 * k:32 * k + 32, 0:P], wr[:, c, :], hT[:, c, bass.ts(k, P)],
                                      start=(c == 0), stop=(c == CK - 1))
                    last.then_inc(lt_done, 1)
                elif kind == "R":
                    wait(pe, lt_out, b - 1)
                    turn(misc, lambda k: lgT[:], 1).then_inc(lg_done, 1)
                elif kind == "F":
                    wait(pe, oh_done, b - 1)
                    out = misc[:, 0:TT * K * E].rearrange("p (t k e) -> p t k e", t=TT, k=K)
                    flat = misc[:, 0:TT * K * E]
                    mm(flat, tri_bf[:], onehot_bf[:].rearrange("p t k e -> p (t k e)"), start=True, stop=False)
                    for j in range(TT - 1):
                        mm(out[:, j + 1:TT].rearrange("p t k e -> p t (k e)"), ones_bf[:],
                           onehot_bf[:, j].rearrange("p k e -> p (k e)")
                           .rearrange("p (a n) -> p a n", a=1).to_broadcast([P, TT - 1 - j, K * E]),
                           start=False, stop=False)
                    for j in range(TT):
                        last = mm(out[:, :, 1, :], ones_bf[:],
                                  onehot_bf[:, j, 0:1, :].to_broadcast([P, TT, E]), start=False, stop=(j == TT - 1))
                    last.then_inc(pf_done, 1)

            def body(b):
                for g in range(4):
                    s = 4 * b + g
                    for u in range(SLOTS):
                        if (g, u) not in before_late(b):
                            continue
                        if there(b, 0, 7):
                            pass1(b, g, u)
                        if not isinstance(b, int) or 0 <= s - 2 <= 31:
                            pass2(s - 2, (g - 2) % 4, u)
                        if u in (3, 5, 7) and (not isinstance(b, int) or 0 <= s - 2 <= 31):
                            pv(s - 2, b - (g < 2), (g - 2) % 4, (u - 3) // 2)
                        if u == 1 and (not isinstance(b, int) or 0 <= s - 3 <= 31):
                            pv(s - 3, b - (g < 3), (g - 3) % 4, 3)
                        if (g, u) in PIECES:
                            piece(b, g, u)

            pe.wait_ge(ld_const, 16)
            pe.wait_ge(ld_w, 16 * 13)
            for g, u in FIRST:
                if PIECES[g, u] == ("Q", 0):
                    pe.wait_ge(w_split, 3)
                piece(-1, g, u)
            pe.wait_ge(made, 5)
            pe.wait_ge(ld_ones, 32)
            body(0)
            body(1)
            with pe.Fori(2, 7) as b:
                body(b)
            body(7)
            body(8)
            rt["late_slot"]["pe"] = piece

        @block.scalar
        def _(act):
            A = nc.scalar.activation

            def exps(t, u):
                j, pr = u // 2, u % 2
                q0 = min(P * j, T - 2 * P)
                for hh in range(2):
                    wait(act, p2_done, 16 * t + 2 * u + hh + 1)
                    if pr == 0 and hh == 0:
                        wait(act, pv_done, 4 * t + j - 1)
                    A(probs[:, j % 2, 2 * pr + hh, P * j:T], ps[:, S2 + hh, P * j - q0:T - q0], ACT.Exp,
                      scale=float(DH) ** -0.5).then_inc(exp_done, 1)

            def max_out(b, g):
                s = 4 * b + g
                wait(act, maxT_done, s)
                wait(act, p2_done, 16 * (s - 3) + 1)
                A(negmax[:, (g - 1) % 2, :], misc[0:GH, :], ACT.Copy, scale=-1.0).then_inc(negmax_out, 1)

            def body_slot(b, g, u):
                s = 4 * b + g
                if u == 1 and piece_there(b, g, "M"):
                    max_out(b, g)
                if u == 2 and (not isinstance(b, int) or 0 <= s - 3 <= 31):
                    wait(act, pv_done, 4 * (s - 2))
                    wait(act, atT_done, s - 3)
                    A(pv_sb[:], pvb, ACT.Copy).then_inc(pv_out, 1)
                if (g, u) in ((0, 7), (1, 0)) and piece_there(b, g, "X"):
                    n = g
                    wait(act, xT_done, 2 * b + 2 + n + 1)
                    wait(act, v_done, 2 * (b + 1))
                    A(xnT[0][:, n, :], bank_of(b, 0, 6 + n), ACT.Copy).then_inc(xT_out, 1)
                if (g, u - 1) in Q_AT and piece_there(b, g, "Q"):
                    n = Q_AT.index((g, u - 1))
                    wait(act, qk_done, 4 * b + 4 + n + 1)
                    wait(act, cos_done, 4 * b + 4 + n - 1)
                    wait(act, sin_done, 4 * b + 4 + n - 1)
                    part = 2 * (n % 2) + n // 2
                    A(qk_b[:, n % 2, :], bank_of(b, g, u - 1), ACT.Identity, bias=bqk[:, part:part + 1])\
                        .then_inc(qk_out, 1)
                if (g, u) in ((2, 6), (2, 7)) and piece_there(b, g, "T"):
                    n = u - 6
                    wait(act, oT_done, 2 * b - 2 + n + 1)
                    wait(act, o_done, 2 * (b - 1))
                    A(attnT[:, n, :], misc, ACT.Copy).then_inc(oT_out, 1)
                if (g, u) in ((0, 2), (0, 3)) and there(b, 2, 9):
                    n = u - 2
                    wait(act, hT_done, 2 * (b - 2) + n + 1)
                    A(hT[:, n, :], misc, ACT.Copy).then_inc(hT_out, 1)
                if (g, u) == (0, 5) and there(b, 2, 9):
                    wait(act, lt_done, b - 1)
                    A(lgT[:], misc[:, 0:P], ACT.Copy).then_inc(lt_out, 1)
                if (g, u) == (1, 4) and there(b, 2, 9):
                    wait(act, dlt_done, b - 1)
                    A(ex[:], dlt[:], ACT.Exp).then_inc(ex_done, 1)
                if not isinstance(b, int) or 0 <= s - 2 <= 31:
                    exps(s - 2, u)

            def body(b):
                for g, u in before_late(b):
                    body_slot(b, g, u)

            for n in range(CK):
                act.dma_start(bqk[:, n:n + 1], d["bq"][bass.ts(n, P)].rearrange("(p a) -> p a", a=1)).then_inc(ld_w, 16)
                act.dma_start(bqk[:, 2 + n:3 + n], d["bk"][bass.ts(n, P)].rearrange("(p a) -> p a", a=1))\
                    .then_inc(ld_w, 16)
            for all_rows, name in ((bv_all, "bv"), (bo_all, "bo"), (rb_all, "rb")):
                act.dma_start(all_rows[:], d[name].rearrange("(a n) -> a n", a=1).to_broadcast([P, all_rows.shape[1]]))\
                    .then_inc(ld_w, 16)
            act.wait_ge(wr_set, 1)
            act.dma_start(wr[:, :, 0:E], d["wr"].rearrange("(k p) n -> p k n", p=P)).then_inc(ld_w, 16)
            A(lgT[:, 0:1], wr[:, 0, E:E + 1], ACT.Exp)
            act.wait_ge(ld_w, 16 * 13)
            for g, u in ((0, 7), (1, 0), *((g, u + 1) for g, u in Q_AT)):
                body_slot(-1, g, u)
            body(0)
            body(1)
            with act.Fori(2, 7) as b:
                body(b)
            body(7)
            body(8)
            rt["late_slot"]["act"] = body_slot

        @block.vector
        def _(dve):
            V = nc.vector
            count = [0]

            def settle(steps_per_body, b, k, ins):
                ins.then_inc(dve_step, 1)
                dve.wait_ge(dve_step, (count[0] + k) if isinstance(b, int) else (count[0] + (b - 2) * steps_per_body + k))

            class Chain:
                def __init__(self, b):
                    self.b, self.k = b, 0

                def __call__(self, ins):
                    self.k += 1
                    settle(DVE_STEPS, self.b, self.k, ins)

            def layer_stats(chain, src, stats, mv, done):
                for k in range(TT):
                    ins = V.bn_stats(stats[:, k, :], src[:, k, :])
                chain(ins)
                if not isinstance(chain.b, int):
                    dve.sem_inc(dve_passed, 1)
                for k in range(TT):
                    ins = V.bn_aggr(mv[:, k, :], stats[:, k, :])
                ins.then_inc(done, 1)

            def normalise(dst, src, mv, rs, done):
                for k in range(TT):
                    ins = V.tensor_scalar(dst[:, k, :], src[:, k, :], mv[:, k, 0:1], rs[:, 1, k:k + 1],
                                          ALU.subtract, ALU.mult)
                ins.then_inc(done, 1)

            def choose(chain, b, k, src):
                chain(V.reduce_max(top[:, k, :], src, AXX))
                chain(V.tensor_tensor(eq[:], src, top[:, k, :].unsqueeze(2).to_broadcast([P, TT, E]), ALU.is_equal))
                chain(V.tensor_tensor(eq[:], eq[:], rank.unsqueeze(1).to_broadcast([P, TT, E]), ALU.mult))
                chain(V.reduce_max(picked[:, k, :], eq[:], AXX))
                chain(V.tensor_tensor(onehot[:, :, k, :], rank.unsqueeze(1).to_broadcast([P, TT, E]),
                                      picked[:, k, :].unsqueeze(2).to_broadcast([P, TT, E]), ALU.is_equal))

            def route(chain, b, part):
                if part == 0:
                    wait(dve, lg_done, b - 1)
                    V.tensor_tensor(logits[:], misc[:, 0:P].rearrange("p (t r) -> p t r", t=TT)[:, :, 0:E],
                                    rb_all[:].unsqueeze(1).to_broadcast([P, TT, E]), ALU.add).then_inc(lg_out, 1)
                    return
                if part == 1:
                    dve.wait_ge(lg_out, b - 1)
                    choose(chain, b, 0, logits[:])
                    return
                chain(V.scalar_tensor_tensor(logits[:], onehot[:, :, 0, :], -3e38, logits[:], ALU.mult, ALU.add))
                choose(chain, b, 1, logits[:])
                V.tensor_copy(onehot_bf[:], onehot[:]).then_inc(oh_done, 1)
                V.tensor_tensor(dlt[:], top[:, 1, :], top[:, 0, :], ALU.subtract).then_inc(dlt_done, 1)

            def probabilities(chain, b):
                wait(dve, ex_done, b - 1)
                pr = rt["prob"][:, bass.ts(b - 2, TT * K)].rearrange("p (t k) -> p t k", k=K)
                chain(V.tensor_scalar(dlt[:], ex[:], 1.0, None, ALU.add))
                chain(V.reciprocal(dlt[:], dlt[:]))
                chain(V.tensor_copy(pr[:, :, 0], dlt[:]))
                chain(V.tensor_tensor(pr[:, :, 1], ex[:], dlt[:], ALU.mult))

            def slots(chain, b, part):
                if part == 0:
                    wait(dve, pf_done, b - 1)
                    V.tensor_tensor(posm[:], misc[:, 0:TT * K * E].rearrange("p (t k e) -> p t k e", t=TT, k=K),
                                    onehot[:], ALU.mult).then_inc(pf_out, 1)
                    return
                dve.wait_ge(pf_out, b - 1)
                chain(V.reduce_sum(pos[:], posm[:], AXX))
                chain(V.tensor_scalar(over[:], pos[:], float(CAP - 1), float(NSLOT), ALU.is_gt, ALU.mult))
                chain(V.tensor_scalar(pos[:], pos[:], float(CAP - 1), base[:, 0:1], ALU.min, ALU.add))
                chain(V.scalar_tensor_tensor(slot_f[:], picked[:].rearrange("p k t -> p t k"), -float(EROWS),
                                             pos[:], ALU.mult, ALU.add))
                chain(V.tensor_copy(rt["slot"][:, bass.ts(b - 2, TT * K)], slot_f[:].rearrange("p t k -> p (t k)")))
                V.tensor_tensor(put_at[:].rearrange("p (t k) -> p t k", k=K), slot_f[:], over[:], ALU.add)\
                    .then_inc(put_done, 1)
                chain(V.tensor_scalar(base[:], base[:], float(CAP), None, ALU.add))

            def body_slot(chain, b, g, u):
                s = 4 * b + g
                if u == 4 and piece_there(b, g, "A"):
                    at = misc.rearrange("p (t h r) -> p t h r", t=TT, h=GH)
                    wait(dve, atT_done, s - 2)
                    chain(V.reciprocal(rden[:], at[:, :, :, DH]))
                    g3 = (g - 3) % 4
                    if g == 3:
                        wait(dve, oT_done, 2 * b)
                    V.tensor_tensor(attn[:, :, g3 * GH * DH:(g3 + 1) * GH * DH].rearrange("p t (h r) -> p t h r", h=GH),
                                    at[:, :, :, 0:DH], rden[:].unsqueeze(3).to_broadcast([P, TT, GH, DH]),
                                    ALU.mult).then_inc(at_out, 1)
                if (g, u) in ((0, 7), (1, 0)) and there(b, -1, 6):
                    n = g
                    wait(dve, xT_out, 2 * b + 2 + n + 1)
                    wait(dve, v_done, 2 * (b + 1))
                    V.tensor_tensor(xnT[1][:, n, :], bank_of(b, 0, 6 + n), xnT[0][:, n, :].bitcast(F32), ALU.subtract)\
                        .then_inc(xl_out, 1)
                if (g, u) in ((2, 5), (3, 0)) and there(b, -1, 6):
                    n = g - 2
                    wait(dve, v_done, 2 * b + 2 + n + 1)
                    wait(dve, v_moved, b + 1)
                    V.tensor_tensor(v_next[:, 2 * n:2 * n + 2, :], bank_of(b, 2, 4 + 3 * n).rearrange("p (k c) -> p k c", k=2),
                                    bv_all[:].unsqueeze(1).to_broadcast([P, 2, C]), ALU.add).then_inc(v_out, 1)
                if (g, u) in ((3, 2), (3, 3)) and piece_there(b, g, "O"):
                    n = u - 2
                    wait(dve, o_done, 2 * b - 2 + n + 1)
                    wait(dve, xr_done, b)
                    wait(dve, st_x1, 16 * (b - 1))
                    V.tensor_tensor(x1[:, 2 * n:2 * n + 2, :], misc.rearrange("p (k c) -> p k c", k=2),
                                    xr[:, 2 * n:2 * n + 2, :], ALU.add).then_inc(o_out, 1)
                if (g, u) == (1, 6) and there(b, 2, 9):
                    slots(chain, b, 0)
                if (g, u) in ((0, 6), (1, 1), (1, 2)) and there(b, 2, 9):
                    route(chain, b, ((0, 6), (1, 1), (1, 2)).index((g, u)))
                if there(b, 0, 7):
                    wait(dve, p1_done, 8 * s + u + 1)
                    if u == 0:
                        wait(dve, maxT_done, s - 1)
                    i, pr = u // 2, u % 2
                    V.reduce_max(mx[:, g % 2, i, 2 * pr:2 * pr + 2],
                                 ps[:, S1 + 2 * (u % 2):S1 + 2 * (u % 2) + 2, 0:P * (i + 1)], AXX)\
                        .then_inc(red_done, 1)
                if (g, u) == (0, 0) and there(b, -1, 6):
                    wait(dve, ld_x, 16 * (b + 2))
                    layer_stats(chain, x_in, stats1, mv1, mv1_done)
                if (g, u) == (0, 5) and there(b, -1, 6):
                    wait(dve, rs1_done, b + 2)
                    wait(dve, xT_done, 2 * (b + 1))
                    normalise(xn, x_in, mv1, rs1, xn_done)
                if (g, u) == (2, 6) and there(b, 2, 9):
                    probabilities(chain, b)
                if (g, u) == (2, 1) and there(b, 2, 9):
                    slots(chain, b, 1)
                if (g, u) in ((1, 3), (1, 6), (2, 0), (2, 5)) and there(b, -1, 6):
                    n = ((1, 3), (1, 6), (2, 0), (2, 5)).index((g, u))
                    wait_apart(dve, qk_out, 4 * b + 4 + n + 1, dve_passed)
                    wait_apart(dve, hilo_done, 4 * b + 4 + n - 1, dve_passed)
                    chain(V.stream_shuffle(rope_s[:, n % 2, :], qk_b[:, n % 2, :], [i ^ GH for i in range(32)]))
                    V.tensor_tensor(rope_s[:, n % 2, :], rope_s[:, n % 2, :], sin, ALU.mult).then_inc(sin_done, 1)
                if (g, u) in ((1, 4), (1, 7), (2, 1), (2, 7)) and there(b, -1, 6):
                    n = ((1, 4), (1, 7), (2, 1), (2, 7)).index((g, u))
                    wait(dve, sin_done, 4 * b + 4 + n + 1)
                    wait(dve, cos_done, 4 * b + 4 + n + 1)
                    V.tensor_tensor(rope_s[:, n % 2, :], rope_c[:, n % 2, :], rope_s[:, n % 2, :], ALU.add)\
                        .then_inc(rope_done, 1)
                if (g, u) == (2, 2) and there(b, 0, 7):
                    wait(dve, v_out, 2 * (b + 1))
                    wait(dve, pv_done, 16 * b)
                    V.tensor_copy(v_sb[:, :, :, 0:DH],
                                  v_next[:].rearrange("p t (h r) -> p t h r", h=HEADS)).then_inc(v_moved, 1)
                if (g, u) == (3, 3) and piece_there(b, g, "O"):
                    wait(dve, o_out, 2 * b)
                    layer_stats(chain, x1, stats2, mv2, mv2_done)
                if (g, u) == (3, 7) and piece_there(b, g, "O"):
                    wait(dve, rs2_done, b)
                    wait(dve, st_tok, 16 * 8 * (b - 1))
                    wait(dve, hT_done, 2 * (b - 1))
                    normalise(hn, x1, mv2, rs2, h_done)

            def body(b):
                chain = Chain(b)
                for g, u in before_late(b):
                    body_slot(chain, b, g, u)
                    if isinstance(b, int) and (b, g, u) in FIRST_SPLIT_AT:
                        rt["split_first_hi"](dve, FIRST_SPLIT_AT.index((b, g, u)))
                return chain if not there(b, -1, 7) else chain.k

            DVE_STEPS = 4 + 1 + 1 + 11 + 4 + 6 + 4

            chain = Chain(0)
            V.memset(wr[:], 0.0).then_inc(wr_set, 1)
            body_slot(chain, -1, 0, 0)
            chain(V.memset(v_sb[:], 1.0))
            V.memset(ones_bf[:], 1.0).then_inc(made, 1)
            chain(V.memset(base[:], float(E * EROWS)))
            dve.wait_ge(ld_const, 16)
            body_slot(chain, -1, 0, 5)
            dve.wait_ge(ld_w, 16 * 13)
            V.tensor_copy(ident_bf[:], ident).then_inc(made, 1)
            V.tensor_copy(causal_bf[:], consts[:, CAUSAL - 2 * T:CAUSAL - 2 * T + P]).then_inc(made, 1)
            V.tensor_copy(later_bf[:], consts[:, LATER - 2 * T:LATER - 2 * T + P]).then_inc(made, 1)
            V.tensor_copy(tri_bf[:], consts[:, TRI - 2 * T:TRI - 2 * T + P]).then_inc(made, 1)
            for raw_w, w in ((raw_q, wq), (raw_k, wk), (raw_v, wv)):
                chain(V.tensor_copy(w[0], raw_w))
                V.tensor_tensor(w[1], raw_w, w[0].bitcast(F32), ALU.subtract).then_inc(w_split, 1)
            for g, u in ((0, 7), (1, 0), (1, 3), (1, 4), (1, 6), (1, 7), (2, 0), (2, 1), (2, 5), (2, 7), (3, 0)):
                body_slot(chain, -1, g, u)
            count[0] += chain.k
            count[0] += body(0)
            count[0] += body(1)
            with dve.Fori(2, 7) as b:
                n = body(b)
                assert n == DVE_STEPS, n
            count[0] += 5 * DVE_STEPS
            count[0] += body(7)
            last_chain = body(8)
            rt["late_slot"]["dve"] = lambda b, g, u: body_slot(last_chain, b, g, u)

        @block.gpsimd
        def _(pool):
            G = nc.gpsimd

            def rsqrt(before, mv, rs, done, newton_step):
                k = [0]

                def step(ins):
                    k[0] += 1
                    ins.then_inc(newton_step, 1)
                    wait_apart(pool, newton_step, NEWTON * before + k[0], pool_passed)

                v, y, a = rs[:, 0, :], rs[:, 1, :], rs[:, 2, :]
                step(G.tensor_scalar(v, mv[:, :, 1], EPS, None, ALU.add))
                step(G.tensor_scalar(y.bitcast(I32), v.bitcast(I32), -0.5, RSQRT_MAGIC, ALU.mult, ALU.add))
                for it in range(3):
                    step(G.tensor_tensor(a, y, y, ALU.mult))
                    step(G.tensor_tensor(a, a, v, ALU.mult))
                    step(G.tensor_scalar(a, a, -0.5, 1.5, ALU.mult, ALU.add))
                    if it < 2:
                        step(G.tensor_tensor(y, y, a, ALU.mult))
                G.tensor_tensor(y, y, a, ALU.mult).then_inc(done, 1)

            SCATTER_AT = ((2, 1), (2, 3), (2, 4), (2, 6))
            NEWTON = 13

            def body_slot(b, g, u):
                s = 4 * b + g
                if (g, u) == (0, 1) and there(b, -1, 6):
                    wait(pool, mv1_done, b + 2)
                    wait_apart(pool, xn_done, b + 1, pool_passed)
                    rsqrt(b + 1, mv1, rs1, rs1_done, newton1)
                if (g, u) == (3, 4) and there(b, 1, 8):
                    wait(pool, mv2_done, b)
                    wait_apart(pool, h_done, b - 1, pool_passed)
                    rsqrt(b - 1, mv2, rs2, rs2_done, newton2)
                if (g, u - 1) in Q_AT and there(b, -1, 6):
                    n = Q_AT.index((g, u - 1))
                    wait(pool, qk_out, 4 * b + 4 + n + 1)
                    wait(pool, rope_done, 4 * b + 4 + n - 1)
                    G.tensor_tensor(rope_c[:, n % 2, :], qk_b[:, n % 2, :], cos, ALU.mult).then_inc(cos_done, 1)
                if (g, u) in ((1, 5), (2, 0), (2, 2), (2, 7)) and there(b, -1, 6):
                    n = ((1, 5), (2, 0), (2, 2), (2, 7)).index((g, u))
                    wait(pool, rope_done, 4 * b + 4 + n + 1)
                    wait_apart(pool, st_hilo[n // 2], 32 * (b + 1), pool_passed)
                    G.tensor_scalar(hilo[:, n, 0, :], rope_s[:, n % 2, :], 1.0, 0.0, ALU.mult, ALU.add)\
                        .then_inc(hilo_half, 1)
                    pool.wait_ge(hilo_half, 4 * b + 4 + n + 1)
                    G.tensor_tensor(hilo[:, n, 1, :], rope_s[:, n % 2, :], hilo[:, n, 0, :].bitcast(F32),
                                    ALU.subtract).then_inc(hilo_done, 1)
                if (g, u) == (2, 1) and there(b, 1, 8):
                    wait(pool, ld_xr, 16 * b)
                    G.tensor_tensor(xr[:], xr[:], bo_all[:].unsqueeze(1).to_broadcast([P, TT, C]), ALU.add)\
                        .then_inc(xr_done, 1)
                if (g, u) in SCATTER_AT and there(b, 2, 9):
                    for n in range(2):
                        scatter(b, 2 * SCATTER_AT.index((g, u)) + n)

            def scatter(b, n):
                if n == 0:
                    wait_apart(pool, put_done, b - 1, pool_passed)
                G.indirect_dma_start(out=rt["tok"], out_offset=bass.IndirectOffsetOnAxis(ap=put_at[:, n:n + 1], axis=0),
                                     in_=hn[:, n // K, :], in_offset=None, bounds_check=NSLOT - 1, oob_is_err=False)\
                    .then_inc(st_tok, 16)

            def fill(n):
                flat = rt["tok"].rearrange("n c -> (n c)").rearrange("(p x) -> p x", p=P)
                pool.wait_ge(z_ready, 1)
                pool.dma_start(flat[:, bass.ts(n, zeros.shape[1])], zeros[:]).then_inc(st_zero, 16)

            def body(b):
                for n, (g, u) in enumerate(before_late(b)):
                    body_slot(b, g, u)
                    if isinstance(b, int) and b < 2 and n % 5 == 3 and n < 30:
                        fill(6 * b + n // 5)
                    if isinstance(b, int) and (b, g, u) in FIRST_SPLIT_AT:
                        rt["split_first_lo"](pool, FIRST_SPLIT_AT.index((b, g, u)))

            pool.dma_start(kst[ZROW:ROWS].rearrange("r g h t -> r (g h t)"),
                          d["rows"][1:2].bitcast(F32R).to_broadcast([2, NG * GH * T])).then_inc(ld_ones, 16)
            pool.dma_start(qst[ZROW:MROW].rearrange("r g h t -> r (g h t)"), d["rows"][0:1].bitcast(F32R))\
                .then_inc(ld_ones, 16)
            G.memset(zeros[:], 0.0).then_inc(z_ready, 1)
            for g, u in ((0, 1), (1, 2), (1, 5), (1, 7), (2, 0), (2, 2), (2, 7)):
                body_slot(-1, g, u)
            body(0)
            body(1)
            pool.wait_ge(st_zero, 16 * FILLS)
            with pool.Fori(2, 7) as b:
                body(b)
            body(7)
            body(8)
            rt["late_slot"]["pool"] = body_slot


def channel_order(a):
    return a.reshape(*a.shape[:-1], NG, GH, DH).swapaxes(-1, -2).reshape(a.shape)


def constants():
    r = np.arange(P)
    inv = (np.float32(1.0) / np.float32(THETA) ** (np.arange(0, DH, 2, dtype=np.float32) / np.float32(DH)))
    dim = r // GH % DH
    freq = inv[dim // 2].astype(np.float32)
    ang = np.arange(T, dtype=np.float32)[None, :] * freq[:, None]
    table = np.zeros((P, NCONST), np.float32)
    table[:, COS:COS + T] = np.cos(ang)
    table[:, SIN:SIN + T] = np.sin(ang) * np.where(dim % 2 == 0, -1.0, 1.0)[:, None]
    table[:, IDENT:IDENT + P] = np.eye(P)
    table[:, CAUSAL:CAUSAL + P] = np.where(r[None, :] > r[:, None], MASKED, 0.0)
    table[:, LATER:LATER + P] = np.where(r[:, None] > r[None, :], MASKED, 0.0)
    table[:, TRI:TRI + P] = r[:, None] < r[None, :]
    table[:, RANK:RANK + E] = E - np.arange(E)
    return table


def first_weights(nc, d, rt, outer):
    def sem(name):
        rt[name] = outer.enter_context(nc.semaphore(name))
        return rt[name]

    region = Region(nc, rt["early"])
    raw = rt["raw"] = region.take("raw", [P, 2, 2 * HID])
    w0 = rt["w0"] = [[region.take(f"w{kind}0_{part}", [P, 2 * HID], F32R) for kind in "fgp"] for part in ("hi", "lo")]
    ld_raw = rt["ld_raw"] = [sem(f"ld_raw{i}") for i in range(2)]
    w_half, w_ready = sem("w_half"), sem("w_ready")

    def load_weights(sp, e, j, epar):
        src = d[("wf", "wg", "wp")[j]][e].rearrange("(k p) n -> p k n", p=P)
        dst = raw[:, (3 * epar + j) % 2, :].rearrange("p (k n) -> p k n", k=src.shape[1])
        sp.dma_start(dst, src).then_inc(ld_raw[(3 * epar + j) % 2], 16)

    def load_first_weights(sp, part):
        if part == 0:
            sp.wait_ge(rt["xn_done"], BATCH)
            sp.wait_ge(rt["v_done"], 2 * BATCH)
            sp.wait_ge(rt["v_moved"], BATCH)
            sp.wait_ge(rt["st_zero"], 16 * FILLS)
            for c in range(CK):
                sp.wait_ge(rt[f"st_hilo{c}"], 32 * BATCH)
            load_weights(sp, 0, 0, 0)
            load_weights(sp, 0, 1, 0)
        else:
            sp.wait_ge(w_ready, 1)
            load_weights(sp, 0, 2, 0)

    def split_first_hi(dve, j):
        dve.wait_ge(ld_raw[j % 2], 16 * (j // 2 + 1))
        nc.vector.tensor_copy(w0[0][j], raw[:, j % 2, :]).then_inc(w_half, 1)

    def split_first_lo(pool, j):
        pool.wait_ge(w_half, j + 1)
        nc.gpsimd.tensor_tensor(w0[1][j], raw[:, j % 2, :], w0[0][j].bitcast(F32), ALU.subtract).then_inc(w_ready, 1)

    rt.update(load_weights=load_weights, load_first_weights=load_first_weights,
              split_first_hi=split_first_hi, split_first_lo=split_first_lo)


LATE_SLOTS = {
    "sp": {7: ((8, 3, 4),)},
    "pe": {-2: ((8, 2, 3), (8, 2, 5), (8, 2, 6)), -1: ((8, 3, 1), (8, 3, 2)),
           4: ((9, 0, 1),), 5: ((9, 0, 2),), 6: ((9, 0, 4),), 7: ((9, 0, 5),), 9: ((9, 1, 5),)},
    "act": {-2: ((8, 2, 2), (8, 2, 6), (8, 2, 7)), 4: ((9, 0, 2),), 5: ((9, 0, 3),), 6: ((9, 0, 5),), 9: ((9, 1, 4),)},
    "dve": {-2: ((8, 2, 4),), -1: ((8, 3, 2), (8, 3, 3), (8, 2, 6)), 3: ((8, 3, 7),), 7: ((9, 0, 6),), 8: ((9, 1, 1), (9, 1, 2)),
            9: ((9, 1, 6), (9, 2, 1)), 10: ((9, 2, 6),)},
    "pool": {-1: ((8, 2, 3), (8, 2, 4), (8, 2, 6)), 0: ((8, 3, 4),),
             9: ((9, 2, 1), (9, 2, 3), (9, 2, 4), (9, 2, 6))},
}


def expert_phase(nc, d, rt, block):
    FULL = 3 * P
    BLK = ((0, FULL), (FULL, FULL), (2 * FULL, EROWS - 2 * FULL))
    WMAX = BLK[2][1]
    RING = 12
    NT = tuple(-(-w // P) for _, w in BLK)
    TB = (0, NT[0], NT[0] + NT[1])
    NTE = sum(NT)
    OB = 5
    WP = 2 * HID // 8
    ctx = ExitStack()
    with ctx:
        def sb(name, shape, dt=F32):
            return ctx.enter_context(nc.sbuf_tensor(name, shape, dt))

        def sem(name):
            return ctx.enter_context(nc.semaphore(name))

        ident, raw = rt["ident"], rt["raw"]
        region = Region(nc, rt["late"])
        late_g, late_p = ([region.take(f"w{kind}1_{part}", [P, 2 * HID], F32R) for part in ("hi", "lo")] for kind in "gp")
        w_hi, w_lo = ([rt["w0"][i], [sb(f"wf1_{i}", [P, 2 * HID], F32R), late_g[i], late_p[i]]] for i in range(2))
        b_fc = sb("b_fc", [P, E, HK])
        b_gate = sb("b_gate", [P, E, HK])
        b_proj = sb("b_proj", [P, 2, C])
        rows = sb("rows", [P, 2, 4, C])
        xh = sb("xh", [P, 2, CK, WMAX], F32R)
        xl = sb("xl", [P, 2, CK, WMAX], F32R)
        ah = sb("ah", [P, RING, WMAX], F32R)
        al = sb("al", [P, RING, WMAX], F32R)
        fc = sb("fc", [P, 2, WMAX])
        gated = sb("gated", [P, 2, WMAX])
        hid = sb("hid", [P, 2, WMAX])
        o_sb = sb("o_sb", [P, OB, C])
        ps = rt["ps"]
        FC, GATE, TURN, PROJ = 0, 2, 4, 6

        ld_once, ld_tail = sem("ld_once"), sem("ld_tail")
        ld_rows = [sem(f"ld_rows{i}") for i in range(2)]
        ld_raw = rt["ld_raw"]
        ld_bp = [sem(f"ld_bp{i}") for i in range(2)]
        st_o = [sem(f"st_o{i}") for i in range(OB)]
        w_split, w_ready = sem("w_slice"), rt["w_ready"]
        turned, xh_done, xl_done = sem("turned"), sem("xh_done"), sem("xl_done")
        fc_done, gate_done, fc_out, gated_done = sem("fc_done"), sem("gate_done"), sem("fc_out"), sem("gated_done")
        hid_done, ah_done, al_done = sem("hid_done"), sem("ah_done"), sem("al_done")
        LAST = E - 1
        NB = TT * K
        got = [w_[0][kind][:].bitcast(F32).rearrange("p (n c) -> p n c", n=NB) for w_ in (w_hi, w_lo) for kind in range(3)]
        y = [raw[:, i // 2, :].rearrange("p (i t c) -> p i t c", i=2, t=TT)[:, i % 2] for i in range(4)]
        gathered = [sem(f"gathered{i}") for i in range(len(got))]
        ld_y = [sem(f"ld_y{i}") for i in range(len(y))]
        st_y = [sem(f"st_y{i}") for i in range(len(y))]
        summed, first_sum = sem("summed"), sem("first_sum")
        proj_done, tile_out = sem("proj_done"), sem("tile_out")
        act_passed, pool_passed = sem("act_passed"), sem("pool_passed_e")

        def step_of(e, n):
            return (e - 1, 2) if n < 0 else (e + 1, 0) if n > 2 else (e, n)

        def nth_weights(half, par, j):
            return 3 * half + (3 * par + j) // 2

        def nth_rows(half, par, n):
            return 3 * half + (3 * par + n) // 2

        def real(e):
            return not isinstance(e, int) or 0 <= e < E

        def experts(eng, body):
            body(0, 0)
            with eng.Fori(0, E // 2 - 1) as i:
                body(i, 1)
                body(i + 1, 0)
            body(E // 2 - 1, 1)

        def tiles(n):
            return [(k, min(P, BLK[n][1] - P * k)) for k in range(NT[n])]

        def side(par, n):
            return (3 * par + n) % 2

        def slots_at(name, e, off, size):
            return rt[name][bass.ds(e * EROWS + off, size), :]

        def turns(e, n, hc, at, late_at):
            if isinstance(e, int) and (e, n) == (0, 1):
                return (0, 1) if hc == late_at else ()
            return ((hc - at) // 2,) if hc in (at, at + 2) and real(step_of(e, n + 1)[0]) else ()

        def late_slots(engine, e, c):
            if isinstance(e, int) and e == 0:
                for at in LATE_SLOTS[engine].get(c, ()):
                    rt["late_slot"][engine](*at)

        @block.sync
        def _(sp):
            def load_rows(e, n, par):
                off, width = BLK[n]
                full = width // P
                sp.dma_start(rows[:, par, 0:full], slots_at("tok", e, off, full * P).rearrange("(k p) c -> p k c", p=P))\
                    .then_inc(ld_rows[par], 16)
                if width % P:
                    sp.dma_start(rows[0:width % P, par, full], slots_at("tok", e, off + full * P, width % P))\
                        .then_inc(ld_tail, 16)

            def load_bias(e, epar):
                sp.dma_start(b_proj[:, epar, :], d["bp"][e].to_broadcast([P, C])).then_inc(ld_bp[epar], 16)

            def store(e, n):
                for k, size in tiles(n):
                    q = TB[n] + k
                    wait(sp, tile_out, NTE * e + q + 1)
                    sp.dma_start(slots_at("o", e, BLK[n][0] + P * k, size), o_sb[0:size, q % OB, :]).then_inc(st_o[q % OB], 16)

            def body(half, par):
                e = 2 * half + par
                for n in range(3):
                    e2, n2 = step_of(e, n + 1)
                    last_rows = isinstance(e, int) and (e, n) == (0, 1)
                    if real(e2) and not last_rows:
                        if not (isinstance(e, int) and 3 * e + n < 1):
                            sp.wait_ge(turned, 2 * (3 * e + n))
                        load_rows(e2, n2, side(par, n + 1))
                    if real(e + 1):
                        sp.wait_ge(w_ready, 3 * e + n + 2)
                        rt["load_weights"](sp, e + 1, n, 1 - par)
                    e0, n0 = step_of(e, n - 1)
                    if real(e0):
                        store(e0, n0)
                    late_slots("sp", e, 8 * n + HK - 1)
                    if last_rows:
                        sp.wait_ge(turned, 2)
                        sp.wait_ge(rt["st_tok"], 16 * NB * BATCH)
                        load_rows(e2, n2, side(par, n + 1))
                    if n == 0 and real(e + 1):
                        load_bias(e + 1, 1 - par)

            sp.wait_ge(rt["pv_done"], 4 * NG * BATCH)
            sp.wait_ge(rt["h_done"], BATCH - 1)
            load_rows(0, 0, 0)
            sp.dma_start(b_fc[:], d["bf"]).then_inc(ld_once, 16)
            sp.dma_start(b_gate[:], d["bg"]).then_inc(ld_once, 16)
            load_bias(0, 0)
            experts(sp, body)
            store(LAST, 2)
            for stored in st_o:
                sp.wait_ge(stored, 16 * NTE // OB * E)
            for stored in st_y:
                sp.wait_ge(stored, 16 * BATCH // len(y))
            sp.wait_ge(rt["st_x1"], 16 * BATCH)

        @block.tensor
        def _(pe):
            mm = nc.tensor.matmul


            def turn(e, half, epar, n, c):
                par = side(epar, n)
                if c == 0:
                    pe.wait_ge(ld_rows[par], 16 * nth_rows(half, epar, n) + 16)
                    if n == 2:
                        pe.wait_ge(ld_tail, 16 * e + 16)
                if not (isinstance(e, int) and 3 * e + n < 1):
                    pe.wait_ge(xl_done, 2 * (3 * e + n - 1) + c + 1)
                for k, size in tiles(n):
                    last = nc.tensor.transpose(ps[:, TURN + c, P * k:P * k + size], rows[0:size, par, k, bass.ts(c, P)],
                                               ident[0:size, 0:size])
                last.then_inc(turned, 1)

            def up(e, n, par, hc):
                width, sd = BLK[n][1], side(par, n)
                u = 8 * (3 * e + n) + hc
                if hc == 0:
                    pe.wait_ge(xl_done, 2 * (3 * e + n) + 2)
                if n == 0 and hc == 0:
                    pe.wait_ge(w_ready, 3 * e + 2)
                for kind, bank, free, done in ((0, FC, fc_out, fc_done), (1, GATE, gated_done, gate_done)):
                    if not (isinstance(e, int) and u < 2):
                        pe.wait_ge(free, u - 1)
                    w = [w_[par][kind][:].rearrange("p (c n) -> p c n", c=CK) for w_ in (w_hi, w_lo)]
                    product3(nc, ps[:, bank + hc % 2, 0:width],
                            [([w_[:, c, bass.ts(hc, P)] for w_ in w], [x[:, sd, c, 0:width] for x in (xh, xl)])
                             for c in range(CK)]).then_inc(done, 1)

            def project(e, n, par):
                if n == 0:
                    pe.wait_ge(w_ready, 3 * e + 3)
                    if isinstance(e, int) and e == 0:
                        pe.wait_ge(rt["pv_out"], NG * BATCH)
                        pe.wait_ge(rt["pf_out"], BATCH)
                for k, size in tiles(n):
                    q = TB[n] + k
                    if not (isinstance(e, int) and NTE * e + q < 2):
                        pe.wait_ge(tile_out, NTE * e + q - 1)
                    if k == 0:
                        pe.wait_ge(al_done, 8 * (3 * e + n) + 8)
                    wh, wl = (w_[par][2][:].rearrange("p (h n) -> p h n", h=HK) for w_ in (w_hi, w_lo))
                    a = [[x[:, (8 * n + hc) % RING, P * k:P * k + size] for x in (ah, al)] for hc in range(HK)]
                    product3(nc, ps[0:size, PROJ + q % 2, 0:C],
                            [(a[hc], (wh[:, hc, :], wl[:, hc, :])) for hc in range(HK)]).then_inc(proj_done, 1)

            def body(half, par):
                e = 2 * half + par
                for n in range(3):
                    for hc in range(HK):
                        up(e, n, par, hc)
                        e0, n0 = step_of(e, n - 1)
                        if hc == 2 and real(e0):
                            project(e0, n0, par if n else 1 - par)
                        e2, n2 = step_of(e, n + 1)
                        half2, par2 = (half, par) if n < 2 else (half + par, 1 - par)
                        for c in turns(e, n, hc, 2, 5):
                            turn(e2, half2, par2, n2, c)
                        late_slots("pe", e, 8 * n + hc)

            late_slots("pe", 0, -2)
            pe.wait_ge(ld_once, 16 * 2)
            turn(0, 0, 0, 0, 0)
            turn(0, 0, 0, 0, 1)
            late_slots("pe", 0, -1)
            experts(pe, body)
            project(E - 1, 2, 1)

        def split_in(eng, e, n, par, c, high):
            k = 2 * (3 * e + n) + c
            width = BLK[n][1]
            src = ps[:, TURN + c, 0:width]
            if high:
                eng.wait_ge(turned, k + 1)
                nc.scalar.activation(xh[:, par, c, 0:width], src, ACT.Copy).then_inc(xh_done, 1)
            else:
                eng.wait_ge(xh_done, k + 1)
                nc.vector.tensor_tensor(xl[:, par, c, 0:width], src, xh[:, par, c, 0:width].bitcast(F32), ALU.subtract)\
                    .then_inc(xl_done, 1)

        @block.scalar
        def _(act):
            A = nc.scalar.activation

            def silu(e, n, hc):
                u = 8 * (3 * e + n) + hc
                n, hc = (n, hc) if hc >= 0 else ((n - 1) % 3, HK - 1)
                if isinstance(e, int) and u < 0:
                    return
                width = BLK[n][1]
                act.wait_ge(gated_done, u + 1)
                if not (isinstance(e, int) and u < 2):
                    act.wait_ge(al_done, u - 1)
                A(hid[:, hc % 2, 0:width], gated[:, hc % 2, 0:width], ACT.Silu).then_inc(hid_done, 1)

            def body(half, par):
                e = 2 * half + par
                for n in range(3):
                    width = BLK[n][1]
                    for hc in range(HK):
                        u = 8 * (3 * e + n) + hc
                        wait_apart(act, fc_done, u + 1, act_passed)
                        if not (isinstance(e, int) and u < 2):
                            wait_apart(act, gated_done, u - 1, act_passed)
                        A(fc[:, hc % 2, 0:width], ps[:, FC + hc % 2, 0:width], ACT.Identity,
                          bias=b_fc[:, e, hc:hc + 1]).then_inc(fc_out, 1)
                        silu(e, n, hc - 1)
                        e2, n2 = step_of(e, n + 1)
                        for c in turns(e, n, hc, 3, 6):
                            split_in(act, e2, n2, side(par, n + 1), c, True)
                        late_slots("act", e, 8 * n + hc)

            late_slots("act", 0, -2)
            act.wait_ge(ld_once, 16 * 2)
            for c in range(CK):
                split_in(act, 0, 0, 0, c, True)
            experts(act, body)
            silu(E, 0, -1)

            def batch_rows(name, b):
                return name[bass.ts(b, T), :].rearrange("(t p) c -> p t c", p=P)

            def load_y(b):
                act.dma_start(y[b % 4], batch_rows(rt["x1"], b)).then_inc(ld_y[b % 4], 16)

            act.wait_ge(w_ready, 3 * E)
            act.wait_ge(rt["st_x1"], 16 * BATCH)
            for b in range(4):
                load_y(b)
            for b in range(BATCH):
                act.wait_ge(summed, b + 1)
                act.dma_start(batch_rows(d["out"], b), y[b % 4]).then_inc(st_y[b % 4], 16)
                if 0 < b < 5:
                    act.wait_ge(st_y[b - 1], 16)
                    load_y(b + 3)

        @block.vector
        def _(dve):
            V = nc.vector

            def hid_hi(e, n, hc):
                u = 8 * (3 * e + n) + hc
                if isinstance(e, int) and u < 0:
                    return
                e, n, hc = (e, n, hc) if hc >= 0 else (*step_of(e, n - 1), HK - 1)
                gone = NTE * e + (TB[n] if hc >= RING - HK else (-NT[2], 0, TB[1])[n])
                if not (isinstance(gone, int) and gone <= 0):
                    dve.wait_ge(proj_done, gone)
                width = BLK[n][1]
                dve.wait_ge(hid_done, u + 1)
                V.tensor_copy(ah[:, (8 * n + hc) % RING, 0:width], hid[:, hc % 2, 0:width]).then_inc(ah_done, 1)

            def hid_lo(n, hc):
                u = 8 * (3 * LAST + n) + hc
                n, hc = (n, hc) if hc >= 0 else (n - 1, HK - 1)
                width, at = BLK[n][1], (8 * n + hc) % RING
                dve.wait_ge(ah_done, u + 1)
                dve.wait_ge(al_done, u)
                V.tensor_tensor(al[:, at, 0:width], hid[:, hc % 2, 0:width], ah[:, at, 0:width].bitcast(F32),
                                ALU.subtract).then_inc(al_done, 1)

            def combine(b):
                dve.wait_ge(gathered[b % len(got)], 16 * NB * (b // len(got) + 1))
                dve.wait_ge(ld_y[b % 4], 16 * (b // 4 + 1))
                for k, done in ((0, first_sum), (1, summed)):
                    for t in range(TT):
                        col = b * NB + K * t + k
                        ins = V.scalar_tensor_tensor(y[b % 4][:, t, :], got[b % len(got)][:, K * t + k, :],
                                                     rt["prob"][:, col:col + 1], y[b % 4][:, t, :], ALU.mult, ALU.add)
                    ins.then_inc(done, 1)
                    if k == 0:
                        dve.wait_ge(first_sum, b + 1)

            def tiles_out(e, half, n, par):
                if n == 0:
                    dve.wait_ge(ld_bp[par], 16 * half + 16)
                for k, size in tiles(n):
                    q = TB[n] + k
                    dve.wait_ge(proj_done, NTE * e + q + 1)
                    if not (isinstance(e, int) and NTE * e + q < OB):
                        dve.wait_ge(st_o[q % OB], 16 * (NTE // OB * e + q // OB))
                    V.tensor_tensor(o_sb[0:size, q % OB, :], ps[0:size, PROJ + q % 2, 0:C], b_proj[0:size, par, :],
                                    ALU.add).then_inc(tile_out, 1)

            def body(half, par):
                e = 2 * half + par
                for n in range(3):
                    width = BLK[n][1]
                    for hc in range(HK):
                        u = 8 * (3 * e + n) + hc
                        dve.wait_ge(gate_done, u + 1)
                        dve.wait_ge(fc_out, u + 1)
                        if not (isinstance(e, int) and u < 2):
                            dve.wait_ge(hid_done, u - 1)
                        V.scalar_tensor_tensor(gated[:, hc % 2, 0:width], ps[:, GATE + hc % 2, 0:width],
                                               b_gate[:, e, hc:hc + 1], fc[:, hc % 2, 0:width],
                                               ALU.add, ALU.mult).then_inc(gated_done, 1)
                        hid_hi(e, n, hc - 1)
                        if isinstance(e, int) and e == LAST and 8 * n + hc > 8:
                            hid_lo(n, hc - 1)
                        e0, n0 = step_of(e, n - 1)
                        if hc == 2 and real(e0):
                            tiles_out(e0, half if n else half - (1 - par), n0, par if n else 1 - par)
                        e2, n2 = step_of(e, n + 1)
                        for c in turns(e, n, hc, 4, 7):
                            split_in(dve, e2, n2, side(par, n + 1), c, False)
                        late_slots("dve", e, 8 * n + hc)

            late_slots("dve", 0, -2)
            for c in range(CK):
                split_in(dve, 0, 0, 0, c, False)
            late_slots("dve", 0, -1)
            experts(dve, body)
            hid_hi(E, 0, -1)
            hid_lo(3, -1)
            tiles_out(LAST, LAST // 2, 2, 1)
            for b in range(BATCH):
                combine(b)

        @block.gpsimd
        def _(pool):
            G = nc.gpsimd

            def hid_lo(e, n, hc):
                u = 8 * (3 * e + n) + hc
                if isinstance(e, int) and u < 0:
                    return
                n, hc = (n, hc) if hc >= 0 else ((n - 1) % 3, HK - 1)
                width, at = BLK[n][1], (8 * n + hc) % RING
                pool.wait_ge(ah_done, u + 1)
                G.tensor_tensor(al[:, at, 0:width], hid[:, hc % 2, 0:width], ah[:, at, 0:width].bitcast(F32),
                                ALU.subtract).then_inc(al_done, 1)

            def body(half, par):
                e = 2 * half + par
                """Beside the hidden chunks' low parts, a 24th of the next expert's weights is split a chunk."""
                for n in range(3 if real(e + 1) else 1):
                    for hc in range(HK):
                        ahead = real(e + 1)
                        cols = slice(WP * hc, WP * (hc + 1))
                        src = raw[:, (3 * (1 - par) + n) % 2, cols]
                        if ahead:
                            if isinstance(e, int) and e == 0:
                                if (n, hc) == (0, 0):
                                    pool.wait_ge(rt["pv_done"], 4 * NG * BATCH)
                                if (n, hc) == (1, 0):
                                    pool.wait_ge(rt["o_out"], 2 * BATCH)
                                if (n, hc) == (2, 0):
                                    pool.wait_ge(rt["lt_done"], BATCH)
                                    pool.wait_ge(rt["st_x1"], 16 * BATCH)
                                if (n, hc) == (2, 4):
                                    pool.wait_ge(rt["st_tok"], 16 * NB * BATCH)
                            if hc == 0:
                                pool.wait_ge(ld_raw[(3 * (1 - par) + n) % 2], 16 * nth_weights(half + par, 1 - par, n) + 16)
                                if n < 2 and not (isinstance(e, int) and e < 1):
                                    pool.wait_ge(gate_done, 24 * e)
                                if n == 2 and not (isinstance(e, int) and e < 1):
                                    pool.wait_ge(proj_done, NTE * e)
                                if not isinstance(e, int):
                                    pool.sem_inc(pool_passed, 1)
                            G.tensor_scalar(w_hi[1 - par][n][:, cols], src, 1.0, 0.0, ALU.mult, ALU.add)\
                                .then_inc(w_split, 1)
                        hid_lo(e, n, hc - 1)
                        if ahead:
                            pool.wait_ge(w_split, 8 * (3 * e + n) + hc + 1)
                            ins = G.tensor_tensor(w_lo[1 - par][n][:, cols], src,
                                                  w_hi[1 - par][n][:, cols].bitcast(F32), ALU.subtract)
                            if hc == HK - 1:
                                ins.then_inc(w_ready, 1)
                        late_slots("pool", e, 8 * n + hc)

            def stored(q):
                pool.wait_ge(st_o[q % OB], 16 * (NTE // OB * LAST + q // OB + 1))

            def gather(b):
                buf = b % len(got)
                if b >= len(got):
                    pool.wait_ge(summed, b - len(got) + 1)
                there_now = LAST * EROWS + (b + 1) * CAP
                for n in range(NB):
                    G.indirect_dma_start(
                        out=got[buf][:, n, :], out_offset=None, in_=rt["o"][0:there_now],
                        in_offset=bass.IndirectOffsetOnAxis(ap=rt["slot"][:, b * NB + n:b * NB + n + 1], axis=0),
                        bounds_check=there_now - 1, oob_is_err=False).then_inc(gathered[buf], 16)

            late_slots("pool", 0, -1)
            experts(pool, body)
            hid_lo(LAST, 1, -1)
            pool.wait_ge(gate_done, 24 * LAST)
            pool.wait_ge(proj_done, NTE * LAST)
            for i in range(OB):
                pool.wait_ge(st_o[i], 16 * NTE // OB * LAST)
            rows_out = 0
            for b in range(BATCH):
                for q in range(NTE):
                    n = max(n for n in range(3) if TB[n] <= q)
                    first_row = BLK[n][0] + P * (q - TB[n])
                    if rows_out <= first_row < (b + 1) * CAP:
                        stored(q)
                rows_out = (b + 1) * CAP
                gather(b)


def build(nc, d):
    ctx = ExitStack()
    with ctx:
        def dram(name, shape):
            return nc.dram_tensor(name, shape, F32, kind="Internal").ap()

        rt = {
            "qk": dram("qk_parts", [BATCH, 2, 2, C, T]),
            "x1": dram("x1_rows", [BATCH * T, C]),
            "tok": dram("slot_tokens", [NSLOT, C]),
            "o": dram("slot_outputs", [NSLOT, C]),
            "slot": ctx.enter_context(nc.sbuf_tensor("slot_all", [P, BATCH * TT * K], I32)),
            "prob": ctx.enter_context(nc.sbuf_tensor("prob_all", [P, BATCH * TT * K], F32)),
            "early": set_apart(nc, ctx, "early", 17 * 4 * HID),
            "late": set_apart(nc, ctx, "late", 4 * 4 * 2 * HID),
            "kept": set_apart(nc, ctx, "kept", 4 * 1536),
            "ps": ctx.enter_context(nc.psum_tensor("ps", [P, 8, T], F32)),
            "late_slot": {},
        }
        block = ctx.enter_context(nc.Block())
        first_weights(nc, d, rt, ctx)
        attention_phase(nc, d, rt, block, ctx)
        expert_phase(nc, d, rt, block)


def kernel(**inputs):
    import numpy as _np
    import concourse.bacc as _bacc
    from concourse import mybir as _mybir
    from concourse.bass_utils import run_bass_kernel_spmd as _run

    def attn(name):
        return _np.asarray(inputs["L0_attn_" + name])

    def ffn(name):
        return _np.asarray(inputs["L0_ffn_" + name])

    arrays = {
        "x": attn("x").reshape(BATCH * T, C),
        "wqT": channel_order(attn("Wq").T), "wkT": channel_order(attn("Wk").T),
        "wvT": attn("Wv").T, "woT": attn("Wo").T,
        "bq": channel_order(attn("bq")), "bk": channel_order(attn("bk")), "bv": attn("bv"), "bo": attn("bo"),
        "wr": ffn("router_w"), "rb": ffn("router_b"),
        "wf": ffn("w_c_fc"), "wg": ffn("w_gate"), "wp": ffn("w_c_proj"),
        "bf": ffn("b_c_fc").reshape(E, HK, P).transpose(2, 0, 1),
        "bg": ffn("b_gate").reshape(E, HK, P).transpose(2, 0, 1),
        "bp": ffn("b_c_proj"),
        "consts": constants(),
        "rows": np.stack([np.zeros(NG * GH * T, np.float32), np.ones(NG * GH * T, np.float32)]),
    }
    arrays = {"in_" + k: _np.ascontiguousarray(v) for k, v in arrays.items()}
    nc = _bacc.Bacc("TRN2", target_bir_lowering=False, num_devices=1)
    d = {k[3:]: nc.dram_tensor(k, v.shape, _mybir.dt.from_np(v.dtype), kind="ExternalInput").ap()
         for k, v in arrays.items()}
    d["out"] = nc.dram_tensor("out_rows", [BATCH * T, C], F32, kind="ExternalOutput").ap()
    build(nc, d)
    r = _run(nc, [arrays], core_ids=[0])
    return r.results[0]["out_rows"].reshape(BATCH, T, C)
```
